# Optimizing a Trainium2 kernel written in Bass

```python
import numpy as np
import jax
import jax.numpy as jnp

def _softmax(x, axis=-1):
    return jax.nn.softmax(x, axis=axis)

def _gelu(x):
    return jax.nn.gelu(x, approximate=True)

def _silu(x):
    return jax.nn.silu(x)

def _sigmoid(x):
    return jax.nn.sigmoid(x)

def _layernorm(x, axis=-1, eps=1e-05):
    m = jnp.mean(x, axis=axis, keepdims=True)
    v = jnp.var(x, axis=axis, keepdims=True)
    return (x - m) / jnp.sqrt(v + eps)

def _scatter_add(tgt, idx, src, axis=0):
    return tgt.at[idx].add(src)

def _segment_sum(src, seg, n):
    return jax.ops.segment_sum(src, seg, n)
kernel_name = 'mk_gnn_ffn_d1_gnn_r8_70faad'

def setup_inputs(seed: int=0):
    np.random.seed(seed)
    _w = jnp.asarray

    def _rec_inputs():
        import jax
        import jax.numpy as jnp
        _gk = jax.random.key(seed)
        x = -0.0003713 + 1 * jax.random.normal(jax.random.fold_in(_gk, 1), (6250, 256), jnp.float32)
        src = jax.random.randint(jax.random.fold_in(_gk, 2), (100000,), 0, 6250, jnp.int32)
        dst = jax.random.randint(jax.random.fold_in(_gk, 3), (100000,), 0, 6250, jnp.int32)
        _o = jnp.argsort(dst, stable=True)
        src = src[_o]
        dst = dst[_o]
        return (x, src, dst)
    x, src, dst = _rec_inputs()

    def _L0_gnn_setup():
        import jax, jax.numpy as jnp
        import numpy as np
        NEG_SLOPE = 0.2

        def gatv2_layer(x, Wl, Wr, att, bias, src, dst, n_nodes, heads, ch, concat):
            xl = (x @ Wl).reshape(n_nodes, heads, ch)
            xr = (x @ Wr).reshape(n_nodes, heads, ch)
            m = xl[src] + xr[dst]
            e = jax.nn.leaky_relu(m, NEG_SLOPE)
            logits = jnp.einsum('ehc,hc->eh', e, att)
            mx = jax.ops.segment_max(logits, dst, num_segments=n_nodes)
            ex = jnp.exp(logits - mx[dst])
            denom = jax.ops.segment_sum(ex, dst, num_segments=n_nodes)
            alpha = ex / denom[dst]
            out = jax.ops.segment_sum(alpha[:, :, None] * xl[src], dst, num_segments=n_nodes)
            if concat:
                out = out.reshape(n_nodes, heads * ch)
            else:
                out = out.mean(axis=1)
            return out + bias
        N, E = (6250, 100000)
        IN, HID, OUT, H = (256, 64, 256, 4)
        key = jax.random.key(seed)
        ks = jax.random.split(key, 12)
        s = lambda fan_in: 1.0 / np.sqrt(fan_in)
        return {'x': jax.random.normal(ks[0], (N, IN), dtype=jnp.float32), 'edge_index': jax.random.randint(ks[1], (2, E), 0, N, dtype=jnp.int64), 'Wl1': jax.random.normal(ks[2], (IN, H * HID), jnp.float32) * s(IN), 'Wr1': jax.random.normal(ks[3], (IN, H * HID), jnp.float32) * s(IN), 'att1': jax.random.normal(ks[4], (H, HID), jnp.float32) * s(HID), 'b1': jnp.zeros((H * HID,), jnp.float32), 'Wl2': jax.random.normal(ks[5], (H * HID, OUT), jnp.float32) * s(H * HID), 'Wr2': jax.random.normal(ks[6], (H * HID, OUT), jnp.float32) * s(H * HID), 'att2': jax.random.normal(ks[7], (1, OUT), jnp.float32) * s(OUT), 'b2': jnp.zeros((OUT,), jnp.float32)}
    _L0_gnn_all = _L0_gnn_setup()
    _L0_gnn_in = {k: v for k, v in _L0_gnn_all.items() if k in ('Wl1', 'Wr1', 'att1', 'b1', 'Wl2', 'Wr2', 'att2', 'b2')}
    del _L0_gnn_all

    def _L0_ffn_setup():
        import math
        import jax, jax.numpy as jnp
        import numpy as np
        CAPACITY_FACTOR = 1.25
        key = jax.random.key(seed)
        ks = jax.random.split(key, 5)
        B, L, D, F, E = (8, 1024, 256, 1024, 8)
        h = jax.random.normal(ks[0], (B, L, D), dtype=jnp.float32)
        gate_w = jax.random.normal(ks[1], (D, E), dtype=jnp.float32) * 0.02
        gate_b = jnp.zeros((E,), dtype=jnp.float32)
        w1 = jax.random.normal(ks[2], (E, D, F), dtype=jnp.float32) * (1.0 / math.sqrt(D))
        b1 = jnp.zeros((E, F), dtype=jnp.float32)
        w2 = jax.random.normal(ks[3], (E, F, D), dtype=jnp.float32) * (1.0 / math.sqrt(F))
        b2 = jnp.zeros((E, D), dtype=jnp.float32)
        return {'h': h, 'gate_w': gate_w, 'gate_b': gate_b, 'w1': w1, 'b1': b1, 'w2': w2, 'b2': b2}
    _L0_ffn_all = _L0_ffn_setup()
    _L0_ffn_in = {k: v for k, v in _L0_ffn_all.items() if k in ('gate_w', 'gate_b', 'w1', 'b1', 'w2', 'b2')}
    del _L0_ffn_all
    return {'x': x, 'src': src, 'dst': dst, 'L0_gnn_Wl1': _L0_gnn_in['Wl1'], 'L0_gnn_Wr1': _L0_gnn_in['Wr1'], 'L0_gnn_att1': _L0_gnn_in['att1'], 'L0_gnn_b1': _L0_gnn_in['b1'], 'L0_gnn_Wl2': _L0_gnn_in['Wl2'], 'L0_gnn_Wr2': _L0_gnn_in['Wr2'], 'L0_gnn_att2': _L0_gnn_in['att2'], 'L0_gnn_b2': _L0_gnn_in['b2'], 'L0_ffn_gate_w': _L0_ffn_in['gate_w'], 'L0_ffn_gate_b': _L0_ffn_in['gate_b'], 'L0_ffn_w1': _L0_ffn_in['w1'], 'L0_ffn_b1': _L0_ffn_in['b1'], 'L0_ffn_w2': _L0_ffn_in['w2'], 'L0_ffn_b2': _L0_ffn_in['b2']}

def reference(x, src, dst, L0_gnn_Wl1, L0_gnn_Wr1, L0_gnn_att1, L0_gnn_b1, L0_gnn_Wl2, L0_gnn_Wr2, L0_gnn_att2, L0_gnn_b2, L0_ffn_gate_w, L0_ffn_gate_b, L0_ffn_w1, L0_ffn_b1, L0_ffn_w2, L0_ffn_b2):
    import jax
    import jax.numpy as jnp

    def _L0_gnn_ref(x, edge_index, Wl1, Wr1, att1, b1, Wl2, Wr2, att2, b2):
        import jax, jax.numpy as jnp
        import numpy as np
        NEG_SLOPE = 0.2

        def gatv2_layer(x, Wl, Wr, att, bias, src, dst, n_nodes, heads, ch, concat):
            xl = (x @ Wl).reshape(n_nodes, heads, ch)
            xr = (x @ Wr).reshape(n_nodes, heads, ch)
            m = xl[src] + xr[dst]
            e = jax.nn.leaky_relu(m, NEG_SLOPE)
            logits = jnp.einsum('ehc,hc->eh', e, att)
            mx = jax.ops.segment_max(logits, dst, num_segments=n_nodes)
            ex = jnp.exp(logits - mx[dst])
            denom = jax.ops.segment_sum(ex, dst, num_segments=n_nodes)
            alpha = ex / denom[dst]
            out = jax.ops.segment_sum(alpha[:, :, None] * xl[src], dst, num_segments=n_nodes)
            if concat:
                out = out.reshape(n_nodes, heads * ch)
            else:
                out = out.mean(axis=1)
            return out + bias
        N = x.shape[0]
        loops = jnp.arange(N, dtype=edge_index.dtype)
        src = jnp.concatenate([edge_index[0], loops])
        dst = jnp.concatenate([edge_index[1], loops])
        h = gatv2_layer(x, Wl1, Wr1, att1, b1, src, dst, N, 4, 64, concat=True)
        h = jax.nn.elu(h)
        out = gatv2_layer(h, Wl2, Wr2, att2, b2, src, dst, N, 1, 256, concat=False)
        return out

    def _L0_ffn_ref(h, gate_w, gate_b, w1, b1, w2, b2):
        import math
        import jax, jax.numpy as jnp
        import numpy as np
        CAPACITY_FACTOR = 1.25
        B, L, D = h.shape
        E = gate_w.shape[1]
        T = B * L
        C = max(1, math.ceil(CAPACITY_FACTOR * T / E))
        x = h.reshape(T, D)
        logits = x @ gate_w + gate_b
        probs = jax.nn.softmax(logits, axis=-1)
        idx = jnp.argmax(probs, axis=-1)
        prb = jnp.take_along_axis(probs, idx[:, None], axis=1)[:, 0]
        one_hot = jax.nn.one_hot(idx, E, dtype=jnp.float32)
        pos = (jnp.cumsum(one_hot, axis=0) * one_hot).sum(-1).astype(jnp.int32) - 1
        kept = pos < C
        pos_safe = jnp.where(kept, pos, C)
        buf = jnp.zeros((E, C, D), dtype=h.dtype).at[idx, pos_safe].set(x, mode='drop')
        hmid = jax.nn.relu(jnp.einsum('ecd,edf->ecf', buf, w1) + b1[:, None, :])
        ybuf = jnp.einsum('ecf,efd->ecd', hmid, w2) + b2[:, None, :]
        pos_g = jnp.minimum(pos, C - 1)
        y_tok = ybuf[idx, pos_g] * (prb * kept)[:, None]
        y = y_tok.reshape(B, L, D)
        y = jnp.nan_to_num(y, nan=0.0, posinf=10000.0, neginf=-10000.0)
        return y
    edge_index = jnp.stack([src, dst])
    x = x + _L0_gnn_ref(_layernorm(x, axis=-1), edge_index, L0_gnn_Wl1, L0_gnn_Wr1, L0_gnn_att1, L0_gnn_b1, L0_gnn_Wl2, L0_gnn_Wr2, L0_gnn_att2, L0_gnn_b2)
    x = x + _L0_ffn_ref(_layernorm(x, axis=-1)[None], L0_ffn_gate_w, L0_ffn_gate_b, L0_ffn_w1, L0_ffn_b1, L0_ffn_w2, L0_ffn_b2)[0]
    return x

_drawn_inputs = setup_inputs


def setup_inputs(seed=0):
    import zlib

    import numpy as np

    out = dict(_drawn_inputs(seed))
    spreads = {'L0_gnn_b1': (0.0, 0.1),
     'L0_gnn_b2': (0.0, 0.1),
     'L0_ffn_gate_b': (0.0, 0.1),
     'L0_ffn_b1': (0.0, 0.63),
     'L0_ffn_b2': (0.0, 0.443)}
    factors = {'L0_gnn_Wr2': 5.872, 'L0_gnn_att2': 2.739}
    for name, (base, spread) in spreads.items():
        noise = np.random.default_rng([zlib.crc32(name.encode()), seed]).standard_normal(out[name].shape)
        drawn = base * np.exp(spread * noise) if base else spread * noise
        out[name] = jnp.asarray(drawn.astype(out[name].dtype))
    for name, factor in factors.items():
        out[name] = (out[name] * factor).astype(out[name].dtype)
    return out
```

```python
from contextlib import ExitStack

import concourse.bass as bass
from concourse import mybir

ALU = mybir.AluOpType
ACT = mybir.ActivationFunctionType
F32 = mybir.dt.float32
I32 = mybir.dt.int32
U32 = mybir.dt.uint32
BF16 = mybir.dt.bfloat16
AX = mybir.AxisListType

P = 128
N, D, E = 6250, 256, 100000
H1 = 4
NB = -(-N // P)
LAST = N - P * (NB - 1)
NPAD = NB * P
W = D + H1
EROWS = -(-E // P) + 2
ROWS = -(-E // P)
NG = 440
assert (ROWS + NB - 1 + NB) // 2 <= NG
NS = 2 * NG
Q = 110
J = NS // Q
TL = J * P
GQ = J // 2
assert Q * J == NS
BIG = 1.0e30
EPS = 1e-5
NX, F = 8, 1024
CAP = -(-5 * N // (4 * NX))
SLOTS = 1024
ZROW = NX * SLOTS - 1
ECH = 125
assert E % ECH == 0
AUXW = 9
AW = D + AUXW
RING = 16
DUMP = 4


class Mark:

    def __init__(self, sem):
        self.sem, self.n = sem, 0

    def __call__(self, ins):
        ins.then_inc(self.sem, 1)
        self.n += 1
        return self.n


def bcast_mid(ap, n):
    return ap.unsqueeze(1).broadcast_to([ap.shape[0], n, ap.shape[1]])


def bcast_last(ap, n):
    return ap.unsqueeze(len(ap.shape)).broadcast_to([*ap.shape, n])


class Phase:

    def __init__(self, nc, name):
        self.nc, self.name, self.sems, self.stack = nc, name, [], ExitStack()

    def __enter__(self):
        return self

    def __exit__(self, *_):
        self.stack.close()
        self.nc.clear_and_free_semaphores(self.sems)
        self.nc.all_engine_barrier()

    def sem(self, name):
        self.sems.append(self.nc.alloc_semaphore(f"{self.name}_{name}"))
        return self.sems[-1]

    def sb(self, name, shape, dt=F32):
        return self.stack.enter_context(self.nc.sbuf_tensor(f"{self.name}_{name}", shape, dt))


def build(nc, x, src, dst, gnn, ffn, out):
    with ExitStack() as ctx:
        def sb(name, shape, dt=F32, stack=ctx):
            return stack.enter_context(nc.sbuf_tensor(name, shape, dt))

        def dram(name, shape, dt=F32):
            return nc.dram_tensor(name, shape, dt, kind="Internal").ap()

        T = {}
        T["src_rows"] = dram("src_rows", (EROWS, P), I32)
        T["dst_rows"] = dram("dst_rows", (EROWS, P), I32)
        T["keys"] = dram("keys", (Q * TL + 2,), F32)
        T["rel"] = dram("rel", ((NS + J) * P,), BF16)
        T["block_row"] = dram("block_row", (NG,), I32)
        T["sum_row"] = dram("sum_row", (NG,), I32)
        T["keep"] = dram("keep", (NG,), F32)
        T["xl"] = dram("xl", (NPAD, W))
        T["xr"] = dram("xr", (NPAD, W))
        T["edges_xl"] = dram("edges_xl", (NG, P, 2 * W))
        T["sums"] = dram("sums", (NPAD + DUMP * P, AW))
        T["tokens"] = dram("tokens", (NX * SLOTS, W))
        T["answers"] = dram("answers", (NX * SLOTS, D))
        T["psum"] = ctx.enter_context(nc.psum_tensor("psum", [P, 8, 512], F32))
        T["x"] = sb("x_res", [P, NB, D])
        T["ident"] = sb("ident", [P, P])
        T["ones"] = sb("ones", [P, P])
        T["lane"] = sb("lane", [P, 2, P])
        T["eps"] = sb("eps", [P, 1])
        with ExitStack() as g:
            T["block_row_s"] = sb("block_row_s", [1, NG], I32, g)
            T["sum_row_s"] = sb("sum_row_s", [1, NG], I32, g)
            T["keep_s"] = sb("keep_s", [P, NG], F32, g)
            T["turn_cut"] = sb("turn_cut", [Q, TL + 1], F32, g)
            T["invalid"] = sb("invalid", [Q, TL], F32, g)
            T["is_last"] = sb("is_last", [Q, TL], F32, g)
            T["cut_any"] = sb("cut_any", [H1, 2, Q], F32, g)
            T["src_lane"] = sb("src_lane", [P, NS + RING], I32, g)
            T["rel_lane"] = sb("rel_lane", [P, NS], F32, g)
            T["part"] = sb("part", [P, 1], F32, g)
            T["logits"] = sb("logits", [P, NS, H1], F32, g)
            T["aux"] = sb("aux", [P, NS, AUXW], F32, g)
            T["self_logits"] = sb("self_logits", [P, NB, H1], F32, g)
            with Phase(nc, "tables") as ph:
                make_tables(nc, ph, T, x, src, dst)
            for layer in range(2):
                with Phase(nc, f"nodes{layer}") as ph:
                    nodes(nc, ph, T, gnn, layer)
                with Phase(nc, f"score{layer}") as ph:
                    score(nc, ph, T, gnn[layer], layer)
                with Phase(nc, f"softmax{layer}") as ph:
                    softmax(nc, ph, T, layer)
                with Phase(nc, f"combine{layer}") as ph:
                    combine(nc, ph, T, layer)
            with Phase(nc, "nodes2") as ph:
                nodes(nc, ph, T, gnn, 2)
        experts(nc, T, ffn, out)


def blocks(eng, body):
    with eng.Fori(0, NB // 2) as n:
        for k in range(2):
            body(2 * n + k, k, n)
    body(NB - 1, 0, NB // 2)


def make_tables(nc, ph, T, x, src, dst):
    sb, sem = ph.sb, ph.sem
    src_i = sb("src_i", [ECH, E // ECH], I32)
    dst_i = sb("dst_i", [ECH, E // ECH], I32)
    dst_f = sb("dst_f", [ECH, E // ECH])
    junk = sb("junk", [ECH, 2, E // ECH])
    pad_i = sb("pad_i", [1, 2, EROWS * P - E], I32)
    iot = sb("iot", [P, P], I32)
    iot_p = sb("iot_p", [P, 1], I32)
    iot_g = sb("iot_g", [Q, GQ], I32)
    thr = sb("thr", [P, NB + 1])
    blk = sb("blk", [P, NB])
    below = sb("below", [ECH, NB + 1])
    off = sb("off", [P, NB + 1])
    off_i = sb("off_i", [P, 2, NB + 1], I32)
    row_i = sb("row_i", [P, 2, NB + 1], I32)
    row_f = sb("row_f", [P, 2, NB + 1])
    n_i = sb("n_i", [P, NB], I32)
    ngi = sb("ngi", [P, NB], I32)
    n_f = sb("n_f", [P, 2, NB])
    t_in = sb("t_in", [P, NB])
    t_ex = sb("t_ex", [P, NB])
    g_id = sb("g_id", [Q, GQ])
    big4 = sb("big4", [Q, 5, GQ, NB])
    b_g = sb("b_g", [Q, GQ])
    sel = sb("sel", [Q, 6, GQ])
    dump4 = sb("dump4", [Q, GQ])
    rows_s = sb("rows_s", [Q, J], I32)
    tab_i = sb("tab_i", [Q, 2, GQ], I32)
    srcT_i = sb("srcT_i", [Q, TL], I32)
    dstT_i = sb("dstT_i", [Q, TL], I32)
    srcT = sb("srcT", [Q, TL])
    dstT = sb("dstT", [Q, TL])
    relT = sb("relT", [Q, TL])
    valid = sb("valid", [Q, TL])
    rel16 = sb("rel16", [Q, TL], BF16)
    keyx = sb("keyx", [Q, TL + 2])
    cuts = sb("cuts", [Q, 2, H1])
    edge_pad = sb("edge_pad", [1, 2])

    in_loaded = [sem(f"in_loaded{i}") for i in range(3)]
    x_loaded = sem("x_loaded")
    rows_stored = sem("rows_stored")
    const_done = sem("const_done")
    dve_done = sem("tables_dve")
    off_counted = sem("off_counted")
    rows_gathered = sem("rows_gathered")
    keys_stored = sem("keys_stored")
    tabs_stored = sem("tabs_stored")
    keys_back = sem("keys_back")
    tabs_back = sem("tabs_back")
    turned = sem("turned")
    turned_copied = sem("turned_copied")
    psum = T["psum"]

    with nc.Block() as block:
        V_BELOW, V_ROWS, V_TABS, V_KEYS, V_TURN = [0], [0], [0], [0], [0, 0]

        @block.vector
        def _(dve):
            done = Mark(dve_done)

            def after(n):
                dve.wait_ge(dve_done, n)

            def link(ins):
                after(done(ins))

            dve.wait_ge(const_done, 11)
            for c in range(2):
                done(dve.tensor_copy(T["lane"][:, c, :], iot[:]))
            done(dve.tensor_copy(T["part"][:], iot_p[:]))
            done(dve.tensor_copy(g_id[:], iot_g[:]))
            done(dve.tensor_copy(blk[:], iot[:, 0:NB]))
            done(dve.tensor_scalar(thr[:], iot[:, 0:NB + 1], float(P), None, ALU.mult))
            done(dve.memset(below[:, 0:1], 0.0))
            done(dve.memset(below[:, NB:], float(E // ECH)))
            dve.wait_ge(in_loaded[0], 16)
            link(dve.tensor_copy(dst_f[:], dst_i[:]))
            for b in range(1, NB):
                dve.wait_ge(dve_done, done.n - 1)
                done(dve.tensor_scalar(junk[:, b % 2], dst_f[:], float(P * b), 0.0, ALU.is_lt, ALU.add,
                                       accum_out=below[:, b:b + 1]))
            V_BELOW[0] = done.n
            dve.wait_ge(off_counted, 1)
            link(dve.tensor_copy(off[:], psum[:, 0, 0:NB + 1]))
            done(dve.tensor_copy(off_i[:, 0, :], off[:]))
            link(dve.tensor_scalar(off_i[:, 1, :], off[:], float(P - 1), None, ALU.add))
            link(dve.tensor_scalar(row_i[:], off_i[:], 7, None, ALU.arith_shift_right))
            link(dve.tensor_copy(row_f[:], row_i[:]))
            link(dve.tensor_tensor(n_f[:, 0, :], row_f[:, 1, 1:], row_f[:, 0, 0:NB], ALU.subtract))
            link(dve.tensor_scalar(n_i[:], n_f[:, 0, :], 1.0, 1.0, ALU.max, ALU.add))
            link(dve.tensor_scalar(ngi[:], n_i[:], 1, None, ALU.arith_shift_right))
            link(dve.tensor_copy(n_f[:, 1, :], ngi[:]))
            link(dve.tensor_tensor_scan(t_in[:], T["ones"][:, 0:NB], n_f[:, 1, :], 0.0, ALU.mult, ALU.add))
            link(dve.tensor_tensor(t_ex[:], t_in[:], n_f[:, 1, :], ALU.subtract))
            sh = [Q, GQ, NB]
            tin_b, tex_b = bcast_mid(t_in[0:Q], GQ), bcast_mid(t_ex[0:Q], GQ)
            gid_b = bcast_last(g_id[:], NB)
            link(dve.tensor_tensor(big4[:, 0], tin_b, gid_b, ALU.is_le))
            link(dve.tensor_reduce(b_g[:], big4[:, 0], AX.X, ALU.add))
            link(dve.tensor_scalar(b_g[:], b_g[:], float(NB - 1), None, ALU.min))
            link(dve.tensor_tensor(big4[:, 1], bcast_mid(blk[0:Q], GQ), bcast_last(b_g[:], NB), ALU.is_equal))
            done(dve.tensor_tensor(big4[:, 2], big4[:, 1], tex_b, ALU.mult))
            done(dve.tensor_tensor(big4[:, 3], big4[:, 1], bcast_mid(row_f[0:Q, 0, 0:NB], GQ), ALU.mult))
            done(dve.tensor_scalar(sel[:, 4, :], g_id[:], 1.0, None, ALU.add))
            after(done.n)
            link(dve.tensor_tensor(big4[:, 4], tin_b, bcast_last(sel[:, 4, :], NB), ALU.is_equal))
            done(dve.tensor_reduce(sel[:, 0, :], big4[:, 2], AX.X, ALU.add))
            done(dve.tensor_reduce(sel[:, 1, :], big4[:, 3], AX.X, ALU.add))
            link(dve.tensor_reduce(sel[:, 2, :], big4[:, 4], AX.X, ALU.add))
            link(dve.tensor_tensor(sel[:, 5, :], g_id[:], sel[:, 0, :], ALU.subtract))
            done(dve.tensor_scalar(sel[:, 3, :], sel[:, 5, :], 0.5, None, ALU.is_gt))
            link(dve.tensor_scalar(sel[:, 5, :], sel[:, 5, :], 2.0, None, ALU.mult))
            link(dve.tensor_tensor(sel[:, 5, :], sel[:, 5, :], sel[:, 1, :], ALU.add))
            rows_v = rows_s[:].rearrange("q (g t) -> q g t", t=2)
            done(dve.tensor_scalar(rows_v[:, :, 0], sel[:, 5, :], float(ROWS), None, ALU.min))
            link(dve.tensor_scalar(rows_v[:, :, 1], sel[:, 5, :], float(ROWS), 1.0, ALU.min, ALU.add))
            V_ROWS[0] = done.n
            link(dve.tensor_scalar(sel[:, 0, :], b_g[:], float(P), None, ALU.mult))
            done(dve.tensor_copy(tab_i[:, 0, :], sel[:, 0, :]))
            link(dve.tensor_scalar(dump4[:], T["lane"][0:Q, 0, 0:GQ], float(P), float(NPAD), ALU.mult, ALU.add))
            link(dve.tensor_tensor(sel[:, 1, :], sel[:, 0, :], dump4[:], ALU.subtract))
            link(dve.tensor_tensor(sel[:, 1, :], sel[:, 1, :], sel[:, 2, :], ALU.mult))
            link(dve.tensor_tensor(tab_i[:, 1, :], sel[:, 1, :], dump4[:], ALU.add))
            V_TABS[0] = done.n
            dve.wait_ge(rows_gathered, 16 * 2 * J)
            done(dve.tensor_copy(srcT[:], srcT_i[:]))
            V_TURN[0] = done.n
            link(dve.tensor_copy(dstT[:], dstT_i[:]))
            g3 = lambda t: t[:].rearrange("q (g l) -> q g l", g=GQ)
            link(dve.tensor_tensor(g3(relT), g3(dstT), bcast_last(sel[:, 0, :], 2 * P), ALU.subtract))
            done(dve.tensor_copy(rel16[:], relT[:]))
            link(dve.tensor_scalar(valid[:], relT[:], 0.0, None, ALU.is_ge))
            link(dve.scalar_tensor_tensor(valid[:], relT[:], float(P), valid[:], ALU.is_lt, ALU.mult))
            done(dve.tensor_scalar(T["invalid"][:], valid[:], -1.0, BIG, ALU.add, ALU.mult))
            link(dve.scalar_tensor_tensor(dstT[:], dstT[:], 1.0, valid[:], ALU.add, ALU.mult))
            link(dve.tensor_scalar(keyx[:, 1:1 + TL], dstT[:], -1.0, None, ALU.add))
            V_KEYS[0] = done.n
            dve.wait_ge(keys_back, 32)
            cut = T["turn_cut"]
            link(dve.tensor_tensor(cut[:], keyx[:, 0:TL + 1], keyx[:, 1:TL + 2], ALU.not_equal))
            link(dve.tensor_scalar(cut[:], cut[:], -BIG, None, ALU.mult))
            done(dve.scalar_tensor_tensor(T["is_last"][:], cut[:, 1:], -1.0, valid[:], ALU.is_lt, ALU.mult))
            done(dve.tensor_reduce(dump4[:, 0:1], cut[:, 0:TL], AX.X, ALU.min))
            link(dve.tensor_reduce(dump4[:, 1:2], cut[:, 1:], AX.X, ALU.min))
            done(dve.tensor_copy(cuts[:], bcast_last(dump4[:, 0:2], H1)))
            V_TURN[1] = done.n
            for n in range(6):
                dve.wait_ge(turned, n + 1)
                h = n % 2
                ps = psum[:, 1 + n, :].rearrange("p (j l) -> p j l", j=4)[:, :, 0:Q]
                if n < 2:
                    to = T["src_lane"][:, 0:NS]
                elif n < 4:
                    to = T["rel_lane"][:]
                else:
                    to = T["aux"][:, :, AUXW - 1]
                to = to.rearrange("p (q j) -> p j q", j=J)[:, 4 * h:4 * h + 4, :]
                done(dve.tensor_copy(to, ps))
            dve.wait_ge(turned, 7)
            for c in range(2):
                done(dve.tensor_copy(T["cut_any"][:, c, :], psum[0:H1, 7, c * P:c * P + Q]))

        @block.gpsimd
        def _(pool):
            pool.memset(T["ones"][:], 1.0).then_inc(const_done, 1)
            pool.wait_ge(const_done, 1)
            pool.affine_select(out=T["ident"][:], in_=T["ones"][:], compare_op=ALU.is_equal, fill=0.0, base=0,
                               pattern=[[-1, P]], channel_multiplier=1).then_inc(const_done, 1)
            pool.iota(iot[:], pattern=[[1, P]], base=0, channel_multiplier=0).then_inc(const_done, 1)
            pool.iota(iot_p[:], pattern=[[0, 1]], base=0, channel_multiplier=1).then_inc(const_done, 1)
            pool.iota(iot_g[:], pattern=[[1, GQ]], base=0, channel_multiplier=GQ).then_inc(const_done, 1)
            pool.memset(pad_i[:, 0, :], 0).then_inc(const_done, 1)
            pool.memset(pad_i[:, 1, :], 1 << 20).then_inc(const_done, 1)
            pool.memset(T["x"][:, NB - 1, :], 0.0).then_inc(const_done, 1)
            pool.memset(edge_pad[:], -2.0).then_inc(const_done, 1)
            pool.memset(T["src_lane"][:, NS:], 0).then_inc(const_done, 1)
            pool.memset(T["eps"][:], EPS).then_inc(const_done, 1)
            pool.wait_ge(dve_done, V_ROWS[0])
            pool.wait_ge(rows_stored, 64)
            for j in range(J):
                for table, to in ((T["src_rows"], srcT_i), (T["dst_rows"], dstT_i)):
                    pool.indirect_dma_start(
                        out=to[:, j * P:(j + 1) * P], out_offset=None, in_=table,
                        in_offset=bass.IndirectOffsetOnAxis(ap=rows_s[:, j:j + 1], axis=0),
                        bounds_check=EROWS - 1, oob_is_err=False).then_inc(rows_gathered, 16)

        @block.sync
        def _(sp):
            sp.dma_start(dst_i[:], dst.rearrange("(p f) -> p f", p=ECH)).then_inc(in_loaded[0], 16)
            sp.dma_start(src_i[:], src.rearrange("(p f) -> p f", p=ECH)).then_inc(in_loaded[1], 16)
            sp.wait_ge(const_done, 11)
            sp.dma_start(T["x"][:, 0:NB - 1, :], x[0:P * (NB - 1)].rearrange("(b p) d -> p b d", p=P)
                         ).then_inc(x_loaded, 16)
            sp.dma_start(T["x"][0:LAST, NB - 1, :], x[P * (NB - 1):N]).then_inc(x_loaded, 16)
            flat_s = T["src_rows"].rearrange("r l -> (r l)")
            flat_d = T["dst_rows"].rearrange("r l -> (r l)")
            sp.wait_ge(in_loaded[0], 16)
            sp.dma_start(flat_d[0:E].rearrange("(p f) -> p f", p=ECH), dst_i[:]).then_inc(rows_stored, 16)
            sp.dma_start(flat_d[E:].rearrange("(o f) -> o f", o=1), pad_i[:, 1, :]).then_inc(rows_stored, 16)
            sp.wait_ge(in_loaded[1], 16)
            sp.dma_start(flat_s[0:E].rearrange("(p f) -> p f", p=ECH), src_i[:]).then_inc(rows_stored, 16)
            sp.dma_start(flat_s[E:].rearrange("(o f) -> o f", o=1), pad_i[:, 0, :]).then_inc(rows_stored, 16)
            sp.wait_ge(dve_done, V_TABS[0])
            for n, name in enumerate(("block_row", "sum_row")):
                sp.dma_start(T[name].rearrange("(q g) -> q g", q=Q), tab_i[:, n, :]).then_inc(tabs_stored, 16)
            sp.dma_start(T["keep"].rearrange("(q g) -> q g", q=Q), sel[:, 3, :]).then_inc(tabs_stored, 16)
            sp.wait_ge(tabs_stored, 48)
            sp.dma_start(T["block_row_s"][:], T["block_row"].unsqueeze(0)).then_inc(tabs_back, 16)
            sp.dma_start(T["sum_row_s"][:], T["sum_row"].unsqueeze(0)).then_inc(tabs_back, 16)
            sp.dma_start(T["keep_s"][:], T["keep"].partition_broadcast(P)).then_inc(tabs_back, 16)
            sp.wait_ge(dve_done, V_KEYS[0])
            sp.dma_start(T["keys"][1:1 + Q * TL].rearrange("(q l) -> q l", q=Q), keyx[:, 1:1 + TL]
                         ).then_inc(keys_stored, 16)
            sp.dma_start(T["keys"][0:1].unsqueeze(0), edge_pad[:, 0:1]).then_inc(keys_stored, 16)
            sp.dma_start(T["keys"][1 + Q * TL:].unsqueeze(0), edge_pad[:, 1:2]).then_inc(keys_stored, 16)
            sp.dma_start(T["rel"][0:Q * TL].rearrange("(q l) -> q l", q=Q), rel16[:]).then_inc(keys_stored, 16)
            sp.dma_start(T["rel"][Q * TL:].unsqueeze(0), rel16[0:1, :]).then_inc(keys_stored, 16)
            sp.wait_ge(keys_stored, 80)
            sp.dma_start(keyx[:, 0:1], T["keys"][0:Q * TL].rearrange("(q l) -> q l", q=Q)[:, 0:1],
                         allow_slow_non_contiguous=True).then_inc(keys_back, 16)
            sp.dma_start(keyx[:, TL + 1:], T["keys"][2:2 + Q * TL].rearrange("(q l) -> q l", q=Q)[:, TL - 1:],
                         allow_slow_non_contiguous=True).then_inc(keys_back, 16)
            sp.wait_ge(tabs_back, 48)
            sp.wait_ge(x_loaded, 32)

        @block.tensor
        def _(pe):
            pe.wait_ge(dve_done, V_BELOW[0])
            pe.matmul(psum[:, 0, 0:NB + 1], T["ones"][0:ECH, :], below[:], start=True, stop=True
                      ).then_inc(off_counted, 1)
            for n in range(6):
                pe.wait_ge(dve_done, V_TURN[0] if n < 2 else V_TURN[1])
                what = (srcT, relT, T["is_last"])[n // 2]
                for j in range(4):
                    jj = 4 * (n % 2) + j
                    ins = pe.transpose(psum[:, 1 + n, j * P:j * P + Q], what[:, jj * P:(jj + 1) * P],
                                       T["ident"][0:Q, 0:Q])
                ins.then_inc(turned, 1)
            for c in range(2):
                ins = pe.transpose(psum[0:H1, 7, c * P:c * P + Q], cuts[:, c, :], T["ident"][0:Q, 0:Q])
            ins.then_inc(turned, 1)


def heads_of(ap, heads):
    return ap.rearrange("p (h c) -> p h c", h=heads)


def at_block(t, i):
    return t[:, bass.ds(i, 1), :].rearrange("p o f -> p (o f)")


def nodes(nc, ph, T, gnn, phase):
    sb, sem = ph.sb, ph.sem
    psum = T["psum"]
    merging, projecting = phase > 0, phase < 2
    heads = H1 if phase == 0 else 1
    old = H1 if phase == 1 else 1
    h = sb("h", [P, 2, D])
    stats = sb("stats", [P, NB, 6])
    mean_var = sb("mean_var", [P, NB, 2])
    rstd = sb("rstd", [P, 2, NB])
    if projecting:
        w_l, w_r, att, _ = gnn[phase]
        w = sb("w", [P, 2, 2, W])
        att_row = sb("att_row", [P, D])
        att_lin = sb("att_lin", [P, D])
        att_relu = sb("att_relu", [P, D])
        w_att = sb("w_att", [P, 4, D])
        hT = sb("hT", [P, 2, 2, P])
        proj = sb("proj", [P, 2, 2, W])
        m_self = sb("m_self", [P, 2, W])
        r_self = sb("r_self", [P, 2, D])
        red = sb("red", [P, 2, H1])
    if merging:
        bias = gnn[phase - 1][3]
        bias_row = sb("bias_row", [P, D])
        aux = sb("aux_sums", [P, NB, AUXW])
        sm = sb("sm", [P, 8, NB, old])
        sums, own, va, vb, v, e_pos, e_neg, e_exp = (
            sb(n, [P, 2, D]) for n in ("sums", "own", "va", "vb", "v", "e_pos", "e_neg", "e_exp"))
        wa, wb = sm[:, 5], sm[:, 6]

    weights_in, self_in = sem("weights_in"), sem("aux_in")
    chain, chain_pool = sem("chain"), sem("chain_pool")
    stats_done, exp_ready, exp_done, wts_ready = sem("stats_done"), sem("exp_ready"), sem("exp_done"), sem("wts_ready")
    w_ready = sem("w_ready")
    h_ready, h_turned, turned_sb = sem("h_ready"), sem("h_turned"), sem("turned_sb")
    projected, xl_copied, xr_copied = sem("projected"), sem("xl_copied"), sem("xr_copied")
    m_done, relu_done, red_done, self_done = sem("m_done"), sem("relu_done"), sem("red_done"), sem("self_done")
    a_done, b_done, b_steps, v_ready, elu_steps = sem("a_done"), sem("b_done"), sem("b_steps"), sem("v_ready"), sem("elu_steps")
    x_done = sem("x_done")
    out_l = [sem(f"xl_out{k}") for k in range(2)]
    out_r = [sem(f"xr_out{k}") for k in range(2)]
    sums_in = [sem(f"sums_in{k}") for k in range(2)]
    own_in = [sem(f"own_in{k}") for k in range(2)]
    n_weights = 5 * projecting + merging

    with nc.Block() as block:
        @block.vector
        def _(dve):
            done = Mark(chain)

            def link(ins):
                dve.wait_ge(chain, done(ins))

            if phase == 0:
                for i in range(NB):
                    done(dve.bn_stats(stats[:, i, :], T["x"][:, i, :]))
                dve.wait_ge(chain, done.n)
                for i in range(NB):
                    dve.bn_aggr(mean_var[:, i, :], stats[:, i, :]).then_inc(stats_done, 1)
                dve.wait_ge(exp_done, 1)
                link(dve.reciprocal(rstd[:, 1, :], rstd[:, 0, :]))
            if merging:
                dve.sem_inc(v_ready, 2)
                dve.wait_ge(self_in, 16)
                me, mm, d1, d2, den, _, _, t = (sm[:, n] for n in range(8))
                own_l = T["self_logits"][:, :, 0:old]
                link(dve.tensor_scalar(t, aux[:, :, 2 * H1:2 * H1 + 1].broadcast_to([P, NB, old]), -1.0, BIG,
                                       ALU.add, ALU.mult))
                link(dve.tensor_tensor(me, aux[:, :, H1:H1 + old], t, ALU.add))
                link(dve.tensor_tensor(mm, me, own_l, ALU.max))
                dve.tensor_tensor(d1, me, mm, ALU.subtract).then_inc(exp_ready, 1)
                dve.tensor_tensor(d2, own_l, mm, ALU.subtract).then_inc(exp_ready, 1)
                dve.wait_ge(exp_done, 2)
                link(dve.tensor_tensor(den, aux[:, :, 0:old], d1, ALU.mult))
                link(dve.tensor_tensor(den, den, d2, ALU.add))
                link(dve.reciprocal(t, den))
                dve.tensor_tensor(wa, d1, t, ALU.mult).then_inc(wts_ready, 1)
                dve.tensor_tensor(wb, d2, t, ALU.mult).then_inc(wts_ready, 1)
                dve.wait_ge(wts_ready, 2)
            if projecting:
                dve.wait_ge(weights_in, 16 * n_weights)
                done(dve.tensor_scalar(att_relu[:], att_row[:], 0.8, None, ALU.mult))
                link(dve.tensor_scalar(att_lin[:], att_row[:], 0.2, None, ALU.mult))
                link(dve.memset(w[:, :, :, D:], 0.0))
                link(dve.tensor_tensor(w_att[:], w[:, :, :, 0:D].rearrange("p a b c -> p (a b) c"),
                                       bcast_mid(att_lin[:], 4), ALU.mult))
                for a in range(4):
                    dve.tensor_reduce(w[:, a // 2, a % 2, D:D + heads], heads_of(w_att[:, a, :], heads),
                                      AX.X, ALU.add).then_inc(w_ready, 1)

            def normalised(i, k, n):
                dve.wait_ge(h_turned, i + 1)
                dve.tensor_scalar(h[:, k, :], at_block(T["x"], i), mean_var[:, bass.ds(i, 1), 0],
                                  rstd[:, 1, bass.ds(i, 1)], ALU.subtract, ALU.mult).then_inc(h_ready, 1)

            def merged(i, k, n):
                dve.wait_ge(sums_in[k], 16 * (n + 1))
                dve.tensor_tensor(heads_of(va[:, k, :], old), heads_of(sums[:, k, :], old),
                                  bcast_last(at_block(wa, i), D // old), ALU.mult).then_inc(a_done, 1)
                dve.wait_ge(a_done, i + 1)
                dve.wait_ge(b_done, i + 1)
                if phase == 1:
                    dve.wait_ge(elu_steps, 3 * i + 3)
                dve.tensor_tensor(v[:, k, :], va[:, k, :], vb[:, k, :], ALU.add).then_inc(v_ready, 1)
                if phase == 1:
                    dve.wait_ge(elu_steps, 3 * i + 9)
                    dve.wait_ge(h_turned, i + 1)
                    dve.scalar_tensor_tensor(h[:, k, :], e_exp[:, k, :], -1.0, e_pos[:, k, :], ALU.add, ALU.add
                                             ).then_inc(h_ready, 1)
                else:
                    dve.wait_ge(v_ready, i + 3)
                    dve.tensor_tensor(at_block(T["x"], i), at_block(T["x"], i), v[:, k, :], ALU.add
                                      ).then_inc(x_done, 1)

            def own_logits(i, k, n):
                dve.wait_ge(projected, 2 * i + 2)
                dve.wait_ge(out_r[k], 16 * n)
                dve.wait_ge(m_done, i + 1)
                dve.tensor_copy(proj[:, k, 1, :], psum[:, 4 + k, 0:W]).then_inc(xr_copied, 1)
                dve.wait_ge(m_done, i + 3)
                dve.wait_ge(red_done, i)
                dve.scalar_tensor_tensor(r_self[:, k, :], m_self[:, k, 0:D], 0.0, att_relu[:], ALU.max, ALU.mult
                                         ).then_inc(relu_done, 1)
                dve.wait_ge(relu_done, i + 1)
                dve.wait_ge(self_done, i + 1)
                dve.tensor_reduce(red[:, k, 0:heads], heads_of(r_self[:, k, :], heads), AX.X, ALU.add
                                  ).then_inc(red_done, 1)

            def body(i, k, n):
                merged(i, k, n) if merging else normalised(i, k, n)
                if projecting:
                    own_logits(i, k, n)

            blocks(dve, body)

        @block.scalar
        def _(act):
            if phase == 0:
                act.wait_ge(stats_done, NB)
                act.activation(rstd[:, 0, :], mean_var[:, :, 1], ACT.Sqrt, bias=T["eps"][:]).then_inc(exp_done, 1)
            if merging:
                act.sem_inc(elu_steps, 6)
                act.wait_ge(exp_ready, 2)
                for d in (2, 3):
                    act.activation(sm[:, d], sm[:, d], ACT.Exp).then_inc(exp_done, 1)

            def body(i, k, n):
                if phase == 1:
                    act.wait_ge(v_ready, i + 3)
                    act.wait_ge(h_ready, i)
                    act.activation(e_pos[:, k, :], v[:, k, :], ACT.Relu).then_inc(elu_steps, 1)
                    act.activation(e_neg[:, k, :], v[:, k, :], ACT.Relu, scale=-1.0).then_inc(elu_steps, 1)
                    act.wait_ge(elu_steps, 3 * i + 8)
                    act.activation(e_exp[:, k, :], e_neg[:, k, :], ACT.Exp, scale=-1.0).then_inc(elu_steps, 1)
                act.wait_ge(h_turned, i + 3)
                act.wait_ge(projected, 2 * i)
                act.copy(hT[:, k].rearrange("p a f -> p (a f)"), psum[:, k, 0:D]).then_inc(turned_sb, 1)
                act.wait_ge(projected, 2 * i + 1)
                act.wait_ge(out_l[k], 16 * n)
                act.wait_ge(m_done, i + 1)
                act.copy(proj[:, k, 0, :], psum[:, 2 + k, 0:W]).then_inc(xl_copied, 1)

            if projecting:
                blocks(act, body)

        @block.tensor
        def _(pe):
            def body(i, k, n):
                pe.wait_ge(h_ready, i + 1)
                pe.wait_ge(turned_sb, i)
                for a in range(2):
                    ins = pe.transpose(psum[:, k, a * P:(a + 1) * P], h[:, k, a * P:(a + 1) * P], T["ident"][:])
                ins.then_inc(h_turned, 1)
                pe.wait_ge(turned_sb, i + 1)
                pe.wait_ge(xl_copied, i)
                for side in range(2):
                    if side == 1:
                        pe.wait_ge(xr_copied, i)
                    for a in range(2):
                        ins = pe.matmul(psum[:, 2 + 2 * side + k, 0:W], hT[:, k, a, :], w[:, a, side, :],
                                        start=a == 0, stop=a == 1)
                    ins.then_inc(projected, 1)

            if projecting:
                pe.sem_inc(h_turned, 2)
                pe.wait_ge(w_ready, 4)
                blocks(pe, body)

        @block.gpsimd
        def _(pool):
            if projecting:
                pool.sem_inc(m_done, 2)
                pool.sem_inc(self_done, 2)
            if merging:
                pool.wait_ge(weights_in, 16 * n_weights)
                pool.wait_ge(wts_ready, 2)

            def body(i, k, n):
                if merging:
                    pool.wait_ge(own_in[k], 16 * (n + 1))
                    pool.wait_ge(v_ready, i + 1)
                    pool.tensor_tensor(heads_of(vb[:, k, :], old), heads_of(own[:, k, :], old),
                                       bcast_last(at_block(wb, i), D // old), ALU.mult).then_inc(b_steps, 1)
                    pool.wait_ge(b_steps, i + 1)
                    pool.tensor_tensor(vb[:, k, :], vb[:, k, :], bias_row[:], ALU.add).then_inc(b_done, 1)
                if projecting:
                    pool.wait_ge(xl_copied, i + 1)
                    pool.wait_ge(xr_copied, i + 1)
                    pool.wait_ge(self_done, i + 1)
                    pool.tensor_tensor(m_self[:, k, :], proj[:, k, 0, :], proj[:, k, 1, :], ALU.add
                                       ).then_inc(m_done, 1)
                    pool.wait_ge(m_done, i + 3)
                    pool.wait_ge(red_done, i + 1)
                    pool.tensor_tensor(at_block(T["self_logits"], i)[:, 0:heads], red[:, k, 0:heads],
                                       m_self[:, k, D:D + heads], ALU.add).then_inc(self_done, 1)

            blocks(pool, body)

        @block.sync
        def _(sp):
            if projecting:
                for side, m in enumerate((w_l, w_r)):
                    for a in range(2):
                        sp.dma_start(w[:, a, side, 0:D], m[a * P:(a + 1) * P, :]).then_inc(weights_in, 16)
                sp.dma_start(att_row[:], att.rearrange("h c -> (h c)").partition_broadcast(P)).then_inc(weights_in, 16)
            if merging:
                sp.dma_start(bias_row[:], bias.partition_broadcast(P)).then_inc(weights_in, 16)
                sp.dma_start(aux[:], T["sums"][0:NPAD, D:AW].rearrange("(b p) a -> p b a", p=P)).then_inc(self_in, 16)

            def load(i, k):
                if merging:
                    sp.wait_ge(v_ready, i + 1)
                    sp.dma_start(sums[:, k, :], T["sums"][bass.ds(i * P, P), 0:D]).then_inc(sums_in[k], 16)
                    sp.dma_start(own[:, k, :], T["xl"][bass.ds(i * P, P), 0:D]).then_inc(own_in[k], 16)

            def store(i, k):
                if projecting:
                    sp.wait_ge(xl_copied, i + 1)
                    sp.dma_start(T["xl"][bass.ds(i * P, P), :], proj[:, k, 0, :]).then_inc(out_l[k], 16)
                    sp.wait_ge(xr_copied, i + 1)
                    sp.dma_start(T["xr"][bass.ds(i * P, P), :], proj[:, k, 1, :]).then_inc(out_r[k], 16)

            load(0, 0)
            with sp.Fori(0, NB // 2) as n:
                load(2 * n + 1, 1)
                store(2 * n, 0)
                load(2 * n + 2, 0)
                store(2 * n + 1, 1)
            store(NB - 1, 0)
            if projecting:
                for k in range(2):
                    uses = NB // 2 + (k == 0)
                    sp.wait_ge(out_l[k], 16 * uses)
                    sp.wait_ge(out_r[k], 16 * uses)


def score(nc, ph, T, weights, layer):
    sb, sem = ph.sb, ph.sem
    psum = T["psum"]
    heads = H1 if layer == 0 else 1
    ITER = NS // RING
    HALF = RING // 2
    G = RING // 2
    XR = 4
    BANKS = 8
    xg = sb("xg", [P, RING, W])
    xr = sb("xr", [P, XR, W])
    index = sb("index", [P, 2, HALF], I32)
    rel_row = sb("rel_row", [P, 2, HALF * P], BF16)
    pick = sb("pick", [P, 2, HALF * P])
    relu = sb("relu", [P, 2, 2, D])
    red = sb("red", [P, 2, 2, H1])
    att_row = sb("att_row", [P, D])
    att_relu = sb("att_relu", [P, D])
    landed = [sem(f"landed{k}") for k in range(RING)]
    spilled = [sem(f"spilled{k}") for k in range(G)]
    xr_in = [sem(f"xr_in{k}") for k in range(XR)]
    rel_in = [sem(f"rel_in{k}") for k in range(2)]
    att_in, att_done, index_done = sem("att_in"), sem("att_done"), sem("index_done")
    asked = sem("asked")
    picked, mm_done, ps_free = sem("picked"), sem("mm_done"), sem("ps_free")
    relu_done, red_done = sem("relu_done"), sem("red_done")

    with nc.Block() as block:
        @block.gpsimd
        def _(pool):
            with pool.Fori(0, ITER) as i:
                for k in range(RING):
                    if k % HALF == 0:
                        pool.wait_ge(index_done, 2 * i + k // HALF + 1)
                    pool.wait_ge(mm_done, RING * i + k + 1)
                    pool.wait_ge(spilled[k // 2], 16 * i)
                    pool.sem_inc(asked, 1)
                    pool.indirect_dma_start(
                        out=xg[:, k, :], out_offset=None, in_=T["xl"],
                        in_offset=bass.IndirectOffsetOnAxis(ap=index[:, k // HALF, k % HALF:k % HALF + 1], axis=0),
                        bounds_check=NPAD - 1, oob_is_err=False).then_inc(landed[k], 16)

        @block.scalar
        def _(act):
            def indices(half, first):
                act.copy(index[:, half, :], T["src_lane"][:, bass.ds(first, HALF)]).then_inc(index_done, 1)

            indices(0, 0)
            indices(1, HALF)
            with act.Fori(0, ITER) as i:
                for g in range(G):
                    act.wait_ge(landed[2 * g], 16 * (i + 1))
                    act.wait_ge(landed[2 * g + 1], 16 * (i + 1))
                    act.dma_start(T["edges_xl"][bass.ds(G * i + g, 1)].rearrange("o p f -> p (o f)"),
                                  xg[:, 2 * g:2 * g + 2, :].rearrange("p t f -> p (t f)")).then_inc(spilled[g], 16)
                    if g % (G // 2) == G // 2 - 1:
                        half = g // (G // 2)
                        indices(half, RING * i + RING + HALF * half)
            for g in range(G):
                act.wait_ge(spilled[g], 16 * ITER)

        @block.sync
        def _(sp):
            sp.dma_start(att_row[:], weights[2].rearrange("h c -> (h c)").partition_broadcast(P)).then_inc(att_in, 16)
            sp.sem_inc(picked, 2)

            def rel_rows(half_id, half):
                sp.wait_ge(picked, half_id + 1)
                sp.dma_start(rel_row[:, half, :], T["rel"][bass.ds(HALF * P * half_id, HALF * P)].partition_broadcast(P)
                             ).then_inc(rel_in[half], 16)

            rel_rows(0, 0)
            with sp.Fori(0, ITER) as i:
                for g in range(G):
                    if g == 0:
                        rel_rows(2 * i + 1, 1)
                    if g == G // 2:
                        rel_rows(2 * i + 2, 0)
                    row = sp.value_load(T["block_row_s"][0:1, bass.ds(G * i + g, 1)], min_val=0, max_val=NPAD - P)
                    sp.wait_ge(mm_done, RING * i + 2 * g + RING + 2 - 2 * XR)
                    sp.dma_start(xr[:, g % XR, :], T["xr"][bass.ds(row, P), :]).then_inc(xr_in[g % XR], 16)

        @block.tensor
        def _(pe):
            pe.sem_inc(mm_done, RING)
            with pe.Fori(0, ITER) as i:
                for k in range(RING):
                    g = k // 2
                    bank = k % BANKS
                    if k % HALF == 0:
                        pe.wait_ge(picked, 2 * i + k // HALF + 3)
                    if k % 2 == 0:
                        pe.wait_ge(xr_in[g % XR], 16 * (G // XR * i + g // XR + 1))
                        pe.wait_ge(ps_free, G * i + g + 1)
                    pe.wait_ge(landed[k], 16 * (i + 1))
                    pe.matmul(psum[:, bank, 0:W], T["ident"][:], xg[:, k, :], start=True, stop=False)
                    pe.matmul(psum[:, bank, 0:W], pick[:, k // HALF, (k % HALF) * P:(k % HALF + 1) * P],
                              xr[:, g % XR, :], start=False, stop=True).then_inc(mm_done, 1)

        @block.vector
        def _(dve):
            dve.sem_inc(ps_free, BANKS // 2)
            dve.wait_ge(att_in, 16)
            dve.tensor_scalar(att_relu[:], att_row[:], 0.8, None, ALU.mult).then_inc(att_done, 1)
            dve.wait_ge(att_done, 1)

            def make_pick(i, half):
                dve.wait_ge(rel_in[half], 16 * (i + 1))
                dve.wait_ge(mm_done, RING * i + HALF * (half + 1))
                dve.tensor_scalar(pick[:, half, :], rel_row[:, half, :], T["part"][:], None, ALU.is_equal
                                  ).then_inc(picked, 1)

            make_pick(0, 0)
            with dve.Fori(0, ITER) as i:
                for g in range(G):
                    if g == 1:
                        make_pick(i, 1)
                    if g == 5:
                        make_pick(i + 1, 0)
                    pair, b = g % 2, 2 * g % BANKS
                    step = RING * i + 2 * g
                    dve.wait_ge(mm_done, step + RING + 2)
                    dve.scalar_tensor_tensor(relu[:, pair], psum[:, b:b + 2, 0:D], 0.0, bcast_mid(att_relu[:], 2),
                                             ALU.max, ALU.mult).then_inc(relu_done, 1)
                    dve.wait_ge(relu_done, G * i + g + 1)
                    dve.tensor_reduce(red[:, pair, :, 0:heads],
                                      relu[:, pair].rearrange("p t (h c) -> p t h c", h=heads), AX.X, ALU.add
                                      ).then_inc(red_done, 1)
                    dve.wait_ge(red_done, G * i + g + 1)
                    dve.tensor_tensor(T["logits"][:, bass.ds(step, 2), 0:heads], red[:, pair, :, 0:heads],
                                      psum[:, b:b + 2, D:D + heads], ALU.add).then_inc(ps_free, 1)


def softmax(nc, ph, T, layer):
    sb, sem = ph.sb, ph.sem
    psum = T["psum"]
    heads = H1 if layer == 0 else 1
    lg = sb("lg", [Q, H1, TL])
    fwd = sb("fwd", [Q, H1, TL])
    scratch = sb("scratch", [Q, 2, TL])
    tails = sb("tails", [Q, 2, H1])
    tails_t = sb("tails_t", [H1, 2, Q])
    carry_t = sb("carry_t", [H1, 2, Q + 1])
    carry = sb("carry", [Q, 2, H1])
    turned, chain, tails_turned, back = sem("turned"), sem("chain"), sem("tails_turned"), sem("back")
    exp_done, back_copied, carry_ready = sem("exp_done"), sem("back_copied"), sem("carry_ready")
    tails_ready, diff_ready, max_ready, copied = sem("tails_ready"), sem("diff_ready"), sem("max_ready"), sem("copied")
    n_turn = 2 * heads

    with nc.Block() as block:
        @block.vector
        def _(dve):
            done = Mark(chain)

            def link(ins):
                dve.wait_ge(chain, done(ins))

            link(dve.memset(tails[:], 0.0))
            for c in range(2):
                link(dve.memset(carry_t[:, c, :], -BIG))
            for n in range(n_turn):
                h, half = n // 2, n % 2
                dve.wait_ge(turned, n + 1)
                lanes = slice(half * 4 * P, (half + 1) * 4 * P)
                dve.tensor_tensor(lg[:, h, lanes], psum[0:Q, n, :], T["invalid"][:, lanes], ALU.add
                                  ).then_inc(copied, 1)
            dve.wait_ge(copied, n_turn)
            for c in range(2):
                order = slice(None, None, -1 if c else None)
                cut = T["turn_cut"][:, c:TL + c][:, order]
                tail = 0 if c else TL - 1
                for final in range(2):
                    for h in range(heads):
                        frm = (fwd if c else lg)[:, h, order]
                        to = (fwd[:, h] if final else scratch[:, h % 2])[:, order]
                        init = carry[:, c, h:h + 1] if final else -BIG
                        done(dve.tensor_tensor_scan(to, cut, frm, init, ALU.add, ALU.max))
                        if not final:
                            dve.wait_ge(chain, done.n)
                            ins = dve.tensor_copy(tails[:, c, h:h + 1], to[:, TL - 1:TL])
                            ins.then_inc(tails_ready, 1)
                    dve.wait_ge(chain, done.n)
                    if final:
                        continue
                    dve.wait_ge(tails_turned, c + 1)
                    link(dve.tensor_copy(tails_t[:, c, :], psum[0:H1, c, 0:Q]))
                    rev = slice(None, None, -1 if c else None)
                    to = carry_t[:, c, 0:Q] if c else carry_t[:, c, 1:]
                    link(dve.tensor_tensor_scan(to[:, rev], T["cut_any"][:, c, :][:, rev], tails_t[:, c, :][:, rev],
                                                -BIG, ALU.add, ALU.max))
                    dve.tensor_copy(tails_t[:, c, :], carry_t[:, c, 1:] if c else carry_t[:, c, 0:Q]
                                    ).then_inc(carry_ready, 1)
                    dve.wait_ge(back, c + 1)
                    link(dve.tensor_copy(carry[:, c, :], psum[0:Q, 2 + c, 0:H1]))
            for h in range(heads):
                dve.tensor_tensor(lg[:, h, :], lg[:, h, :], fwd[:, h, :], ALU.subtract).then_inc(diff_ready, 1)
            for h in range(heads):
                dve.tensor_tensor(fwd[:, h, :], fwd[:, h, :], T["is_last"][:], ALU.mult).then_inc(max_ready, 1)

            def back_to(n, what):
                h, half = n // 2, n % 2
                to = T["aux"][:, :, what * H1 + h].rearrange("p (q j) -> p j q", j=J)[:, 4 * half:4 * half + 4, :]
                return to, psum[:, n, :].rearrange("p (j l) -> p j l", j=4)[:, :, 0:Q]

            for n in range(n_turn):
                dve.wait_ge(back, 2 + n_turn + n + 1)
                to, frm = back_to(n, 1)
                dve.tensor_copy(to, frm).then_inc(copied, 1)

        @block.scalar
        def _(act):
            for h in range(heads):
                act.wait_ge(diff_ready, h + 1)
                act.activation(lg[:, h, :], lg[:, h, :], ACT.Exp).then_inc(exp_done, 1)
            for n in range(n_turn):
                h, half = n // 2, n % 2
                act.wait_ge(back, 2 + n + 1)
                to = T["aux"][:, :, h].rearrange("p (q j) -> p j q", j=J)[:, 4 * half:4 * half + 4, :]
                act.copy(to, psum[:, n, :].rearrange("p (j l) -> p j l", j=4)[:, :, 0:Q]).then_inc(back_copied, 1)

        @block.tensor
        def _(pe):
            for n in range(n_turn):
                h, half = n // 2, n % 2
                for j in range(4):
                    steps = T["logits"][:, :, h].rearrange("p (q j) -> p j q", j=J)[:, 4 * half + j, :]
                    ins = pe.transpose(psum[0:Q, n, j * P:(j + 1) * P], steps, T["ident"][:])
                ins.then_inc(turned, 1)
            pe.wait_ge(copied, n_turn)
            for c in range(2):
                pe.wait_ge(tails_ready, heads * (c + 1))
                pe.transpose(psum[0:H1, c, 0:Q], tails[:, c, :], T["ident"][0:Q, 0:Q]).then_inc(tails_turned, 1)
                pe.wait_ge(carry_ready, c + 1)
                pe.transpose(psum[0:Q, 2 + c, 0:H1], tails_t[:, c, :], T["ident"][0:H1, 0:H1]).then_inc(back, 1)
            for what in range(2):
                for n in range(n_turn):
                    h, half = n // 2, n % 2
                    if what == 0:
                        pe.wait_ge(exp_done, h + 1)
                    else:
                        pe.wait_ge(max_ready, h + 1)
                        pe.wait_ge(back_copied, n + 1)
                    frm = (lg, fwd)[what]
                    for j in range(4):
                        jj = 4 * half + j
                        ins = pe.transpose(psum[:, n, j * P:j * P + Q], frm[:, h, jj * P:(jj + 1) * P],
                                           T["ident"][0:Q, 0:Q])
                    ins.then_inc(back, 1)


def combine(nc, ph, T, layer):
    sb, sem = ph.sb, ph.sem
    psum = T["psum"]
    heads = H1 if layer == 0 else 1
    G = 4
    ITER = NG // G
    rows = sb("rows", [P, G, 2 * W])
    scaled = sb("scaled", [P, G, 2, D])
    put = sb("put", [P, G, 2, P])
    total = sb("total", [P, G, AW])
    rows_in = [sem(f"rows_in{k}") for k in range(G)]
    stored = [sem(f"stored{k}") for k in range(G)]
    put_done, scaled_done, summed, total_done, zeroed = (
        sem("put_done"), sem("scaled_done"), sem("summed"), sem("total_done"), sem("zeroed"))

    with nc.Block() as block:
        @block.sync
        def _(sp):
            with sp.Fori(0, ITER) as i:
                for g in range(G):
                    sp.wait_ge(scaled_done, G * i + g + 1)
                    sp.dma_start(rows[:, g, :], T["edges_xl"][bass.ds(G * i + g, 1)].rearrange("o p f -> p (o f)")
                                 ).then_inc(rows_in[g], 16)

        @block.vector
        def _(dve):
            for g in range(G):
                dve.memset(total[:, g, :], 0.0).then_inc(zeroed, 1)
            dve.wait_ge(zeroed, G)
            dve.sem_inc(total_done, 2 * G)
            dve.sem_inc(scaled_done, G)

            def scale(i, g):
                group = G * i + g
                dve.wait_ge(summed, group + 1)
                for t in range(2):
                    dve.tensor_scalar(put[:, g, t, :], T["lane"][:, 0, :], T["rel_lane"][:, bass.ds(2 * group + t, 1)],
                                      None, ALU.is_equal).then_inc(put_done, 1)
                dve.wait_ge(rows_in[g], 16 * (i + 1))
                dve.tensor_tensor(
                    scaled[:, g].rearrange("p t (h c) -> p t h c", h=heads),
                    rows[:, g, :].rearrange("p (t w) -> p t w", t=2)[:, :, 0:D].rearrange(
                        "p t (h c) -> p t h c", h=heads),
                    bcast_last(T["aux"][:, bass.ds(2 * group, 2), 0:heads], D // heads), ALU.mult
                ).then_inc(scaled_done, 1)

            def add(i, g):
                group = G * i + g
                keep = T["keep_s"][:, bass.ds(group, 1)]
                dve.wait_ge(summed, group + G + 1)
                dve.wait_ge(stored[g], 16 * i)
                dve.wait_ge(total_done, 2 * group + 2 * G)
                old = total[:, (g - 1) % G]
                dve.scalar_tensor_tensor(total[:, g, 0:D], old[:, 0:D], keep, psum[:, g, 0:D], ALU.mult, ALU.add
                                         ).then_inc(total_done, 1)
                dve.scalar_tensor_tensor(total[:, g, D:], old[:, D:], keep, psum[:, G + g, 0:AUXW], ALU.mult, ALU.add
                                         ).then_inc(total_done, 1)

            with dve.Fori(0, ITER) as i:
                scale(i, 0)
                for g in range(1, G):
                    scale(i, g)
                    add(i, g - 1)
                add(i, G - 1)

        @block.tensor
        def _(pe):
            pe.sem_inc(summed, G)
            with pe.Fori(0, ITER) as i:
                for g in range(G):
                    group = G * i + g
                    pe.wait_ge(put_done, 2 * group + 2)
                    pe.wait_ge(scaled_done, group + G + 1)
                    pe.wait_ge(total_done, 2 * group + 2)
                    for t in range(2):
                        pe.matmul(psum[:, g, 0:D], put[:, g, t, :], scaled[:, g, t, :], start=t == 0, stop=t == 1)
                    for t in range(2):
                        ins = pe.matmul(psum[:, G + g, 0:AUXW], put[:, g, t, :],
                                        T["aux"][:, bass.ds(2 * group + t, 1), :].rearrange("p o a -> p (o a)"),
                                        start=t == 0, stop=t == 1)
                    ins.then_inc(summed, 1)

        @block.scalar
        def _(act):
            with act.Fori(0, ITER) as i:
                for g in range(G):
                    row = act.value_load(T["sum_row_s"][0:1, bass.ds(G * i + g, 1)], min_val=0,
                                         max_val=NPAD + (DUMP - 1) * P)
                    act.wait_ge(total_done, 2 * (G * i + g) + 2 + 2 * G)
                    act.dma_start(T["sums"][bass.ds(row, P), :], total[:, g, :]).then_inc(stored[g], 16)
            for g in range(G):
                act.wait_ge(stored[g], 16 * ITER)


def experts(nc, T, ffn, out):
    with ExitStack() as stack:
        T["give"] = stack.enter_context(nc.sbuf_tensor("give", [P, NB], I32))
        T["take"] = stack.enter_context(nc.sbuf_tensor("take", [P, NB], I32))
        with Phase(nc, "route") as ph:
            route(nc, ph, T, ffn)
        with Phase(nc, "ffn") as ph:
            feed_forward(nc, ph, T, ffn)
        with Phase(nc, "gather") as ph:
            gather(nc, ph, T, out)


def route(nc, ph, T, ffn):
    sb, sem = ph.sb, ph.sem
    psum = T["psum"]
    gate_w, gate_b = ffn[0:2]
    stats = sb("stats", [P, NB, 6])
    mean_var = sb("mean_var", [P, NB, 2])
    rstd = sb("rstd", [P, 2, NB])
    token = sb("token", [P, NB, W])
    h = sb("h", [P, 2, D])
    hT = sb("hT", [P, 2, 2, P])
    gw = sb("gw", [P, 2, NX])
    gb = sb("gb", [P, NX])
    lo = sb("lo", [P, NB, NX])
    pr = sb("pr", [P, NB, NX])
    one_hot = sb("one_hot", [P, NB, NX])
    cand = sb("cand", [P, NB, NX])
    incl = sb("incl", [P, NB, NX])
    tri = sb("tri", [P, P])
    back8 = sb("back8", [P, NX])
    col = sb("col", [P, 6, NB])
    zeros = sb("zeros", [P, 4 * W])
    chain, stats_done, root_done = sem("chain"), sem("stats_done"), sem("root_done")
    h_ready, h_turned, turned_sb, kept_copy = sem("h_ready"), sem("h_turned"), sem("turned_sb"), sem("kept_copy")
    gated, logit_done, diff_done, exp_done = sem("gated"), sem("logit_done"), sem("diff_done"), sem("exp_done")
    tri_done, hot_done, counted, slots_done = sem("tri_done"), sem("hot_done"), sem("counted"), sem("slots_done")
    gate_in, zeroed, given, made = sem("gate_in"), sem("zeroed"), sem("given"), sem("made")

    with nc.Block() as block:
        @block.vector
        def _(dve):
            done = Mark(chain)

            def link(ins):
                dve.wait_ge(chain, done(ins))

            done(dve.memset(token[:, :, D:], 0.0))
            for i in range(NB):
                done(dve.bn_stats(stats[:, i, :], T["x"][:, i, :]))
            dve.wait_ge(chain, done.n)
            for i in range(NB):
                dve.bn_aggr(mean_var[:, i, :], stats[:, i, :]).then_inc(stats_done, 1)
            for e in range(NX):
                done(dve.memset(back8[:, e:e + 1], float(NX - e)))
            dve.wait_ge(root_done, 1)
            link(dve.reciprocal(rstd[:, 1, :], rstd[:, 0, :]))
            dve.wait_ge(gate_in, 48)

            def body(i, k, n):
                dve.wait_ge(h_turned, i + 1)
                dve.wait_ge(kept_copy, i + 1)
                dve.tensor_scalar(h[:, k, :], at_block(T["x"], i), mean_var[:, bass.ds(i, 1), 0],
                                  rstd[:, 1, bass.ds(i, 1)], ALU.subtract, ALU.mult).then_inc(h_ready, 1)
                dve.wait_ge(gated, i + 1)
                dve.tensor_tensor(at_block(lo, i), psum[:, 2 + k, 0:NX], gb[:], ALU.add).then_inc(logit_done, 1)

            blocks(dve, body)
            dve.wait_ge(logit_done, NB)
            top, total, prob, best, pos, ok = (col[:, n] for n in range(6))
            link(dve.tensor_reduce(top, lo[:], AX.X, ALU.max))
            dve.tensor_tensor(pr[:], lo[:], bcast_last(top, NX), ALU.subtract).then_inc(diff_done, 1)
            link(dve.tensor_tensor(one_hot[:], lo[:], bcast_last(top, NX), ALU.is_equal))
            link(dve.tensor_tensor(cand[:], one_hot[:], bcast_mid(back8[:], NB), ALU.mult))
            link(dve.tensor_reduce(best, cand[:], AX.X, ALU.max))
            dve.tensor_tensor(one_hot[:], bcast_mid(back8[:], NB), bcast_last(best, NX), ALU.is_equal
                              ).then_inc(hot_done, 1)
            dve.wait_ge(exp_done, 1)
            link(dve.tensor_reduce(total, pr[:], AX.X, ALU.add))
            link(dve.reciprocal(prob, total))
            done(dve.tensor_copy(token[:, :, D], prob))
            dve.wait_ge(counted, 2)
            f2 = lambda t: t[:].rearrange("p b e -> p (b e)")
            n = NB * NX
            link(dve.tensor_copy(f2(cand), psum[:, 5, 0:n]))
            for e in range(NX):
                done(dve.tensor_tensor_scan(incl[:, :, e], T["ones"][:, 0:NB], cand[:, :, e], 0.0, ALU.mult, ALU.add))
            dve.wait_ge(chain, done.n)
            link(dve.tensor_tensor(incl[:], incl[:], cand[:], ALU.subtract))
            link(dve.tensor_tensor(f2(incl), f2(incl), psum[:, 4, 0:n], ALU.add))
            link(dve.tensor_tensor(incl[:], incl[:], one_hot[:], ALU.mult))
            link(dve.tensor_reduce(pos, incl[:], AX.X, ALU.add))
            done(dve.tensor_scalar(ok, pos, CAP + 0.5, None, ALU.is_lt))
            link(dve.tensor_scalar(best, best, -float(SLOTS), float(NX * SLOTS - 1), ALU.mult, ALU.add))
            link(dve.tensor_tensor(pos, pos, best, ALU.add))
            link(dve.tensor_scalar(top, ok, -65536.0, 65536.0, ALU.mult, ALU.add))
            dve.tensor_tensor(T["give"][:], pos, top, ALU.add).then_inc(slots_done, 1)
            link(dve.scalar_tensor_tensor(total, pos, -float(ZROW), ok, ALU.add, ALU.mult))
            dve.tensor_scalar(T["take"][:], total, float(ZROW), None, ALU.add).then_inc(slots_done, 1)
            dve.wait_ge(chain, done.n)

        @block.scalar
        def _(act):
            act.wait_ge(stats_done, NB)
            act.sem_inc(kept_copy, 2)
            act.activation(rstd[:, 0, :], mean_var[:, :, 1], ACT.Sqrt, bias=T["eps"][:]).then_inc(root_done, 1)

            def body(i, k, n):
                act.wait_ge(h_turned, i + 3)
                act.wait_ge(gated, i)
                act.copy(hT[:, k].rearrange("p a f -> p (a f)"), psum[:, k, 0:D]).then_inc(turned_sb, 1)
                act.copy(at_block(token, i)[:, 0:D], h[:, k, :]).then_inc(kept_copy, 1)

            blocks(act, body)
            act.wait_ge(diff_done, 1)
            act.activation(pr[:], pr[:], ACT.Exp).then_inc(exp_done, 1)

        @block.tensor
        def _(pe):
            pe.sem_inc(h_turned, 2)
            pe.wait_ge(gate_in, 48)

            def body(i, k, n):
                pe.wait_ge(h_ready, i + 1)
                pe.wait_ge(turned_sb, i)
                for a in range(2):
                    ins = pe.transpose(psum[:, k, a * P:(a + 1) * P], h[:, k, a * P:(a + 1) * P], T["ident"][:])
                ins.then_inc(h_turned, 1)
                pe.wait_ge(turned_sb, i + 1)
                pe.wait_ge(logit_done, i)
                for a in range(2):
                    ins = pe.matmul(psum[:, 2 + k, 0:NX], hT[:, k, a, :], gw[:, a, :], start=a == 0, stop=a == 1)
                ins.then_inc(gated, 1)

            blocks(pe, body)
            pe.wait_ge(hot_done, 1)
            pe.wait_ge(tri_done, 1)
            hot = one_hot[:].rearrange("p b e -> p (b e)")
            pe.matmul(psum[:, 4, 0:NB * NX], tri[:], hot, start=True, stop=True).then_inc(counted, 1)
            pe.matmul(psum[:, 5, 0:NB * NX], T["ones"][:], hot, start=True, stop=True).then_inc(counted, 1)

        @block.gpsimd
        def _(pool):
            pool.memset(zeros[:], 0.0).then_inc(made, 1)
            pool.affine_select(out=tri[:], in_=T["ones"][:], compare_op=ALU.is_ge, fill=0.0, base=0,
                               pattern=[[1, P]], channel_multiplier=-1).then_inc(tri_done, 1)
            pool.wait_ge(slots_done, 2)
            pool.wait_ge(kept_copy, NB + 2)
            pool.wait_ge(zeroed, 16 * (16 + NX))
            for i in range(NB):
                pool.indirect_dma_start(
                    out=T["tokens"], out_offset=bass.IndirectOffsetOnAxis(ap=T["give"][:, i:i + 1], axis=0),
                    in_=token[:, i, :], in_offset=None, bounds_check=NX * SLOTS - 1, oob_is_err=False
                ).then_inc(given, 16)
            pool.wait_ge(given, 16 * NB)

        @block.sync
        def _(sp):
            for a in range(2):
                sp.dma_start(gw[:, a, :], gate_w[a * P:(a + 1) * P, :]).then_inc(gate_in, 16)
            sp.dma_start(gb[:], gate_b.partition_broadcast(P)).then_inc(gate_in, 16)
            sp.wait_ge(made, 1)
            for n in range(16):
                rows = NX * SLOTS // 16
                sp.dma_start(T["tokens"][n * rows:(n + 1) * rows, :].rearrange("(p r) w -> p (r w)", p=P), zeros[:]
                             ).then_inc(zeroed, 16)
            for e in range(NX):
                sp.dma_start(T["answers"][e * SLOTS + CAP:(e + 1) * SLOTS, :], zeros[0:SLOTS - CAP, 0:D]
                             ).then_inc(zeroed, 16)


def feed_forward(nc, ph, T, ffn):
    sb, sem = ph.sb, ph.sem
    psum = T["psum"]
    _, _, w1, b1, w2, b2 = ffn
    KF = F // P
    TT = -(-CAP // P)
    REST = CAP - P * (TT - 1)
    HALVES = ((0, 512), (512, CAP - 512))
    tok = sb("tok", [P, 2, TT, W])
    tT = sb("tT", [P, 2, 2, TT * P])
    w1_s = sb("w1", [P, 2, 2, F])
    w2_s = sb("w2", [P, 2, KF, D])
    b1_rows = sb("b1_rows", [NX * KF, P])
    b1_s = sb("b1", [P, NX, KF])
    b2_s = sb("b2", [P, NX, D])
    mid = sb("mid", [P, KF, TT * P])
    y = sb("y", [P, 2, D])
    mask = sb("mask", [P, 2, D], I32)
    raw = sb("raw", [P, 2, 2, D])
    fix = sb("fix", [P, 2, D])
    b1_now = sb("b1_now", [P, 2, KF])
    tok_in = [sem(f"tok_in{k}") for k in range(2)]
    w1_in = [sem(f"w1_in{k}") for k in range(2)]
    w2_in = [sem(f"w2_in{k}") for k in range(2)]
    bias_in, b1_turned, b1_ready, b1_picked = sem("bias_in"), sem("b1_turned"), sem("b1_ready"), sem("b1_picked")
    turned, turned_sb, first, mid_done, second = (
        sem("turned"), sem("turned_sb"), sem("first"), sem("mid_done"), sem("second"))
    y_steps, y_done = sem("y_steps"), sem("y_done")
    y_out = [sem(f"y_out{k}") for k in range(2)]
    BIGGEST = 3.4028234663852886e38
    PIECES = 4 * 1

    def per_expert(eng, body):
        with eng.Fori(0, NX // 2) as n:
            for k in range(2):
                body(2 * n + k, k, n)

    def tile_rows(t):
        return P if t < TT - 1 else REST

    with nc.Block() as block:
        @block.sync
        def _(sp):
            sp.dma_start(b1_rows[:], b1.rearrange("e (c p) -> (e c) p", p=P)).then_inc(bias_in, 16)
            sp.dma_start(b2_s[:].rearrange("p e d -> p (e d)"), b2.rearrange("e d -> (e d)").partition_broadcast(P)
                         ).then_inc(bias_in, 16)

            def body(e, k, n):
                sp.wait_ge(second, TT * e + TT)
                sp.wait_ge(y_done, TT * e + TT)
                sp.dma_start(tok[:, k], T["tokens"][bass.ds(e * SLOTS, SLOTS), :].rearrange("(t p) w -> p t w", p=P)
                             ).then_inc(tok_in[k], 16)
                sp.dma_start(w1_s[:, k], w1[bass.ds(e, 1)].rearrange("o (a p) f -> p (o a) f", p=P)
                             ).then_inc(w1_in[k], 16)
                sp.dma_start(w2_s[:, k], w2[bass.ds(e, 1)].rearrange("o (c p) d -> p (o c) d", p=P)
                             ).then_inc(w2_in[k], 16)

            per_expert(sp, body)

        @block.tensor
        def _(pe):
            pe.sem_inc(second, 2 * TT)
            pe.wait_ge(bias_in, 32)
            pe.transpose(psum[:, 0, 0:NX * KF], b1_rows[:], T["ident"][0:NX * KF, 0:NX * KF]).then_inc(b1_turned, 1)
            pe.wait_ge(b1_ready, 1)

            def body(e, k, n):
                pe.wait_ge(tok_in[k], 16 * (n + 1))
                for piece in range(4):
                    a, t0 = piece // 2, piece % 2 * 4
                    pe.wait_ge(turned_sb, 4 * e + piece)
                    for t in range(4):
                        ins = pe.transpose(psum[:, piece % 2, t * P:(t + 1) * P], tok[:, k, t0 + t, a * P:(a + 1) * P],
                                           T["ident"][:])
                    ins.then_inc(turned, 1)
                pe.wait_ge(turned_sb, 4 * e + 4)
                pe.wait_ge(w1_in[k], 16 * (n + 1))
                for c in range(KF):
                    for half, (t0, size) in enumerate(HALVES):
                        m = 2 * c + half
                        pe.wait_ge(mid_done, 2 * KF * e + m + 1)
                        for a in range(2):
                            ins = pe.matmul(psum[:, 2 + half, 0:size], w1_s[:, k, a, c * P:(c + 1) * P],
                                            tT[:, k, a, t0:t0 + size], start=a == 0, stop=a == 1)
                        ins.then_inc(first, 1)
                pe.wait_ge(mid_done, 2 * KF * e + 2 * KF + 2)
                pe.wait_ge(w2_in[k], 16 * (n + 1))
                for t in range(TT):
                    r = tile_rows(t)
                    pe.wait_ge(y_done, TT * e + t + 2 * TT - 1)
                    for c in range(KF):
                        ins = pe.matmul(psum[0:r, 4 + t % 2, 0:D], mid[:, c, t * P:t * P + r], w2_s[:, k, c, :],
                                        start=c == 0, stop=c == KF - 1)
                    ins.then_inc(second, 1)

            per_expert(pe, body)

        @block.scalar
        def _(act):
            act.sem_inc(mid_done, 2)

            def body(e, k, n):
                for piece in range(4):
                    a, t0 = piece // 2, piece % 2 * 4
                    act.wait_ge(turned, 4 * e + piece + 1)
                    act.copy(tT[:, k, a, t0 * P:(t0 + 4) * P], psum[:, piece % 2, :]).then_inc(turned_sb, 1)
                act.copy(b1_now[:, k, :], at_block(b1_s, e)).then_inc(b1_picked, 1)
                act.wait_ge(b1_picked, e + 1)
                act.wait_ge(second, TT * e + 2 * TT)
                for c in range(KF):
                    for half, (t0, size) in enumerate(HALVES):
                        act.wait_ge(first, 2 * KF * e + 2 * c + half + 1)
                        act.activation(mid[:, c, t0:t0 + size], psum[:, 2 + half, 0:size], ACT.Relu,
                                       bias=b1_now[:, k, c:c + 1]).then_inc(mid_done, 1)
                for t in range(TT):
                    act.wait_ge(y_done, TT * e + t + 2 * TT + 1)
                    act.dma_start(T["answers"][bass.ds(e * SLOTS + t * P, tile_rows(t)), :],
                                  y[0:tile_rows(t), t % 2, :]).then_inc(y_out[t % 2], 16)

            act.wait_ge(b1_turned, 1)
            act.copy(b1_s[:].rearrange("p e c -> p (e c)"), psum[:, 0, 0:NX * KF]).then_inc(b1_ready, 1)
            act.wait_ge(b1_ready, 1)
            per_expert(act, body)
            for s in range(2):
                act.wait_ge(y_out[s], 16 * NX * TT // 2)

        @block.vector
        def _(dve):
            dve.sem_inc(y_done, 2 * TT)
            dve.wait_ge(bias_in, 32)

            def body(e, k, n):
                for t in range(TT):
                    r, s, tile = tile_rows(t), t % 2, TT * e + t
                    yt, r0, r1 = y[0:r, s, :], raw[0:r, s, 0, :], raw[0:r, s, 1, :]
                    fin, fx = mask[0:r, s, :], fix[0:r, s, :]
                    dve.wait_ge(tok_in[k], 16 * (n + 1))
                    dve.wait_ge(second, tile + 2 * TT + 1)
                    dve.tensor_tensor(r0, psum[0:r, 4 + s, 0:D], at_block(b2_s, e)[0:r], ALU.add
                                      ).then_inc(y_steps, 1)
                    dve.wait_ge(y_steps, 7 * tile + 1)
                    dve.tensor_scalar(r1, r0, tok[0:r, k, t, D:D + 1], None, ALU.mult).then_inc(y_steps, 1)
                    dve.wait_ge(y_steps, 7 * tile + 2)
                    dve.tensor_scalar(fin, r1, 0.0, 0.0, ALU.mult, ALU.is_equal).then_inc(y_steps, 1)
                    dve.tensor_scalar(fx, r1, -BIGGEST, -1.0e4, ALU.is_lt, ALU.mult).then_inc(y_steps, 1)
                    dve.tensor_scalar(r0, r1, BIGGEST, 1.0e4, ALU.is_gt, ALU.mult).then_inc(y_steps, 1)
                    dve.wait_ge(y_out[s], 16 * (TT // 2 * e + t // 2))
                    dve.wait_ge(y_steps, 7 * tile + 5)
                    dve.tensor_tensor(yt, fx, r0, ALU.add).then_inc(y_steps, 1)
                    dve.wait_ge(y_steps, 7 * tile + 6)
                    dve.sem_inc(y_steps, 1)
                    dve.copy_predicated(yt, fin, r1).then_inc(y_done, 1)

            per_expert(dve, body)


def gather(nc, ph, T, out):
    sb, sem = ph.sb, ph.sem
    SL = 7
    assert NB % SL == 0
    got = sb("got", [P, SL, D])
    got_in = [sem(f"got_in{k}") for k in range(SL)]
    added, stored = sem("added"), sem("stored")

    with nc.Block() as block:
        @block.gpsimd
        def _(pool):
            for i in range(NB):
                if i >= SL:
                    pool.wait_ge(added, i - SL + 1)
                pool.indirect_dma_start(
                    out=got[:, i % SL, :], out_offset=None, in_=T["answers"],
                    in_offset=bass.IndirectOffsetOnAxis(ap=T["take"][:, i:i + 1], axis=0),
                    bounds_check=NX * SLOTS - 1, oob_is_err=False).then_inc(got_in[i % SL], 16)

        @block.vector
        def _(dve):
            with dve.Fori(0, NB // SL) as n:
                for k in range(SL):
                    dve.wait_ge(got_in[k], 16 * (n + 1))
                    xi = at_block(T["x"], SL * n + k)
                    dve.tensor_tensor(xi, xi, got[:, k, :], ALU.add).then_inc(added, 1)

        @block.sync
        def _(sp):
            for n in range(NB // SL):
                last = n == NB // SL - 1
                full = SL - last
                sp.wait_ge(added, SL * n + SL)
                sp.dma_start(out[P * SL * n:P * (SL * n + full)].rearrange("(b p) d -> p b d", p=P),
                             T["x"][:, SL * n:SL * n + full, :]).then_inc(stored, 16)
            sp.dma_start(out[P * (NB - 1):N], T["x"][0:LAST, NB - 1, :]).then_inc(stored, 16)
            sp.wait_ge(stored, 16 * (NB // SL + 1))


def kernel(x, src, dst, L0_gnn_Wl1, L0_gnn_Wr1, L0_gnn_att1, L0_gnn_b1, L0_gnn_Wl2, L0_gnn_Wr2, L0_gnn_att2,
           L0_gnn_b2, L0_ffn_gate_w, L0_ffn_gate_b, L0_ffn_w1, L0_ffn_b1, L0_ffn_w2, L0_ffn_b2):
    import numpy as np
    import concourse.bacc as bacc
    from concourse.bass_utils import run_bass_kernel_spmd

    nc = bacc.Bacc("TRN2", target_bir_lowering=False, num_devices=1)
    inputs = dict(x=x, src=src, dst=dst, wl1=L0_gnn_Wl1, wr1=L0_gnn_Wr1, att1=L0_gnn_att1, b1=L0_gnn_b1,
                  wl2=L0_gnn_Wl2, wr2=L0_gnn_Wr2, att2=L0_gnn_att2, b2=L0_gnn_b2, gate_w=L0_ffn_gate_w,
                  gate_b=L0_ffn_gate_b, ffn_w1=L0_ffn_w1, ffn_b1=L0_ffn_b1, ffn_w2=L0_ffn_w2, ffn_b2=L0_ffn_b2)
    arrays = {f"in_{name}": np.ascontiguousarray(a) for name, a in inputs.items()}
    ap = {name: nc.dram_tensor(f"in_{name}", arrays[f"in_{name}"].shape,
                               mybir.dt.from_np(arrays[f"in_{name}"].dtype), kind="ExternalInput").ap()
          for name in inputs}
    out = nc.dram_tensor("out", (N, D), F32, kind="ExternalOutput").ap()
    gnn = [tuple(ap[f"{n}{i}"] for n in ("wl", "wr", "att", "b")) for i in (1, 2)]
    ffn = tuple(ap[n] for n in ("gate_w", "gate_b", "ffn_w1", "ffn_b1", "ffn_w2", "ffn_b2"))
    build(nc, ap["x"], ap["src"], ap["dst"], gnn, ffn, out)
    return run_bass_kernel_spmd(nc, [arrays], core_ids=[0]).results[0]["out"]
```

```python
from contextlib import ExitStack

import concourse.bass as bass
from concourse import mybir

ALU = mybir.AluOpType
ACT = mybir.ActivationFunctionType
F32 = mybir.dt.float32
I32 = mybir.dt.int32
U32 = mybir.dt.uint32
BF16 = mybir.dt.bfloat16
AX = mybir.AxisListType

P = 128
N, D, E = 6250, 256, 100000
H1 = 4
NB = -(-N // P)
LAST = N - P * (NB - 1)
NPAD = NB * P
W = D + H1
EROWS = -(-E // P) + 2
ROWS = -(-E // P)
NG = 440
assert (ROWS + NB - 1 + NB) // 2 <= NG
NS = 2 * NG
Q = 110
J = NS // Q
TL = J * P
GQ = J // 2
assert Q * J == NS
BIG = 1.0e30
EPS = 1e-5
NX, F = 8, 1024
CAP = -(-5 * N // (4 * NX))
SLOTS = 1024
ZROW = NX * SLOTS - 1
ECH = 125
assert E % ECH == 0
AUXW = 9
AW = D + AUXW
RING = 16
NOWHERE = 1 << 20


class Mark:

    def __init__(self, sem):
        self.sem, self.n = sem, 0

    def __call__(self, ins):
        ins.then_inc(self.sem, 1)
        self.n += 1
        return self.n


def bcast_mid(ap, n):
    return ap.unsqueeze(1).broadcast_to([ap.shape[0], n, ap.shape[1]])


def bcast_last(ap, n):
    return ap.unsqueeze(len(ap.shape)).broadcast_to([*ap.shape, n])


class Phase:

    def __init__(self, nc, name):
        self.nc, self.name, self.sems, self.stack = nc, name, [], ExitStack()

    def __enter__(self):
        return self

    def __exit__(self, *_):
        self.stack.close()
        self.nc.clear_and_free_semaphores(self.sems)
        self.nc.all_engine_barrier()

    def sem(self, name):
        self.sems.append(self.nc.alloc_semaphore(f"{self.name}_{name}"))
        return self.sems[-1]

    def sb(self, name, shape, dt=F32):
        return self.stack.enter_context(self.nc.sbuf_tensor(f"{self.name}_{name}", shape, dt))


def build(nc, x, src, dst, gnn, ffn, out):
    with ExitStack() as ctx:
        def sb(name, shape, dt=F32, stack=ctx):
            return stack.enter_context(nc.sbuf_tensor(name, shape, dt))

        def dram(name, shape, dt=F32):
            return nc.dram_tensor(name, shape, dt, kind="Internal").ap()

        T = {}
        T["src_rows"] = dram("src_rows", (EROWS, P), I32)
        T["dst_rows"] = dram("dst_rows", (EROWS, P), I32)
        T["keys"] = dram("keys", (Q * TL + 2,), F32)
        T["rel"] = dram("rel", ((NS + J) * P,), BF16)
        T["block_row"] = dram("block_row", (NG,), I32)
        T["sum_row"] = dram("sum_row", (NG,), F32)
        T["keep"] = dram("keep", (NG,), F32)
        T["xl"] = dram("xl", (NPAD, W))
        T["xr"] = dram("xr", (NPAD, W))
        T["edges_xl"] = dram("edges_xl", (NG, P, 2 * W))
        T["sums"] = dram("sums", (NPAD, AW))
        T["tokens"] = dram("tokens", (NX * SLOTS, W))
        T["answers"] = dram("answers", (NX * SLOTS, D))
        T["psum"] = ctx.enter_context(nc.psum_tensor("psum", [P, 8, 512], F32))
        T["x"] = sb("x_res", [P, NB, D])
        T["ident"] = sb("ident", [P, P])
        T["ones"] = sb("ones", [P, P])
        T["lane"] = sb("lane", [P, 2, P])
        T["eps"] = sb("eps", [P, 1])
        with ExitStack() as g:
            T["block_row_s"] = sb("block_row_s", [1, NG], I32, g)
            T["sum_index"] = sb("sum_index", [P, NG], I32, g)
            T["keep_s"] = sb("keep_s", [P, NG], F32, g)
            T["turn_cut"] = sb("turn_cut", [Q, TL + 1], F32, g)
            T["invalid"] = sb("invalid", [Q, TL], F32, g)
            T["is_last"] = sb("is_last", [Q, TL], F32, g)
            T["cut_any"] = sb("cut_any", [H1, 2, Q], F32, g)
            T["src_lane"] = sb("src_lane", [P, NS + RING], I32, g)
            T["rel_lane"] = sb("rel_lane", [P, NS], F32, g)
            T["part"] = sb("part", [P, 1], F32, g)
            T["logits"] = sb("logits", [P, NS, H1], F32, g)
            T["aux"] = sb("aux", [P, NS, AUXW], F32, g)
            T["self_logits"] = sb("self_logits", [P, NB, H1], F32, g)
            with Phase(nc, "tables") as ph:
                make_tables(nc, ph, T, x, src, dst)
            for layer in range(2):
                with Phase(nc, f"nodes{layer}") as ph:
                    nodes(nc, ph, T, gnn, layer)
                with Phase(nc, f"score{layer}") as ph:
                    score(nc, ph, T, gnn[layer], layer)
                with Phase(nc, f"softmax{layer}") as ph:
                    softmax(nc, ph, T, layer)
                with Phase(nc, f"combine{layer}") as ph:
                    combine(nc, ph, T, layer)
            with Phase(nc, "nodes2") as ph:
                nodes(nc, ph, T, gnn, 2)
        experts(nc, T, ffn, out)


def staged(eng, total, slots, *stages):
    lead = max(first for first, _ in stages)

    def peeled(turns):
        for t in turns:
            for first, body in stages:
                if 0 <= t + first < total:
                    body(t + first, (t + first) % slots, (t + first) // slots)

    whole = (total - lead) // slots
    peeled(range(-lead, 0))
    with eng.Fori(0, whole) as n:
        for k in range(slots):
            for first, body in stages:
                body(slots * n + k + first, (k + first) % slots, n + (k + first) // slots)
    peeled(range(whole * slots, total))


def make_tables(nc, ph, T, x, src, dst):
    sb, sem = ph.sb, ph.sem
    src_i = sb("src_i", [ECH, E // ECH], I32)
    dst_i = sb("dst_i", [ECH, E // ECH], I32)
    dst_f = sb("dst_f", [ECH, E // ECH])
    junk = sb("junk", [ECH, 2, E // ECH])
    pad_i = sb("pad_i", [1, 2, EROWS * P - E], I32)
    iot = sb("iot", [P, P], I32)
    iot_p = sb("iot_p", [P, 1], I32)
    iot_g = sb("iot_g", [Q, GQ], I32)
    thr = sb("thr", [P, NB + 1])
    blk = sb("blk", [P, NB])
    below = sb("below", [ECH, NB + 1])
    off = sb("off", [P, NB + 1])
    off_i = sb("off_i", [P, 2, NB + 1], I32)
    row_i = sb("row_i", [P, 2, NB + 1], I32)
    row_f = sb("row_f", [P, 2, NB + 1])
    n_i = sb("n_i", [P, NB], I32)
    ngi = sb("ngi", [P, NB], I32)
    n_f = sb("n_f", [P, 2, NB])
    t_in = sb("t_in", [P, NB])
    t_ex = sb("t_ex", [P, NB])
    g_id = sb("g_id", [Q, GQ])
    big4 = sb("big4", [Q, 5, GQ, NB])
    b_g = sb("b_g", [Q, GQ])
    sel = sb("sel", [Q, 6, GQ])
    some = sb("some", [Q, 2])
    sum_row = sb("sum_row", [P, NG])
    rows_s = sb("rows_s", [Q, J], I32)
    tab_i = sb("tab_i", [Q, GQ], I32)
    srcT_i = sb("srcT_i", [Q, TL], I32)
    dstT_i = sb("dstT_i", [Q, TL], I32)
    srcT = sb("srcT", [Q, TL])
    dstT = sb("dstT", [Q, TL])
    relT = sb("relT", [Q, TL])
    valid = sb("valid", [Q, TL])
    rel16 = sb("rel16", [Q, TL], BF16)
    keyx = sb("keyx", [Q, TL + 2])
    cuts = sb("cuts", [Q, 2, H1])
    edge_pad = sb("edge_pad", [1, 2])

    in_loaded = [sem(f"in_loaded{i}") for i in range(3)]
    x_loaded = sem("x_loaded")
    rows_stored = sem("rows_stored")
    const_done = sem("const_done")
    dve_done = sem("tables_dve")
    off_counted = sem("off_counted")
    rows_gathered = sem("rows_gathered")
    keys_stored = sem("keys_stored")
    tabs_stored = sem("tabs_stored")
    keys_back = sem("keys_back")
    tabs_back = sem("tabs_back")
    turned = sem("turned")
    turned_copied = sem("turned_copied")
    psum = T["psum"]

    with nc.Block() as block:
        V_BELOW, V_ROWS, V_TABS, V_KEYS, V_TURN = [0], [0], [0], [0], [0, 0]

        @block.vector
        def _(dve):
            done = Mark(dve_done)

            def after(n):
                dve.wait_ge(dve_done, n)

            def link(ins):
                after(done(ins))

            dve.wait_ge(const_done, 11)
            for c in range(2):
                done(dve.tensor_copy(T["lane"][:, c, :], iot[:]))
            done(dve.tensor_copy(T["part"][:], iot_p[:]))
            done(dve.tensor_copy(g_id[:], iot_g[:]))
            done(dve.tensor_copy(blk[:], iot[:, 0:NB]))
            done(dve.tensor_scalar(thr[:], iot[:, 0:NB + 1], float(P), None, ALU.mult))
            done(dve.memset(below[:, 0:1], 0.0))
            done(dve.memset(below[:, NB:], float(E // ECH)))
            dve.wait_ge(in_loaded[0], 16)
            link(dve.tensor_copy(dst_f[:], dst_i[:]))
            for b in range(1, NB):
                dve.wait_ge(dve_done, done.n - 1)
                done(dve.tensor_scalar(junk[:, b % 2], dst_f[:], float(P * b), 0.0, ALU.is_lt, ALU.add,
                                       accum_out=below[:, b:b + 1]))
            V_BELOW[0] = done.n
            dve.wait_ge(off_counted, 1)
            link(dve.tensor_copy(off[:], psum[:, 0, 0:NB + 1]))
            done(dve.tensor_copy(off_i[:, 0, :], off[:]))
            link(dve.tensor_scalar(off_i[:, 1, :], off[:], float(P - 1), None, ALU.add))
            link(dve.tensor_scalar(row_i[:], off_i[:], 7, None, ALU.arith_shift_right))
            link(dve.tensor_copy(row_f[:], row_i[:]))
            link(dve.tensor_tensor(n_f[:, 0, :], row_f[:, 1, 1:], row_f[:, 0, 0:NB], ALU.subtract))
            link(dve.tensor_scalar(n_i[:], n_f[:, 0, :], 1.0, 1.0, ALU.max, ALU.add))
            link(dve.tensor_scalar(ngi[:], n_i[:], 1, None, ALU.arith_shift_right))
            link(dve.tensor_copy(n_f[:, 1, :], ngi[:]))
            link(dve.tensor_tensor_scan(t_in[:], T["ones"][:, 0:NB], n_f[:, 1, :], 0.0, ALU.mult, ALU.add))
            link(dve.tensor_tensor(t_ex[:], t_in[:], n_f[:, 1, :], ALU.subtract))
            sh = [Q, GQ, NB]
            tin_b, tex_b = bcast_mid(t_in[0:Q], GQ), bcast_mid(t_ex[0:Q], GQ)
            gid_b = bcast_last(g_id[:], NB)
            link(dve.tensor_tensor(big4[:, 0], tin_b, gid_b, ALU.is_le))
            link(dve.tensor_reduce(b_g[:], big4[:, 0], AX.X, ALU.add))
            link(dve.tensor_scalar(b_g[:], b_g[:], float(NB - 1), None, ALU.min))
            link(dve.tensor_tensor(big4[:, 1], bcast_mid(blk[0:Q], GQ), bcast_last(b_g[:], NB), ALU.is_equal))
            done(dve.tensor_tensor(big4[:, 2], big4[:, 1], tex_b, ALU.mult))
            done(dve.tensor_tensor(big4[:, 3], big4[:, 1], bcast_mid(row_f[0:Q, 0, 0:NB], GQ), ALU.mult))
            done(dve.tensor_scalar(sel[:, 4, :], g_id[:], 1.0, None, ALU.add))
            after(done.n)
            link(dve.tensor_tensor(big4[:, 4], tin_b, bcast_last(sel[:, 4, :], NB), ALU.is_equal))
            done(dve.tensor_reduce(sel[:, 0, :], big4[:, 2], AX.X, ALU.add))
            done(dve.tensor_reduce(sel[:, 1, :], big4[:, 3], AX.X, ALU.add))
            link(dve.tensor_reduce(sel[:, 2, :], big4[:, 4], AX.X, ALU.add))
            link(dve.tensor_tensor(sel[:, 5, :], g_id[:], sel[:, 0, :], ALU.subtract))
            done(dve.tensor_scalar(sel[:, 3, :], sel[:, 5, :], 0.5, None, ALU.is_gt))
            link(dve.tensor_scalar(sel[:, 5, :], sel[:, 5, :], 2.0, None, ALU.mult))
            link(dve.tensor_tensor(sel[:, 5, :], sel[:, 5, :], sel[:, 1, :], ALU.add))
            rows_v = rows_s[:].rearrange("q (g t) -> q g t", t=2)
            done(dve.tensor_scalar(rows_v[:, :, 0], sel[:, 5, :], float(ROWS), None, ALU.min))
            link(dve.tensor_scalar(rows_v[:, :, 1], sel[:, 5, :], float(ROWS), 1.0, ALU.min, ALU.add))
            V_ROWS[0] = done.n
            link(dve.tensor_scalar(sel[:, 0, :], b_g[:], float(P), None, ALU.mult))
            done(dve.tensor_copy(tab_i[:], sel[:, 0, :]))
            link(dve.tensor_scalar(sel[:, 1, :], sel[:, 0, :], -float(NOWHERE), None, ALU.add))
            link(dve.tensor_tensor(sel[:, 1, :], sel[:, 1, :], sel[:, 2, :], ALU.mult))
            link(dve.tensor_scalar(sel[:, 1, :], sel[:, 1, :], float(NOWHERE), None, ALU.add))
            V_TABS[0] = done.n
            dve.wait_ge(rows_gathered, 16 * 2 * J)
            done(dve.tensor_copy(srcT[:], srcT_i[:]))
            V_TURN[0] = done.n
            link(dve.tensor_copy(dstT[:], dstT_i[:]))
            g3 = lambda t: t[:].rearrange("q (g l) -> q g l", g=GQ)
            link(dve.tensor_tensor(g3(relT), g3(dstT), bcast_last(sel[:, 0, :], 2 * P), ALU.subtract))
            done(dve.tensor_copy(rel16[:], relT[:]))
            link(dve.tensor_scalar(valid[:], relT[:], 0.0, None, ALU.is_ge))
            link(dve.scalar_tensor_tensor(valid[:], relT[:], float(P), valid[:], ALU.is_lt, ALU.mult))
            done(dve.tensor_scalar(T["invalid"][:], valid[:], -1.0, BIG, ALU.add, ALU.mult))
            link(dve.scalar_tensor_tensor(dstT[:], dstT[:], 1.0, valid[:], ALU.add, ALU.mult))
            link(dve.tensor_scalar(keyx[:, 1:1 + TL], dstT[:], -1.0, None, ALU.add))
            V_KEYS[0] = done.n
            dve.wait_ge(tabs_back, 48)
            done(dve.tensor_scalar(T["sum_index"][:], sum_row[:], T["part"][:], None, ALU.add))
            dve.wait_ge(keys_back, 32)
            cut = T["turn_cut"]
            link(dve.tensor_tensor(cut[:], keyx[:, 0:TL + 1], keyx[:, 1:TL + 2], ALU.not_equal))
            link(dve.tensor_scalar(cut[:], cut[:], -BIG, None, ALU.mult))
            done(dve.scalar_tensor_tensor(T["is_last"][:], cut[:, 1:], -1.0, valid[:], ALU.is_lt, ALU.mult))
            done(dve.tensor_reduce(some[:, 0:1], cut[:, 0:TL], AX.X, ALU.min))
            link(dve.tensor_reduce(some[:, 1:2], cut[:, 1:], AX.X, ALU.min))
            done(dve.tensor_copy(cuts[:], bcast_last(some[:, 0:2], H1)))
            V_TURN[1] = done.n
            for n in range(6):
                dve.wait_ge(turned, n + 1)
                h = n % 2
                ps = psum[:, 1 + n, :].rearrange("p (j l) -> p j l", j=4)[:, :, 0:Q]
                if n < 2:
                    to = T["src_lane"][:, 0:NS]
                elif n < 4:
                    to = T["rel_lane"][:]
                else:
                    to = T["aux"][:, :, AUXW - 1]
                to = to.rearrange("p (q j) -> p j q", j=J)[:, 4 * h:4 * h + 4, :]
                done(dve.tensor_copy(to, ps))
            dve.wait_ge(turned, 7)
            for c in range(2):
                done(dve.tensor_copy(T["cut_any"][:, c, :], psum[0:H1, 7, c * P:c * P + Q]))

        @block.gpsimd
        def _(pool):
            pool.memset(T["ones"][:], 1.0).then_inc(const_done, 1)
            pool.wait_ge(const_done, 1)
            pool.affine_select(out=T["ident"][:], in_=T["ones"][:], compare_op=ALU.is_equal, fill=0.0, base=0,
                               pattern=[[-1, P]], channel_multiplier=1).then_inc(const_done, 1)
            pool.iota(iot[:], pattern=[[1, P]], base=0, channel_multiplier=0).then_inc(const_done, 1)
            pool.iota(iot_p[:], pattern=[[0, 1]], base=0, channel_multiplier=1).then_inc(const_done, 1)
            pool.iota(iot_g[:], pattern=[[1, GQ]], base=0, channel_multiplier=GQ).then_inc(const_done, 1)
            pool.memset(pad_i[:, 0, :], 0).then_inc(const_done, 1)
            pool.memset(pad_i[:, 1, :], 1 << 20).then_inc(const_done, 1)
            pool.memset(T["x"][:, NB - 1, :], 0.0).then_inc(const_done, 1)
            pool.memset(edge_pad[:], -2.0).then_inc(const_done, 1)
            pool.memset(T["src_lane"][:, NS:], 0).then_inc(const_done, 1)
            pool.memset(T["eps"][:], EPS).then_inc(const_done, 1)
            pool.wait_ge(dve_done, V_ROWS[0])
            pool.wait_ge(rows_stored, 64)
            for j in range(J):
                for table, to in ((T["src_rows"], srcT_i), (T["dst_rows"], dstT_i)):
                    pool.indirect_dma_start(
                        out=to[:, j * P:(j + 1) * P], out_offset=None, in_=table,
                        in_offset=bass.IndirectOffsetOnAxis(ap=rows_s[:, j:j + 1], axis=0),
                        bounds_check=EROWS - 1, oob_is_err=False).then_inc(rows_gathered, 16)

        @block.sync
        def _(sp):
            sp.dma_start(dst_i[:], dst.rearrange("(p f) -> p f", p=ECH)).then_inc(in_loaded[0], 16)
            sp.dma_start(src_i[:], src.rearrange("(p f) -> p f", p=ECH)).then_inc(in_loaded[1], 16)
            sp.wait_ge(const_done, 11)
            sp.dma_start(T["x"][:, 0:NB - 1, :], x[0:P * (NB - 1)].rearrange("(b p) d -> p b d", p=P)
                         ).then_inc(x_loaded, 16)
            sp.dma_start(T["x"][0:LAST, NB - 1, :], x[P * (NB - 1):N]).then_inc(x_loaded, 16)
            flat_s = T["src_rows"].rearrange("r l -> (r l)")
            flat_d = T["dst_rows"].rearrange("r l -> (r l)")
            sp.wait_ge(in_loaded[0], 16)
            sp.dma_start(flat_d[0:E].rearrange("(p f) -> p f", p=ECH), dst_i[:]).then_inc(rows_stored, 16)
            sp.dma_start(flat_d[E:].rearrange("(o f) -> o f", o=1), pad_i[:, 1, :]).then_inc(rows_stored, 16)
            sp.wait_ge(in_loaded[1], 16)
            sp.dma_start(flat_s[0:E].rearrange("(p f) -> p f", p=ECH), src_i[:]).then_inc(rows_stored, 16)
            sp.dma_start(flat_s[E:].rearrange("(o f) -> o f", o=1), pad_i[:, 0, :]).then_inc(rows_stored, 16)
            sp.wait_ge(dve_done, V_TABS[0])
            for name, what in (("block_row", tab_i[:]), ("sum_row", sel[:, 1, :]), ("keep", sel[:, 3, :])):
                sp.dma_start(T[name].rearrange("(q g) -> q g", q=Q), what).then_inc(tabs_stored, 16)
            sp.wait_ge(tabs_stored, 48)
            sp.dma_start(T["block_row_s"][:], T["block_row"].unsqueeze(0)).then_inc(tabs_back, 16)
            sp.dma_start(sum_row[:], T["sum_row"].partition_broadcast(P)).then_inc(tabs_back, 16)
            sp.dma_start(T["keep_s"][:], T["keep"].partition_broadcast(P)).then_inc(tabs_back, 16)
            sp.wait_ge(dve_done, V_KEYS[0])
            sp.dma_start(T["keys"][1:1 + Q * TL].rearrange("(q l) -> q l", q=Q), keyx[:, 1:1 + TL]
                         ).then_inc(keys_stored, 16)
            sp.dma_start(T["keys"][0:1].unsqueeze(0), edge_pad[:, 0:1]).then_inc(keys_stored, 16)
            sp.dma_start(T["keys"][1 + Q * TL:].unsqueeze(0), edge_pad[:, 1:2]).then_inc(keys_stored, 16)
            sp.dma_start(T["rel"][0:Q * TL].rearrange("(q l) -> q l", q=Q), rel16[:]).then_inc(keys_stored, 16)
            sp.dma_start(T["rel"][Q * TL:].unsqueeze(0), rel16[0:1, :]).then_inc(keys_stored, 16)
            sp.wait_ge(keys_stored, 80)
            sp.dma_start(keyx[:, 0:1], T["keys"][0:Q * TL].rearrange("(q l) -> q l", q=Q)[:, 0:1],
                         allow_slow_non_contiguous=True).then_inc(keys_back, 16)
            sp.dma_start(keyx[:, TL + 1:], T["keys"][2:2 + Q * TL].rearrange("(q l) -> q l", q=Q)[:, TL - 1:],
                         allow_slow_non_contiguous=True).then_inc(keys_back, 16)
            sp.wait_ge(tabs_back, 48)
            sp.wait_ge(x_loaded, 32)

        @block.tensor
        def _(pe):
            pe.wait_ge(dve_done, V_BELOW[0])
            pe.matmul(psum[:, 0, 0:NB + 1], T["ones"][0:ECH, :], below[:], start=True, stop=True
                      ).then_inc(off_counted, 1)
            for n in range(6):
                pe.wait_ge(dve_done, V_TURN[0] if n < 2 else V_TURN[1])
                what = (srcT, relT, T["is_last"])[n // 2]
                for j in range(4):
                    jj = 4 * (n % 2) + j
                    ins = pe.transpose(psum[:, 1 + n, j * P:j * P + Q], what[:, jj * P:(jj + 1) * P],
                                       T["ident"][0:Q, 0:Q])
                ins.then_inc(turned, 1)
            for c in range(2):
                ins = pe.transpose(psum[0:H1, 7, c * P:c * P + Q], cuts[:, c, :], T["ident"][0:Q, 0:Q])
            ins.then_inc(turned, 1)


def heads_of(ap, heads):
    return ap.rearrange("p (h c) -> p h c", h=heads)


def at_block(t, i):
    return t[:, bass.ds(i, 1), :].rearrange("p o f -> p (o f)")


def nodes(nc, ph, T, gnn, phase):
    sb, sem = ph.sb, ph.sem
    psum = T["psum"]
    merging, projecting = phase > 0, phase < 2
    heads = H1 if phase == 0 else 1
    old = H1 if phase == 1 else 1
    h = sb("h", [P, 2, D])
    stats = sb("stats", [P, NB, 6])
    mean_var = sb("mean_var", [P, NB, 2])
    rstd = sb("rstd", [P, 2, NB])
    if projecting:
        w_l, w_r, att, _ = gnn[phase]
        w = sb("w", [P, 2, 2, W])
        att_row = sb("att_row", [P, D])
        att_lin = sb("att_lin", [P, D])
        att_relu = sb("att_relu", [P, D])
        w_att = sb("w_att", [P, 4, D])
        hT = sb("hT", [P, 2, 2, P])
        proj = sb("proj", [P, 2, 2, W])
        m_self = sb("m_self", [P, 2, W])
        r_self = sb("r_self", [P, 2, D])
        red = sb("red", [P, 2, H1])
    if merging:
        bias = gnn[phase - 1][3]
        bias_row = sb("bias_row", [P, D])
        aux = sb("aux_sums", [P, NB, AUXW])
        sm = sb("sm", [P, 8, NB, old])
        sums, own, va, vb, v, e_pos, e_neg, e_exp = (
            sb(n, [P, 2, D]) for n in ("sums", "own", "va", "vb", "v", "e_pos", "e_neg", "e_exp"))
        wa, wb = sm[:, 5], sm[:, 6]

    weights_in, self_in = sem("weights_in"), sem("aux_in")
    chain, chain_pool = sem("chain"), sem("chain_pool")
    stats_done, exp_ready, exp_done, wts_ready = sem("stats_done"), sem("exp_ready"), sem("exp_done"), sem("wts_ready")
    w_ready = sem("w_ready")
    h_ready, h_turned, turned_sb = sem("h_ready"), sem("h_turned"), sem("turned_sb")
    projected, xl_copied, xr_copied = sem("projected"), sem("xl_copied"), sem("xr_copied")
    m_done, relu_done, red_done, self_done = sem("m_done"), sem("relu_done"), sem("red_done"), sem("self_done")
    a_done, b_done, b_steps, v_ready, elu_steps = sem("a_done"), sem("b_done"), sem("b_steps"), sem("v_ready"), sem("elu_steps")
    x_done = sem("x_done")
    out_l = [sem(f"xl_out{k}") for k in range(2)]
    out_r = [sem(f"xr_out{k}") for k in range(2)]
    sums_in = [sem(f"sums_in{k}") for k in range(2)]
    own_in = [sem(f"own_in{k}") for k in range(2)]
    n_weights = 5 * projecting + merging

    with nc.Block() as block:
        @block.vector
        def _(dve):
            done = Mark(chain)

            def link(ins):
                dve.wait_ge(chain, done(ins))

            if phase == 0:
                for i in range(NB):
                    done(dve.bn_stats(stats[:, i, :], T["x"][:, i, :]))
                dve.wait_ge(chain, done.n)
                for i in range(NB):
                    dve.bn_aggr(mean_var[:, i, :], stats[:, i, :]).then_inc(stats_done, 1)
                dve.wait_ge(exp_done, 1)
                link(dve.reciprocal(rstd[:, 1, :], rstd[:, 0, :]))
            if merging:
                dve.sem_inc(v_ready, 2)
                dve.sem_inc(a_done, 2)
                dve.wait_ge(self_in, 16)
                me, mm, d1, d2, den, _, _, t = (sm[:, n] for n in range(8))
                own_l = T["self_logits"][:, :, 0:old]
                link(dve.tensor_scalar(t, aux[:, :, 2 * H1:2 * H1 + 1].broadcast_to([P, NB, old]), -1.0, BIG,
                                       ALU.add, ALU.mult))
                link(dve.tensor_tensor(me, aux[:, :, H1:H1 + old], t, ALU.add))
                link(dve.tensor_tensor(mm, me, own_l, ALU.max))
                dve.tensor_tensor(d1, me, mm, ALU.subtract).then_inc(exp_ready, 1)
                dve.tensor_tensor(d2, own_l, mm, ALU.subtract).then_inc(exp_ready, 1)
                dve.wait_ge(exp_done, 2)
                link(dve.tensor_tensor(den, aux[:, :, 0:old], d1, ALU.mult))
                link(dve.tensor_tensor(den, den, d2, ALU.add))
                link(dve.reciprocal(t, den))
                dve.tensor_tensor(wa, d1, t, ALU.mult).then_inc(wts_ready, 1)
                dve.tensor_tensor(wb, d2, t, ALU.mult).then_inc(wts_ready, 1)
                dve.wait_ge(wts_ready, 2)
            if projecting:
                dve.wait_ge(weights_in, 16 * n_weights)
                done(dve.tensor_scalar(att_relu[:], att_row[:], 0.8, None, ALU.mult))
                link(dve.tensor_scalar(att_lin[:], att_row[:], 0.2, None, ALU.mult))
                link(dve.memset(w[:, :, :, D:], 0.0))
                link(dve.tensor_tensor(w_att[:], w[:, :, :, 0:D].rearrange("p a b c -> p (a b) c"),
                                       bcast_mid(att_lin[:], 4), ALU.mult))
                for a in range(4):
                    dve.tensor_reduce(w[:, a // 2, a % 2, D:D + heads], heads_of(w_att[:, a, :], heads),
                                      AX.X, ALU.add).then_inc(w_ready, 1)

            def normalised(i, k, n):
                dve.wait_ge(h_turned, i + 1)
                dve.tensor_scalar(h[:, k, :], at_block(T["x"], i), mean_var[:, bass.ds(i, 1), 0],
                                  rstd[:, 1, bass.ds(i, 1)], ALU.subtract, ALU.mult).then_inc(h_ready, 1)

            def merged(i, k, n):
                dve.wait_ge(sums_in[k], 16 * (n + 1))
                dve.tensor_tensor(heads_of(va[:, k, :], old), heads_of(sums[:, k, :], old),
                                  bcast_last(at_block(wa, i), D // old), ALU.mult).then_inc(a_done, 1)
                if phase == 1:
                    dve.wait_ge(elu_steps, 3 * i + 3)
                dve.wait_ge(b_done, i + 1)
                dve.wait_ge(a_done, i + 3)
                dve.tensor_tensor(v[:, k, :], va[:, k, :], vb[:, k, :], ALU.add).then_inc(v_ready, 1)

            def joined(i, k, n):
                dve.wait_ge(elu_steps, 3 * i + 9)
                dve.wait_ge(h_turned, i + 1)
                dve.scalar_tensor_tensor(h[:, k, :], e_exp[:, k, :], -1.0, e_pos[:, k, :], ALU.add, ALU.add
                                         ).then_inc(h_ready, 1)

            def onto_x(i, k, n):
                dve.wait_ge(v_ready, i + 3)
                dve.tensor_tensor(at_block(T["x"], i), at_block(T["x"], i), v[:, k, :], ALU.add).then_inc(x_done, 1)

            def own_logits(i, k, n):
                dve.wait_ge(m_done, i + 3)
                dve.scalar_tensor_tensor(r_self[:, k, :], m_self[:, k, 0:D], 0.0, att_relu[:], ALU.max, ALU.mult
                                         ).then_inc(relu_done, 1)
                dve.wait_ge(self_done, i + 1)
                dve.wait_ge(relu_done, i + 1)
                dve.tensor_reduce(red[:, k, 0:heads], heads_of(r_self[:, k, :], heads), AX.X, ALU.add
                                  ).then_inc(red_done, 1)

            if phase == 0:
                staged(dve, NB, 2, (2, normalised), (0, own_logits))
            elif phase == 1:
                staged(dve, NB, 2, (3, merged), (2, joined), (0, own_logits))
            else:
                staged(dve, NB, 2, (1, merged), (0, onto_x))

        @block.scalar
        def _(act):
            if phase == 0:
                act.wait_ge(stats_done, NB)
                act.activation(rstd[:, 0, :], mean_var[:, :, 1], ACT.Sqrt, bias=T["eps"][:]).then_inc(exp_done, 1)
            if merging:
                act.sem_inc(elu_steps, 6)
                act.wait_ge(exp_ready, 2)
                for d in (2, 3):
                    act.activation(sm[:, d], sm[:, d], ACT.Exp).then_inc(exp_done, 1)

            def elu(i, k, n):
                act.wait_ge(h_ready, i)
                act.wait_ge(v_ready, i + 3)
                act.activation(e_neg[:, k, :], v[:, k, :], ACT.Relu, scale=-1.0).then_inc(elu_steps, 1)
                act.activation(e_pos[:, k, :], v[:, k, :], ACT.Relu).then_inc(elu_steps, 1)
                act.wait_ge(elu_steps, 3 * i + 7)
                act.activation(e_exp[:, k, :], e_neg[:, k, :], ACT.Exp, scale=-1.0).then_inc(elu_steps, 1)

            def turned_copy(i, k, n):
                act.wait_ge(projected, 2 * i + 2)
                act.wait_ge(h_turned, i + 3)
                act.copy(hT[:, k].rearrange("p a f -> p (a f)"), psum[:, k, 0:D]).then_inc(turned_sb, 1)

            def projections(i, k, n):
                for side, (stored, copied) in enumerate(((out_l, xl_copied), (out_r, xr_copied))):
                    act.wait_ge(stored[k], 16 * n)
                    act.wait_ge(m_done, i + 1)
                    act.wait_ge(projected, 2 * i + 5 + side)
                    act.copy(proj[:, k, side, :], psum[:, 2 + 2 * side + k, 0:W]).then_inc(copied, 1)

            if phase == 0:
                staged(act, NB, 2, (1, turned_copy), (0, projections))
            elif phase == 1:
                staged(act, NB, 2, (1, turned_copy), (0, projections), (3, elu))

        @block.tensor
        def _(pe):
            def turn(i, k, n):
                pe.wait_ge(turned_sb, i + 1)
                pe.wait_ge(h_ready, i + 1)
                for a in range(2):
                    ins = pe.transpose(psum[:, k, a * P:(a + 1) * P], h[:, k, a * P:(a + 1) * P], T["ident"][:])
                ins.then_inc(h_turned, 1)

            def project(i, k, n):
                pe.wait_ge(turned_sb, i + 3)
                for side, copied in enumerate((xl_copied, xr_copied)):
                    pe.wait_ge(copied, i + 1)
                    for a in range(2):
                        ins = pe.matmul(psum[:, 2 + 2 * side + k, 0:W], hT[:, k, a, :], w[:, a, side, :],
                                        start=a == 0, stop=a == 1)
                    ins.then_inc(projected, 1)

            if projecting:
                for credited, slots in ((h_turned, 2), (turned_sb, 2), (xl_copied, 2), (xr_copied, 2), (projected, 4)):
                    pe.sem_inc(credited, slots)
                pe.wait_ge(w_ready, 4)
                staged(pe, NB, 2, (1, turn), (0, project))

        @block.gpsimd
        def _(pool):
            if projecting:
                pool.sem_inc(m_done, 2)
                pool.sem_inc(self_done, 2)
            if merging:
                pool.sem_inc(b_steps, 2)
                pool.wait_ge(weights_in, 16 * n_weights)
                pool.wait_ge(wts_ready, 2)

            def own_part(i, k, n):
                pool.wait_ge(v_ready, i + 1)
                pool.wait_ge(own_in[k], 16 * (n + 1))
                pool.tensor_tensor(heads_of(vb[:, k, :], old), heads_of(own[:, k, :], old),
                                   bcast_last(at_block(wb, i), D // old), ALU.mult).then_inc(b_steps, 1)
                pool.wait_ge(b_steps, i + 3)
                pool.tensor_tensor(vb[:, k, :], vb[:, k, :], bias_row[:], ALU.add).then_inc(b_done, 1)

            def own_sum(i, k, n):
                pool.wait_ge(self_done, i + 1)
                pool.wait_ge(xl_copied, i + 3)
                pool.wait_ge(xr_copied, i + 3)
                pool.tensor_tensor(m_self[:, k, :], proj[:, k, 0, :], proj[:, k, 1, :], ALU.add).then_inc(m_done, 1)

            def own_end(i, k, n):
                pool.wait_ge(red_done, i + 1)
                pool.tensor_tensor(at_block(T["self_logits"], i)[:, 0:heads], red[:, k, 0:heads],
                                   m_self[:, k, D:D + heads], ALU.add).then_inc(self_done, 1)

            if phase == 0:
                staged(pool, NB, 2, (1, own_sum), (0, own_end))
            elif phase == 1:
                staged(pool, NB, 2, (5, own_part), (1, own_sum), (0, own_end))
            else:
                staged(pool, NB, 2, (0, own_part))

        @block.sync
        def _(sp):
            if projecting:
                for side, m in enumerate((w_l, w_r)):
                    for a in range(2):
                        sp.dma_start(w[:, a, side, 0:D], m[a * P:(a + 1) * P, :]).then_inc(weights_in, 16)
                sp.dma_start(att_row[:], att.rearrange("h c -> (h c)").partition_broadcast(P)).then_inc(weights_in, 16)
            if merging:
                sp.dma_start(bias_row[:], bias.partition_broadcast(P)).then_inc(weights_in, 16)
                sp.dma_start(aux[:], T["sums"][0:NPAD, D:AW].rearrange("(b p) a -> p b a", p=P)).then_inc(self_in, 16)

            def load(i, k, n):
                sp.wait_ge(a_done, i + 1)
                sp.dma_start(sums[:, k, :], T["sums"][bass.ds(i * P, P), 0:D]).then_inc(sums_in[k], 16)
                sp.wait_ge(b_steps, i + 1)
                sp.dma_start(own[:, k, :], T["xl"][bass.ds(i * P, P), 0:D]).then_inc(own_in[k], 16)

            def store(i, k, n):
                sp.wait_ge(xl_copied, i + 3)
                sp.dma_start(T["xl"][bass.ds(i * P, P), :], proj[:, k, 0, :]).then_inc(out_l[k], 16)
                sp.wait_ge(xr_copied, i + 3)
                sp.dma_start(T["xr"][bass.ds(i * P, P), :], proj[:, k, 1, :]).then_inc(out_r[k], 16)

            if phase == 0:
                staged(sp, NB, 2, (0, store))
            elif phase == 1:
                staged(sp, NB, 2, (5, load), (0, store))
            else:
                staged(sp, NB, 2, (0, load))
            if projecting:
                for k in range(2):
                    uses = NB // 2 + (k == 0)
                    sp.wait_ge(out_l[k], 16 * uses)
                    sp.wait_ge(out_r[k], 16 * uses)


def score(nc, ph, T, weights, layer):
    sb, sem = ph.sb, ph.sem
    psum = T["psum"]
    heads = H1 if layer == 0 else 1
    ITER = NS // RING
    HALF = RING // 2
    G = RING // 2
    XR = 4
    BANKS = 8
    xg = sb("xg", [P, RING, W])
    xr = sb("xr", [P, XR, W])
    index = sb("index", [P, 2, HALF], I32)
    rel_row = sb("rel_row", [P, 2, HALF * P], BF16)
    pick = sb("pick", [P, 2, HALF * P])
    relu = sb("relu", [P, 2, 2, D])
    red = sb("red", [P, 2, 2, H1])
    att_row = sb("att_row", [P, D])
    att_relu = sb("att_relu", [P, D])
    landed = [sem(f"landed{k}") for k in range(RING)]
    spilled = [sem(f"spilled{k}") for k in range(G)]
    xr_in = [sem(f"xr_in{k}") for k in range(XR)]
    rel_in = [sem(f"rel_in{k}") for k in range(2)]
    att_in, att_done, index_done = sem("att_in"), sem("att_done"), sem("index_done")
    asked = sem("asked")
    picked, mm_done, ps_free = sem("picked"), sem("mm_done"), sem("ps_free")
    relu_done, red_done = sem("relu_done"), sem("red_done")

    with nc.Block() as block:
        @block.gpsimd
        def _(pool):
            with pool.Fori(0, ITER) as i:
                for k in range(RING):
                    if k % HALF == 0:
                        pool.wait_ge(index_done, 2 * i + k // HALF + 1)
                    pool.wait_ge(mm_done, RING * i + k + 1)
                    pool.wait_ge(spilled[k // 2], 16 * i)
                    pool.sem_inc(asked, 1)
                    pool.indirect_dma_start(
                        out=xg[:, k, :], out_offset=None, in_=T["xl"],
                        in_offset=bass.IndirectOffsetOnAxis(ap=index[:, k // HALF, k % HALF:k % HALF + 1], axis=0),
                        bounds_check=NPAD - 1, oob_is_err=False).then_inc(landed[k], 16)

        @block.scalar
        def _(act):
            def indices(half, first):
                act.copy(index[:, half, :], T["src_lane"][:, bass.ds(first, HALF)]).then_inc(index_done, 1)

            indices(0, 0)
            indices(1, HALF)
            with act.Fori(0, ITER) as i:
                for g in range(G):
                    act.wait_ge(landed[2 * g], 16 * (i + 1))
                    act.wait_ge(landed[2 * g + 1], 16 * (i + 1))
                    act.dma_start(T["edges_xl"][bass.ds(G * i + g, 1)].rearrange("o p f -> p (o f)"),
                                  xg[:, 2 * g:2 * g + 2, :].rearrange("p t f -> p (t f)")).then_inc(spilled[g], 16)
                    if g % (G // 2) == G // 2 - 1:
                        half = g // (G // 2)
                        indices(half, RING * i + RING + HALF * half)
            for g in range(G):
                act.wait_ge(spilled[g], 16 * ITER)

        @block.sync
        def _(sp):
            sp.dma_start(att_row[:], weights[2].rearrange("h c -> (h c)").partition_broadcast(P)).then_inc(att_in, 16)
            sp.sem_inc(picked, 2)

            def rel_rows(half_id, half):
                sp.wait_ge(picked, half_id + 1)
                sp.dma_start(rel_row[:, half, :], T["rel"][bass.ds(HALF * P * half_id, HALF * P)].partition_broadcast(P)
                             ).then_inc(rel_in[half], 16)

            rel_rows(0, 0)
            with sp.Fori(0, ITER) as i:
                for g in range(G):
                    if g == 0:
                        rel_rows(2 * i + 1, 1)
                    if g == G // 2:
                        rel_rows(2 * i + 2, 0)
                    row = sp.value_load(T["block_row_s"][0:1, bass.ds(G * i + g, 1)], min_val=0, max_val=NPAD - P)
                    sp.wait_ge(mm_done, RING * i + 2 * g + RING + 2 - 2 * XR)
                    sp.dma_start(xr[:, g % XR, :], T["xr"][bass.ds(row, P), :]).then_inc(xr_in[g % XR], 16)

        @block.tensor
        def _(pe):
            pe.sem_inc(mm_done, RING)
            with pe.Fori(0, ITER) as i:
                for k in range(RING):
                    g = k // 2
                    bank = k % BANKS
                    if k % HALF == 0:
                        pe.wait_ge(picked, 2 * i + k // HALF + 3)
                    if k % 2 == 0:
                        pe.wait_ge(xr_in[g % XR], 16 * (G // XR * i + g // XR + 1))
                        pe.wait_ge(ps_free, G * i + g + 1)
                    pe.wait_ge(landed[k], 16 * (i + 1))
                    pe.matmul(psum[:, bank, 0:W], T["ident"][:], xg[:, k, :], start=True, stop=False)
                    pe.matmul(psum[:, bank, 0:W], pick[:, k // HALF, (k % HALF) * P:(k % HALF + 1) * P],
                              xr[:, g % XR, :], start=False, stop=True).then_inc(mm_done, 1)

        @block.vector
        def _(dve):
            dve.sem_inc(ps_free, BANKS // 2)
            dve.wait_ge(att_in, 16)
            dve.tensor_scalar(att_relu[:], att_row[:], 0.8, None, ALU.mult).then_inc(att_done, 1)
            dve.wait_ge(att_done, 1)

            def make_pick(i, half):
                dve.wait_ge(rel_in[half], 16 * (i + 1))
                dve.wait_ge(mm_done, RING * i + HALF * (half + 1))
                dve.tensor_scalar(pick[:, half, :], rel_row[:, half, :], T["part"][:], None, ALU.is_equal
                                  ).then_inc(picked, 1)

            make_pick(0, 0)
            with dve.Fori(0, ITER) as i:
                for g in range(G):
                    if g == 1:
                        make_pick(i, 1)
                    if g == 5:
                        make_pick(i + 1, 0)
                    pair, b = g % 2, 2 * g % BANKS
                    step = RING * i + 2 * g
                    dve.wait_ge(mm_done, step + RING + 2)
                    dve.scalar_tensor_tensor(relu[:, pair], psum[:, b:b + 2, 0:D], 0.0, bcast_mid(att_relu[:], 2),
                                             ALU.max, ALU.mult).then_inc(relu_done, 1)
                    dve.wait_ge(relu_done, G * i + g + 1)
                    dve.tensor_reduce(red[:, pair, :, 0:heads],
                                      relu[:, pair].rearrange("p t (h c) -> p t h c", h=heads), AX.X, ALU.add
                                      ).then_inc(red_done, 1)
                    dve.wait_ge(red_done, G * i + g + 1)
                    dve.tensor_tensor(T["logits"][:, bass.ds(step, 2), 0:heads], red[:, pair, :, 0:heads],
                                      psum[:, b:b + 2, D:D + heads], ALU.add).then_inc(ps_free, 1)


def softmax(nc, ph, T, layer):
    sb, sem = ph.sb, ph.sem
    psum = T["psum"]
    heads = H1 if layer == 0 else 1
    lg = sb("lg", [Q, H1, TL])
    fwd = sb("fwd", [Q, H1, TL])
    scratch = sb("scratch", [Q, 2, TL])
    tails = sb("tails", [Q, 2, H1])
    tails_t = sb("tails_t", [H1, 2, Q])
    carry_t = sb("carry_t", [H1, 2, Q + 1])
    carry = sb("carry", [Q, 2, H1])
    turned, chain, tails_turned, back = sem("turned"), sem("chain"), sem("tails_turned"), sem("back")
    exp_done, back_copied, carry_ready = sem("exp_done"), sem("back_copied"), sem("carry_ready")
    tails_ready, diff_ready, max_ready, copied = sem("tails_ready"), sem("diff_ready"), sem("max_ready"), sem("copied")
    n_turn = 2 * heads

    with nc.Block() as block:
        @block.vector
        def _(dve):
            done = Mark(chain)

            def link(ins):
                dve.wait_ge(chain, done(ins))

            link(dve.memset(tails[:], 0.0))
            for c in range(2):
                link(dve.memset(carry_t[:, c, :], -BIG))
            for n in range(n_turn):
                h, half = n // 2, n % 2
                dve.wait_ge(turned, n + 1)
                lanes = slice(half * 4 * P, (half + 1) * 4 * P)
                dve.tensor_tensor(lg[:, h, lanes], psum[0:Q, n, :], T["invalid"][:, lanes], ALU.add
                                  ).then_inc(copied, 1)
            dve.wait_ge(copied, n_turn)
            for c in range(2):
                order = slice(None, None, -1 if c else None)
                cut = T["turn_cut"][:, c:TL + c][:, order]
                tail = 0 if c else TL - 1
                for final in range(2):
                    for h in range(heads):
                        frm = (fwd if c else lg)[:, h, order]
                        to = (fwd[:, h] if final else scratch[:, h % 2])[:, order]
                        init = carry[:, c, h:h + 1] if final else -BIG
                        done(dve.tensor_tensor_scan(to, cut, frm, init, ALU.add, ALU.max))
                        if not final:
                            dve.wait_ge(chain, done.n)
                            ins = dve.tensor_copy(tails[:, c, h:h + 1], to[:, TL - 1:TL])
                            ins.then_inc(tails_ready, 1)
                    dve.wait_ge(chain, done.n)
                    if final:
                        continue
                    dve.wait_ge(tails_turned, c + 1)
                    link(dve.tensor_copy(tails_t[:, c, :], psum[0:H1, c, 0:Q]))
                    rev = slice(None, None, -1 if c else None)
                    to = carry_t[:, c, 0:Q] if c else carry_t[:, c, 1:]
                    link(dve.tensor_tensor_scan(to[:, rev], T["cut_any"][:, c, :][:, rev], tails_t[:, c, :][:, rev],
                                                -BIG, ALU.add, ALU.max))
                    dve.tensor_copy(tails_t[:, c, :], carry_t[:, c, 1:] if c else carry_t[:, c, 0:Q]
                                    ).then_inc(carry_ready, 1)
                    dve.wait_ge(back, c + 1)
                    link(dve.tensor_copy(carry[:, c, :], psum[0:Q, 2 + c, 0:H1]))
            for h in range(heads):
                dve.tensor_tensor(lg[:, h, :], lg[:, h, :], fwd[:, h, :], ALU.subtract).then_inc(diff_ready, 1)
            for h in range(heads):
                dve.tensor_tensor(fwd[:, h, :], fwd[:, h, :], T["is_last"][:], ALU.mult).then_inc(max_ready, 1)

            def back_to(n, what):
                h, half = n // 2, n % 2
                to = T["aux"][:, :, what * H1 + h].rearrange("p (q j) -> p j q", j=J)[:, 4 * half:4 * half + 4, :]
                return to, psum[:, n, :].rearrange("p (j l) -> p j l", j=4)[:, :, 0:Q]

            for n in range(n_turn):
                dve.wait_ge(back, 2 + n_turn + n + 1)
                to, frm = back_to(n, 1)
                dve.tensor_copy(to, frm).then_inc(copied, 1)

        @block.scalar
        def _(act):
            for h in range(heads):
                act.wait_ge(diff_ready, h + 1)
                act.activation(lg[:, h, :], lg[:, h, :], ACT.Exp).then_inc(exp_done, 1)
            for n in range(n_turn):
                h, half = n // 2, n % 2
                act.wait_ge(back, 2 + n + 1)
                to = T["aux"][:, :, h].rearrange("p (q j) -> p j q", j=J)[:, 4 * half:4 * half + 4, :]
                act.copy(to, psum[:, n, :].rearrange("p (j l) -> p j l", j=4)[:, :, 0:Q]).then_inc(back_copied, 1)

        @block.tensor
        def _(pe):
            for n in range(n_turn):
                h, half = n // 2, n % 2
                for j in range(4):
                    steps = T["logits"][:, :, h].rearrange("p (q j) -> p j q", j=J)[:, 4 * half + j, :]
                    ins = pe.transpose(psum[0:Q, n, j * P:(j + 1) * P], steps, T["ident"][:])
                ins.then_inc(turned, 1)
            pe.wait_ge(copied, n_turn)
            for c in range(2):
                pe.wait_ge(tails_ready, heads * (c + 1))
                pe.transpose(psum[0:H1, c, 0:Q], tails[:, c, :], T["ident"][0:Q, 0:Q]).then_inc(tails_turned, 1)
                pe.wait_ge(carry_ready, c + 1)
                pe.transpose(psum[0:Q, 2 + c, 0:H1], tails_t[:, c, :], T["ident"][0:H1, 0:H1]).then_inc(back, 1)
            for what in range(2):
                for n in range(n_turn):
                    h, half = n // 2, n % 2
                    if what == 0:
                        pe.wait_ge(exp_done, h + 1)
                    else:
                        pe.wait_ge(max_ready, h + 1)
                        pe.wait_ge(back_copied, n + 1)
                    frm = (lg, fwd)[what]
                    for j in range(4):
                        jj = 4 * half + j
                        ins = pe.transpose(psum[:, n, j * P:j * P + Q], frm[:, h, jj * P:(jj + 1) * P],
                                           T["ident"][0:Q, 0:Q])
                    ins.then_inc(back, 1)


def combine(nc, ph, T, layer):
    sb, sem = ph.sb, ph.sem
    psum = T["psum"]
    heads = H1 if layer == 0 else 1
    R = 8
    rows = sb("rows", [P, R, 2 * W])
    scaled = sb("scaled", [P, R, 2, AW])
    put = sb("put", [P, R, 2, P])
    apart = sb("apart", [P, 2, 2, P])
    index = sb("index", [P, 2, R // 2], I32)
    total = sb("total", [P, R, AW])
    rows_in = [sem(f"rows_in{k}") for k in range(R)]
    stored = [sem(f"stored{k}") for k in range(R)]
    put_dve, put_act, apart_done, scaled_done, aux_done = (
        sem("put_dve"), sem("put_act"), sem("apart_done"), sem("scaled_done"), sem("aux_done"))
    summed, total_done, zeroed, act_turn = sem("summed"), sem("total_done"), sem("zeroed"), sem("act_turn")
    index_done, asked = sem("index_done"), sem("asked")
    act_scales = heads == 1

    def step_rows(g, k, t):
        return rows[:, k, t * W:t * W + D]

    with nc.Block() as block:
        @block.sync
        def _(sp):
            def load(g, k, n):
                sp.wait_ge(scaled_done, g + 1)
                sp.dma_start(rows[:, k, :], T["edges_xl"][bass.ds(g, 1)].rearrange("o p f -> p (o f)")
                             ).then_inc(rows_in[k], 16)

            staged(sp, NG, R, (0, load))

        @block.gpsimd
        def _(pool):
            def store(g, k, n):
                half = k // (R // 2)
                if k % (R // 2) == 0:
                    for used in range(k, k + R // 2):
                        pool.wait_ge(stored[used], 16 * n)
                    pool.sem_inc(asked, 1)
                    pool.tensor_copy(index[:, half, :], T["sum_index"][:, bass.ds(g, R // 2)]).then_inc(index_done, 1)
                    pool.wait_ge(index_done, 2 * n + half + 1)
                pool.wait_ge(total_done, R + g + 1)
                pool.sem_inc(asked, 1)
                pool.indirect_dma_start(
                    out=T["sums"], in_=total[:, k, :], in_offset=None,
                    out_offset=bass.IndirectOffsetOnAxis(ap=index[:, half, k % (R // 2):k % (R // 2) + 1], axis=0),
                    bounds_check=NPAD - 1, oob_is_err=False).then_inc(stored[k], 16)

            staged(pool, NG, R, (0, store))
            for k in range(R):
                pool.wait_ge(stored[k], 16 * NG // R)

        @block.scalar
        def _(act):
            act.sem_inc(scaled_done, R) if act_scales else None

            def prepare(g, k, n):
                act.wait_ge(rows_in[k], 16 * (n + 1))
                act.wait_ge(summed, g + 1)
                act.sem_inc(act_turn, 1)
                if act_scales:
                    for t in range(2):
                        ins = act.activation(scaled[:, k, t, 0:D], step_rows(g, k, t), ACT.Copy,
                                             scale=T["aux"][:, bass.ds(2 * g + t, 1), 0])
                    ins.then_inc(scaled_done, 1)
                else:
                    for t in range(2):
                        act.activation(apart[:, k % 2, t, :], T["lane"][:, 0, :], ACT.Abs, scale=-1.0,
                                       bias=T["rel_lane"][:, bass.ds(2 * g + t, 1)]).then_inc(apart_done, 1)
                act.copy(scaled[:, k, :, D:], T["aux"][:, bass.ds(2 * g, 2), :]).then_inc(aux_done, 1)
                if not act_scales:
                    act.wait_ge(apart_done, 2 * g + 2)
                    act.activation(put[:, k], apart[:, k % 2], ACT.Relu, scale=-1.0, bias=1.0).then_inc(put_act, 1)

            staged(act, NG, R, (0, prepare))

        @block.vector
        def _(dve):
            for g in range(R):
                dve.memset(total[:, g, :], 0.0).then_inc(zeroed, 1)
            dve.wait_ge(zeroed, R)
            dve.sem_inc(total_done, R)
            if not act_scales:
                dve.sem_inc(scaled_done, R)

            def prepare(g, k, n):
                dve.wait_ge(summed, g + 1)
                if act_scales:
                    for t in range(2):
                        ins = dve.tensor_scalar(put[:, k, t, :], T["lane"][:, 0, :],
                                                T["rel_lane"][:, bass.ds(2 * g + t, 1)], None, ALU.is_equal)
                    ins.then_inc(put_dve, 1)
                else:
                    dve.wait_ge(rows_in[k], 16 * (n + 1))
                    dve.tensor_tensor(
                        scaled[:, k, :, 0:D].rearrange("p t (h c) -> p t h c", h=heads),
                        rows[:, k, :].rearrange("p (t w) -> p t w", t=2)[:, :, 0:D].rearrange(
                            "p t (h c) -> p t h c", h=heads),
                        bcast_last(T["aux"][:, bass.ds(2 * g, 2), 0:heads], D // heads), ALU.mult
                    ).then_inc(scaled_done, 1)

            def add(g, k, n):
                dve.wait_ge(summed, g + R + 1)
                dve.wait_ge(stored[k], 16 * n)
                dve.wait_ge(total_done, g + R)
                dve.scalar_tensor_tensor(total[:, k], total[:, (k - 1) % R], T["keep_s"][:, bass.ds(g, 1)],
                                         psum[:, k, 0:AW], ALU.mult, ALU.add).then_inc(total_done, 1)

            staged(dve, NG, R, (2, prepare), (0, add))

        @block.tensor
        def _(pe):
            pe.sem_inc(summed, R)

            def add_up(g, k, n):
                pe.wait_ge(put_dve if act_scales else put_act, g + 1)
                pe.wait_ge(scaled_done, g + R + 1)
                pe.wait_ge(aux_done, g + 1)
                pe.wait_ge(total_done, g + 1)
                for t in range(2):
                    ins = pe.matmul(psum[:, k, 0:AW], put[:, k, t, :], scaled[:, k, t, :], start=t == 0, stop=t == 1)
                ins.then_inc(summed, 1)

            staged(pe, NG, R, (0, add_up))


def experts(nc, T, ffn, out):
    with ExitStack() as stack:
        T["give"] = stack.enter_context(nc.sbuf_tensor("give", [P, NB], I32))
        T["take"] = stack.enter_context(nc.sbuf_tensor("take", [P, NB], I32))
        with Phase(nc, "route") as ph:
            route(nc, ph, T, ffn)
        with Phase(nc, "ffn") as ph:
            feed_forward(nc, ph, T, ffn)
        with Phase(nc, "gather") as ph:
            gather(nc, ph, T, out)


def route(nc, ph, T, ffn):
    sb, sem = ph.sb, ph.sem
    psum = T["psum"]
    gate_w, gate_b = ffn[0:2]
    stats = sb("stats", [P, NB, 6])
    mean_var = sb("mean_var", [P, NB, 2])
    rstd = sb("rstd", [P, 2, NB])
    token = sb("token", [P, NB, W])
    h = sb("h", [P, 2, D])
    hT = sb("hT", [P, 2, 2, P])
    gw = sb("gw", [P, 2, NX])
    gb = sb("gb", [P, NX])
    lo = sb("lo", [P, NB, NX])
    pr = sb("pr", [P, NB, NX])
    one_hot = sb("one_hot", [P, NB, NX])
    cand = sb("cand", [P, NB, NX])
    incl = sb("incl", [P, NB, NX])
    tri = sb("tri", [P, P])
    back8 = sb("back8", [P, NX])
    col = sb("col", [P, 6, NB])
    zeros = sb("zeros", [P, 4 * W])
    chain, stats_done, root_done = sem("chain"), sem("stats_done"), sem("root_done")
    h_ready, h_turned, turned_sb, kept_copy = sem("h_ready"), sem("h_turned"), sem("turned_sb"), sem("kept_copy")
    gated, logit_done, diff_done, exp_done = sem("gated"), sem("logit_done"), sem("diff_done"), sem("exp_done")
    tri_done, hot_done, counted, slots_done = sem("tri_done"), sem("hot_done"), sem("counted"), sem("slots_done")
    gate_in, zeroed, given, made = sem("gate_in"), sem("zeroed"), sem("given"), sem("made")

    with nc.Block() as block:
        @block.vector
        def _(dve):
            done = Mark(chain)

            def link(ins):
                dve.wait_ge(chain, done(ins))

            done(dve.memset(token[:, :, D:], 0.0))
            for i in range(NB):
                done(dve.bn_stats(stats[:, i, :], T["x"][:, i, :]))
            dve.wait_ge(chain, done.n)
            for i in range(NB):
                dve.bn_aggr(mean_var[:, i, :], stats[:, i, :]).then_inc(stats_done, 1)
            for e in range(NX):
                done(dve.memset(back8[:, e:e + 1], float(NX - e)))
            dve.wait_ge(root_done, 1)
            link(dve.reciprocal(rstd[:, 1, :], rstd[:, 0, :]))
            dve.wait_ge(gate_in, 48)

            def normalised(i, k, n):
                dve.wait_ge(h_turned, i + 1)
                dve.wait_ge(kept_copy, i + 1)
                dve.tensor_scalar(h[:, k, :], at_block(T["x"], i), mean_var[:, bass.ds(i, 1), 0],
                                  rstd[:, 1, bass.ds(i, 1)], ALU.subtract, ALU.mult).then_inc(h_ready, 1)

            def logits(i, k, n):
                dve.wait_ge(gated, i + 3)
                dve.tensor_tensor(at_block(lo, i), psum[:, 2 + k, 0:NX], gb[:], ALU.add).then_inc(logit_done, 1)

            staged(dve, NB, 2, (2, normalised), (0, logits))
            dve.wait_ge(logit_done, NB + 2)
            top, total, prob, best, pos, ok = (col[:, n] for n in range(6))
            link(dve.tensor_reduce(top, lo[:], AX.X, ALU.max))
            dve.tensor_tensor(pr[:], lo[:], bcast_last(top, NX), ALU.subtract).then_inc(diff_done, 1)
            link(dve.tensor_tensor(one_hot[:], lo[:], bcast_last(top, NX), ALU.is_equal))
            link(dve.tensor_tensor(cand[:], one_hot[:], bcast_mid(back8[:], NB), ALU.mult))
            link(dve.tensor_reduce(best, cand[:], AX.X, ALU.max))
            dve.tensor_tensor(one_hot[:], bcast_mid(back8[:], NB), bcast_last(best, NX), ALU.is_equal
                              ).then_inc(hot_done, 1)
            dve.wait_ge(exp_done, 1)
            link(dve.tensor_reduce(total, pr[:], AX.X, ALU.add))
            link(dve.reciprocal(prob, total))
            done(dve.tensor_copy(token[:, :, D], prob))
            dve.wait_ge(counted, 2)
            f2 = lambda t: t[:].rearrange("p b e -> p (b e)")
            n = NB * NX
            link(dve.tensor_copy(f2(cand), psum[:, 5, 0:n]))
            for e in range(NX):
                done(dve.tensor_tensor_scan(incl[:, :, e], T["ones"][:, 0:NB], cand[:, :, e], 0.0, ALU.mult, ALU.add))
            dve.wait_ge(chain, done.n)
            link(dve.tensor_tensor(incl[:], incl[:], cand[:], ALU.subtract))
            link(dve.tensor_tensor(f2(incl), f2(incl), psum[:, 4, 0:n], ALU.add))
            link(dve.tensor_tensor(incl[:], incl[:], one_hot[:], ALU.mult))
            link(dve.tensor_reduce(pos, incl[:], AX.X, ALU.add))
            done(dve.tensor_scalar(ok, pos, CAP + 0.5, None, ALU.is_lt))
            link(dve.tensor_scalar(best, best, -float(SLOTS), float(NX * SLOTS - 1), ALU.mult, ALU.add))
            link(dve.tensor_tensor(pos, pos, best, ALU.add))
            link(dve.tensor_scalar(top, ok, -65536.0, 65536.0, ALU.mult, ALU.add))
            dve.tensor_tensor(T["give"][:], pos, top, ALU.add).then_inc(slots_done, 1)
            link(dve.scalar_tensor_tensor(total, pos, -float(ZROW), ok, ALU.add, ALU.mult))
            dve.tensor_scalar(T["take"][:], total, float(ZROW), None, ALU.add).then_inc(slots_done, 1)
            dve.wait_ge(chain, done.n)

        @block.scalar
        def _(act):
            act.wait_ge(stats_done, NB)
            act.sem_inc(kept_copy, 2)
            act.activation(rstd[:, 0, :], mean_var[:, :, 1], ACT.Sqrt, bias=T["eps"][:]).then_inc(root_done, 1)

            def turned_copy(i, k, n):
                act.wait_ge(gated, i + 1)
                act.wait_ge(h_turned, i + 3)
                act.copy(hT[:, k].rearrange("p a f -> p (a f)"), psum[:, k, 0:D]).then_inc(turned_sb, 1)
                act.copy(at_block(token, i)[:, 0:D], h[:, k, :]).then_inc(kept_copy, 1)

            staged(act, NB, 2, (0, turned_copy))
            act.wait_ge(diff_done, 1)
            act.activation(pr[:], pr[:], ACT.Exp).then_inc(exp_done, 1)

        @block.tensor
        def _(pe):
            pe.wait_ge(gate_in, 48)

            def turn(i, k, n):
                pe.wait_ge(turned_sb, i + 1)
                pe.wait_ge(h_ready, i + 1)
                for a in range(2):
                    ins = pe.transpose(psum[:, k, a * P:(a + 1) * P], h[:, k, a * P:(a + 1) * P], T["ident"][:])
                ins.then_inc(h_turned, 1)

            def gate(i, k, n):
                pe.wait_ge(logit_done, i + 1)
                pe.wait_ge(turned_sb, i + 3)
                for a in range(2):
                    ins = pe.matmul(psum[:, 2 + k, 0:NX], hT[:, k, a, :], gw[:, a, :], start=a == 0, stop=a == 1)
                ins.then_inc(gated, 1)

            for credited in (h_turned, turned_sb, logit_done, gated):
                pe.sem_inc(credited, 2)
            staged(pe, NB, 2, (1, turn), (0, gate))
            pe.wait_ge(hot_done, 1)
            pe.wait_ge(tri_done, 1)
            hot = one_hot[:].rearrange("p b e -> p (b e)")
            pe.matmul(psum[:, 4, 0:NB * NX], tri[:], hot, start=True, stop=True).then_inc(counted, 1)
            pe.matmul(psum[:, 5, 0:NB * NX], T["ones"][:], hot, start=True, stop=True).then_inc(counted, 1)

        @block.gpsimd
        def _(pool):
            pool.memset(zeros[:], 0.0).then_inc(made, 1)
            pool.affine_select(out=tri[:], in_=T["ones"][:], compare_op=ALU.is_ge, fill=0.0, base=0,
                               pattern=[[1, P]], channel_multiplier=-1).then_inc(tri_done, 1)
            pool.wait_ge(slots_done, 2)
            pool.wait_ge(kept_copy, NB + 2)
            pool.wait_ge(zeroed, 16 * (16 + NX))
            for i in range(NB):
                pool.indirect_dma_start(
                    out=T["tokens"], out_offset=bass.IndirectOffsetOnAxis(ap=T["give"][:, i:i + 1], axis=0),
                    in_=token[:, i, :], in_offset=None, bounds_check=NX * SLOTS - 1, oob_is_err=False
                ).then_inc(given, 16)
            pool.wait_ge(given, 16 * NB)

        @block.sync
        def _(sp):
            for a in range(2):
                sp.dma_start(gw[:, a, :], gate_w[a * P:(a + 1) * P, :]).then_inc(gate_in, 16)
            sp.dma_start(gb[:], gate_b.partition_broadcast(P)).then_inc(gate_in, 16)
            sp.wait_ge(made, 1)
            for n in range(16):
                rows = NX * SLOTS // 16
                sp.dma_start(T["tokens"][n * rows:(n + 1) * rows, :].rearrange("(p r) w -> p (r w)", p=P), zeros[:]
                             ).then_inc(zeroed, 16)
            for e in range(NX):
                sp.dma_start(T["answers"][e * SLOTS + CAP:(e + 1) * SLOTS, :], zeros[0:SLOTS - CAP, 0:D]
                             ).then_inc(zeroed, 16)


def feed_forward(nc, ph, T, ffn):
    sb, sem = ph.sb, ph.sem
    psum = T["psum"]
    _, _, w1, b1, w2, b2 = ffn
    KF = F // P
    TT = -(-CAP // P)
    REST = CAP - P * (TT - 1)
    HALVES = ((0, 512), (512, CAP - 512))
    tok = sb("tok", [P, 2, TT, W])
    tT = sb("tT", [P, 2, 2, TT * P])
    w1_s = sb("w1", [P, 2, 2, F])
    w2_s = sb("w2", [P, 2, KF, D])
    b1_rows = sb("b1_rows", [NX * KF, P])
    b1_s = sb("b1", [P, NX, KF])
    b2_s = sb("b2", [P, NX, D])
    mid = sb("mid", [P, KF, TT * P])
    y = sb("y", [P, 2, D])
    mask = sb("mask", [P, 2, D], I32)
    raw = sb("raw", [P, 2, 2, D])
    fix = sb("fix", [P, 2, D])
    b1_now = sb("b1_now", [P, 2, KF])
    tok_in = [sem(f"tok_in{k}") for k in range(2)]
    w1_in = [sem(f"w1_in{k}") for k in range(2)]
    w2_in = [sem(f"w2_in{k}") for k in range(2)]
    bias_in, b1_turned, b1_ready, b1_picked = sem("bias_in"), sem("b1_turned"), sem("b1_ready"), sem("b1_picked")
    turned, turned_sb, first, mid_done, second = (
        sem("turned"), sem("turned_sb"), sem("first"), sem("mid_done"), sem("second"))
    y_steps, y_done = sem("y_steps"), sem("y_done")
    y_out = [sem(f"y_out{k}") for k in range(2)]
    BIGGEST = 3.4028234663852886e38
    PIECES = 4 * 1

    def per_expert(eng, body):
        with eng.Fori(0, NX // 2) as n:
            for k in range(2):
                body(2 * n + k, k, n)

    def tile_rows(t):
        return P if t < TT - 1 else REST

    with nc.Block() as block:
        @block.sync
        def _(sp):
            sp.dma_start(b1_rows[:], b1.rearrange("e (c p) -> (e c) p", p=P)).then_inc(bias_in, 16)
            sp.dma_start(b2_s[:].rearrange("p e d -> p (e d)"), b2.rearrange("e d -> (e d)").partition_broadcast(P)
                         ).then_inc(bias_in, 16)

            def body(e, k, n):
                sp.wait_ge(second, TT * e + TT)
                sp.wait_ge(y_done, TT * e + TT)
                sp.dma_start(tok[:, k], T["tokens"][bass.ds(e * SLOTS, SLOTS), :].rearrange("(t p) w -> p t w", p=P)
                             ).then_inc(tok_in[k], 16)
                sp.dma_start(w1_s[:, k], w1[bass.ds(e, 1)].rearrange("o (a p) f -> p (o a) f", p=P)
                             ).then_inc(w1_in[k], 16)
                sp.dma_start(w2_s[:, k], w2[bass.ds(e, 1)].rearrange("o (c p) d -> p (o c) d", p=P)
                             ).then_inc(w2_in[k], 16)

            per_expert(sp, body)

        @block.tensor
        def _(pe):
            pe.sem_inc(second, 2 * TT)
            pe.wait_ge(bias_in, 32)
            pe.transpose(psum[:, 0, 0:NX * KF], b1_rows[:], T["ident"][0:NX * KF, 0:NX * KF]).then_inc(b1_turned, 1)
            pe.wait_ge(b1_ready, 1)

            def body(e, k, n):
                pe.wait_ge(tok_in[k], 16 * (n + 1))
                for piece in range(4):
                    a, t0 = piece // 2, piece % 2 * 4
                    pe.wait_ge(turned_sb, 4 * e + piece)
                    for t in range(4):
                        ins = pe.transpose(psum[:, piece % 2, t * P:(t + 1) * P], tok[:, k, t0 + t, a * P:(a + 1) * P],
                                           T["ident"][:])
                    ins.then_inc(turned, 1)
                pe.wait_ge(turned_sb, 4 * e + 4)
                pe.wait_ge(w1_in[k], 16 * (n + 1))
                for c in range(KF):
                    for half, (t0, size) in enumerate(HALVES):
                        m = 2 * c + half
                        pe.wait_ge(mid_done, 2 * KF * e + m + 1)
                        for a in range(2):
                            ins = pe.matmul(psum[:, 2 + half, 0:size], w1_s[:, k, a, c * P:(c + 1) * P],
                                            tT[:, k, a, t0:t0 + size], start=a == 0, stop=a == 1)
                        ins.then_inc(first, 1)
                pe.wait_ge(mid_done, 2 * KF * e + 2 * KF + 2)
                pe.wait_ge(w2_in[k], 16 * (n + 1))
                for t in range(TT):
                    r = tile_rows(t)
                    pe.wait_ge(y_done, TT * e + t + 2 * TT - 1)
                    for c in range(KF):
                        ins = pe.matmul(psum[0:r, 4 + t % 2, 0:D], mid[:, c, t * P:t * P + r], w2_s[:, k, c, :],
                                        start=c == 0, stop=c == KF - 1)
                    ins.then_inc(second, 1)

            per_expert(pe, body)

        @block.scalar
        def _(act):
            act.sem_inc(mid_done, 2)

            def body(e, k, n):
                for piece in range(4):
                    a, t0 = piece // 2, piece % 2 * 4
                    act.wait_ge(turned, 4 * e + piece + 1)
                    act.copy(tT[:, k, a, t0 * P:(t0 + 4) * P], psum[:, piece % 2, :]).then_inc(turned_sb, 1)
                act.copy(b1_now[:, k, :], at_block(b1_s, e)).then_inc(b1_picked, 1)
                act.wait_ge(b1_picked, e + 1)
                act.wait_ge(second, TT * e + 2 * TT)
                for c in range(KF):
                    for half, (t0, size) in enumerate(HALVES):
                        act.wait_ge(first, 2 * KF * e + 2 * c + half + 1)
                        act.activation(mid[:, c, t0:t0 + size], psum[:, 2 + half, 0:size], ACT.Relu,
                                       bias=b1_now[:, k, c:c + 1]).then_inc(mid_done, 1)
                for t in range(TT):
                    act.wait_ge(y_done, TT * e + t + 2 * TT + 1)
                    act.dma_start(T["answers"][bass.ds(e * SLOTS + t * P, tile_rows(t)), :],
                                  y[0:tile_rows(t), t % 2, :]).then_inc(y_out[t % 2], 16)

            act.wait_ge(b1_turned, 1)
            act.copy(b1_s[:].rearrange("p e c -> p (e c)"), psum[:, 0, 0:NX * KF]).then_inc(b1_ready, 1)
            act.wait_ge(b1_ready, 1)
            per_expert(act, body)
            for s in range(2):
                act.wait_ge(y_out[s], 16 * NX * TT // 2)

        @block.vector
        def _(dve):
            dve.sem_inc(y_done, 2 * TT)
            dve.wait_ge(bias_in, 32)

            def body(e, k, n):
                for t in range(TT):
                    r, s, tile = tile_rows(t), t % 2, TT * e + t
                    yt, r0, r1 = y[0:r, s, :], raw[0:r, s, 0, :], raw[0:r, s, 1, :]
                    fin, fx = mask[0:r, s, :], fix[0:r, s, :]
                    dve.wait_ge(tok_in[k], 16 * (n + 1))
                    dve.wait_ge(second, tile + 2 * TT + 1)
                    dve.tensor_tensor(r0, psum[0:r, 4 + s, 0:D], at_block(b2_s, e)[0:r], ALU.add
                                      ).then_inc(y_steps, 1)
                    dve.wait_ge(y_steps, 7 * tile + 1)
                    dve.tensor_scalar(r1, r0, tok[0:r, k, t, D:D + 1], None, ALU.mult).then_inc(y_steps, 1)
                    dve.wait_ge(y_steps, 7 * tile + 2)
                    dve.tensor_scalar(fin, r1, 0.0, 0.0, ALU.mult, ALU.is_equal).then_inc(y_steps, 1)
                    dve.tensor_scalar(fx, r1, -BIGGEST, -1.0e4, ALU.is_lt, ALU.mult).then_inc(y_steps, 1)
                    dve.tensor_scalar(r0, r1, BIGGEST, 1.0e4, ALU.is_gt, ALU.mult).then_inc(y_steps, 1)
                    dve.wait_ge(y_out[s], 16 * (TT // 2 * e + t // 2))
                    dve.wait_ge(y_steps, 7 * tile + 5)
                    dve.tensor_tensor(yt, fx, r0, ALU.add).then_inc(y_steps, 1)
                    dve.wait_ge(y_steps, 7 * tile + 6)
                    dve.sem_inc(y_steps, 1)
                    dve.copy_predicated(yt, fin, r1).then_inc(y_done, 1)

            per_expert(dve, body)


def gather(nc, ph, T, out):
    sb, sem = ph.sb, ph.sem
    SL = 7
    assert NB % SL == 0
    got = sb("got", [P, SL, D])
    got_in = [sem(f"got_in{k}") for k in range(SL)]
    added, stored = sem("added"), sem("stored")

    with nc.Block() as block:
        @block.gpsimd
        def _(pool):
            for i in range(NB):
                if i >= SL:
                    pool.wait_ge(added, i - SL + 1)
                pool.indirect_dma_start(
                    out=got[:, i % SL, :], out_offset=None, in_=T["answers"],
                    in_offset=bass.IndirectOffsetOnAxis(ap=T["take"][:, i:i + 1], axis=0),
                    bounds_check=NX * SLOTS - 1, oob_is_err=False).then_inc(got_in[i % SL], 16)

        @block.vector
        def _(dve):
            with dve.Fori(0, NB // SL) as n:
                for k in range(SL):
                    dve.wait_ge(got_in[k], 16 * (n + 1))
                    xi = at_block(T["x"], SL * n + k)
                    dve.tensor_tensor(xi, xi, got[:, k, :], ALU.add).then_inc(added, 1)

        @block.sync
        def _(sp):
            for n in range(NB // SL):
                last = n == NB // SL - 1
                full = SL - last
                sp.wait_ge(added, SL * n + SL)
                sp.dma_start(out[P * SL * n:P * (SL * n + full)].rearrange("(b p) d -> p b d", p=P),
                             T["x"][:, SL * n:SL * n + full, :]).then_inc(stored, 16)
            sp.dma_start(out[P * (NB - 1):N], T["x"][0:LAST, NB - 1, :]).then_inc(stored, 16)
            sp.wait_ge(stored, 16 * (NB // SL + 1))


def kernel(x, src, dst, L0_gnn_Wl1, L0_gnn_Wr1, L0_gnn_att1, L0_gnn_b1, L0_gnn_Wl2, L0_gnn_Wr2, L0_gnn_att2,
           L0_gnn_b2, L0_ffn_gate_w, L0_ffn_gate_b, L0_ffn_w1, L0_ffn_b1, L0_ffn_w2, L0_ffn_b2):
    import numpy as np
    import concourse.bacc as bacc
    from concourse.bass_utils import run_bass_kernel_spmd

    nc = bacc.Bacc("TRN2", target_bir_lowering=False, num_devices=1)
    inputs = dict(x=x, src=src, dst=dst, wl1=L0_gnn_Wl1, wr1=L0_gnn_Wr1, att1=L0_gnn_att1, b1=L0_gnn_b1,
                  wl2=L0_gnn_Wl2, wr2=L0_gnn_Wr2, att2=L0_gnn_att2, b2=L0_gnn_b2, gate_w=L0_ffn_gate_w,
                  gate_b=L0_ffn_gate_b, ffn_w1=L0_ffn_w1, ffn_b1=L0_ffn_b1, ffn_w2=L0_ffn_w2, ffn_b2=L0_ffn_b2)
    arrays = {f"in_{name}": np.ascontiguousarray(a) for name, a in inputs.items()}
    ap = {name: nc.dram_tensor(f"in_{name}", arrays[f"in_{name}"].shape,
                               mybir.dt.from_np(arrays[f"in_{name}"].dtype), kind="ExternalInput").ap()
          for name in inputs}
    out = nc.dram_tensor("out", (N, D), F32, kind="ExternalOutput").ap()
    gnn = [tuple(ap[f"{n}{i}"] for n in ("wl", "wr", "att", "b")) for i in (1, 2)]
    ffn = tuple(ap[n] for n in ("gate_w", "gate_b", "ffn_w1", "ffn_b1", "ffn_w2", "ffn_b2"))
    build(nc, ap["x"], ap["src"], ap["dst"], gnn, ffn, out)
    return run_bass_kernel_spmd(nc, [arrays], core_ids=[0]).results[0]["out"]
```

```python
from contextlib import ExitStack

import concourse.bass as bass
from concourse import mybir

ALU = mybir.AluOpType
ACT = mybir.ActivationFunctionType
F32 = mybir.dt.float32
I32 = mybir.dt.int32
U32 = mybir.dt.uint32
BF16 = mybir.dt.bfloat16
AX = mybir.AxisListType

P = 128
N, D, E = 6250, 256, 100000
H1 = 4
NB = -(-N // P)
LAST = N - P * (NB - 1)
NPAD = NB * P
W = D + H1
EROWS = -(-E // P) + 2
ROWS = -(-E // P)
NG = 440
assert (ROWS + NB - 1 + NB) // 2 <= NG
NS = 2 * NG
Q = 110
J = NS // Q
TL = J * P
GQ = J // 2
assert Q * J == NS
BIG = 1.0e30
EPS = 1e-5
NX, F = 8, 1024
CAP = -(-5 * N // (4 * NX))
SLOTS = 1024
ECH = 125
assert E % ECH == 0
AUXW = 2 * H1 + 1
AW = D + AUXW
CH = 8
NC = NG // CH
GL = 2 * P
assert NC * CH == NG
PARTS = 3
BATCH = 7
assert NB % BATCH == 0
NOWHERE = 1 << 20


class Mark:

    def __init__(self, sem):
        self.sem, self.n = sem, 0

    def __call__(self, ins):
        ins.then_inc(self.sem, 1)
        self.n += 1
        return self.n


def bcast_mid(ap, n):
    return ap.unsqueeze(1).broadcast_to([ap.shape[0], n, ap.shape[1]])


def bcast_last(ap, n):
    return ap.unsqueeze(len(ap.shape)).broadcast_to([*ap.shape, n])


class Phase:

    def __init__(self, nc, name):
        self.nc, self.name, self.sems, self.stack = nc, name, [], ExitStack()

    def __enter__(self):
        return self

    def __exit__(self, *_):
        self.stack.close()
        self.nc.clear_and_free_semaphores(self.sems)
        self.nc.all_engine_barrier()

    def sem(self, name):
        self.sems.append(self.nc.alloc_semaphore(f"{self.name}_{name}"))
        return self.sems[-1]

    def sb(self, name, shape, dt=F32):
        return self.stack.enter_context(self.nc.sbuf_tensor(f"{self.name}_{name}", shape, dt))


def build(nc, x, src, dst, gnn, ffn, out):
    with ExitStack() as ctx:
        def sb(name, shape, dt=F32, stack=ctx):
            return stack.enter_context(nc.sbuf_tensor(name, shape, dt))

        def dram(name, shape, dt=F32):
            return nc.dram_tensor(name, shape, dt, kind="Internal").ap()

        T = {}
        T["src_rows"] = dram("src_rows", (EROWS, P), I32)
        T["dst_rows"] = dram("dst_rows", (EROWS, P), I32)
        T["keys"] = dram("keys", (Q * TL + 2,), F32)
        T["rel"] = dram("rel", (NS * P,), BF16)
        T["cuts"] = dram("cuts", (NG, GL + 1))
        T["some_cut"] = dram("some_cut", (2, NG))
        T["block_row"] = dram("block_row", (NG,), I32)
        T["keep"] = dram("keep", (NG,), F32)
        T["xl"] = dram("xl", (NPAD, W))
        T["xr"] = dram("xr", (NPAD, PARTS, W), BF16)
        T["totals"] = dram("totals", (NG * P, AW))
        T["tokens"] = dram("tokens", (NX * SLOTS, W))
        T["x_rows"] = dram("x_rows", (NPAD, D))
        T["psum"] = ctx.enter_context(nc.psum_tensor("psum", [P, 8, 512], F32))
        T["x"] = sb("x_res", [P, NB, D])
        T["ident"] = sb("ident", [P, P])
        T["ones"] = sb("ones", [P, P])
        T["lane"] = sb("lane", [P, 2, P])
        T["eps"] = sb("eps", [P, 1])
        T["mean"] = sb("mean", [P, NB])
        T["rstd"] = sb("rstd", [P, NB])
        with ExitStack() as g:
            T["block_row_s"] = sb("block_row_s", [1, NG], I32, g)
            T["last_rows"] = sb("last_rows", [P, NB], I32, g)
            T["keep_s"] = sb("keep_s", [P, NG], F32, g)
            T["is_last"] = sb("is_last", [P, NS], F32, g)
            T["cut9"] = sb("cut9", [1, NC, 2, H1, CH + 1], F32, g)
            T["src_lane"] = sb("src_lane", [P, NS], I32, g)
            T["rel_lane"] = sb("rel_lane", [P, NS], F32, g)
            T["part"] = sb("part", [P, 1], F32, g)
            T["self_logits"] = sb("self_logits", [P, NB, H1], F32, g)
            with Phase(nc, "tables") as ph:
                make_tables(nc, ph, T, x, src, dst)
            for layer in range(2):
                with Phase(nc, f"nodes{layer}") as ph:
                    nodes(nc, ph, T, gnn, layer)
                with Phase(nc, f"edges{layer}") as ph:
                    edges(nc, ph, T, gnn[layer], layer)
            with Phase(nc, "nodes2") as ph:
                nodes(nc, ph, T, gnn, 2)
        experts(nc, T, ffn, out)


def staged(eng, total, slots, *stages):
    lead = max(first for first, _ in stages)

    def peeled(turns):
        for t in turns:
            for first, body in stages:
                if 0 <= t + first < total:
                    body(t + first, (t + first) % slots, (t + first) // slots)

    whole = (total - lead) // slots
    peeled(range(-lead, 0))
    with eng.Fori(0, whole) as n:
        for k in range(slots):
            for first, body in stages:
                body(slots * n + k + first, (k + first) % slots, n + (k + first) // slots)
    peeled(range(whole * slots, total))


def make_tables(nc, ph, T, x, src, dst):
    sb, sem = ph.sb, ph.sem
    src_i = sb("src_i", [ECH, E // ECH], I32)
    dst_i = sb("dst_i", [ECH, E // ECH], I32)
    dst_f = sb("dst_f", [ECH, E // ECH])
    junk = sb("junk", [ECH, 2, E // ECH])
    pad_i = sb("pad_i", [1, 2, EROWS * P - E], I32)
    iot = sb("iot", [P, P], I32)
    iot_p = sb("iot_p", [P, 1], I32)
    iot_g = sb("iot_g", [Q, GQ], I32)
    thr = sb("thr", [P, NB + 1])
    blk = sb("blk", [P, NB])
    below = sb("below", [ECH, NB + 1])
    off = sb("off", [P, NB + 1])
    off_i = sb("off_i", [P, 2, NB + 1], I32)
    row_i = sb("row_i", [P, 2, NB + 1], I32)
    row_f = sb("row_f", [P, 2, NB + 1])
    n_i = sb("n_i", [P, NB], I32)
    ngi = sb("ngi", [P, NB], I32)
    n_f = sb("n_f", [P, 2, NB])
    t_in = sb("t_in", [P, NB])
    t_ex = sb("t_ex", [P, NB])
    g_id = sb("g_id", [Q, GQ])
    big4 = sb("big4", [Q, 5, GQ, NB])
    b_g = sb("b_g", [Q, GQ])
    sel = sb("sel", [Q, 6, GQ])
    some = sb("some", [Q, 2, GQ])
    some_row = sb("some_row", [1, 2, NG])
    last_f = sb("last_f", [P, NB])
    stats = sb("stats", [P, NB, 6])
    mean_var = sb("mean_var", [P, NB, 2])
    root = sb("root", [P, NB])
    cut = sb("cut", [Q, TL + 1])
    is_last = sb("is_last", [Q, TL])
    rows_s = sb("rows_s", [Q, J], I32)
    tab_i = sb("tab_i", [Q, GQ], I32)
    srcT_i = sb("srcT_i", [Q, TL], I32)
    dstT_i = sb("dstT_i", [Q, TL], I32)
    srcT = sb("srcT", [Q, TL])
    dstT = sb("dstT", [Q, TL])
    relT = sb("relT", [Q, TL])
    valid = sb("valid", [Q, TL])
    rel16 = sb("rel16", [Q, TL], BF16)
    keyx = sb("keyx", [Q, TL + 2])
    edge_pad = sb("edge_pad", [1, 2])

    in_loaded = [sem(f"in_loaded{i}") for i in range(3)]
    x_loaded = sem("x_loaded")
    rows_stored = sem("rows_stored")
    const_done = sem("const_done")
    dve_done = sem("tables_dve")
    off_counted = sem("off_counted")
    rows_gathered = sem("rows_gathered")
    keys_stored = sem("keys_stored")
    tabs_stored = sem("tabs_stored")
    keys_back = sem("keys_back")
    tabs_back = sem("tabs_back")
    some_stored, some_back, cuts_stored = sem("some_stored"), sem("some_back"), sem("cuts_stored")
    turned, root_done = sem("turned"), sem("root_done")
    psum = T["psum"]

    with nc.Block() as block:
        V_BELOW, V_ROWS, V_TABS, V_KEYS, V_STATS, V_TURN = [0], [0], [0], [0], [0], [0, 0]

        @block.vector
        def _(dve):
            done = Mark(dve_done)

            def after(n):
                dve.wait_ge(dve_done, n)

            def link(ins):
                after(done(ins))

            dve.wait_ge(const_done, 10)
            for c in range(2):
                done(dve.tensor_copy(T["lane"][:, c, :], iot[:]))
            done(dve.tensor_copy(T["part"][:], iot_p[:]))
            done(dve.tensor_copy(g_id[:], iot_g[:]))
            done(dve.tensor_copy(blk[:], iot[:, 0:NB]))
            done(dve.tensor_scalar(thr[:], iot[:, 0:NB + 1], float(P), None, ALU.mult))
            done(dve.memset(below[:, 0:1], 0.0))
            done(dve.memset(below[:, NB:], float(E // ECH)))
            dve.wait_ge(in_loaded[0], 16)
            link(dve.tensor_copy(dst_f[:], dst_i[:]))
            for b in range(1, NB):
                dve.wait_ge(dve_done, done.n - 1)
                done(dve.tensor_scalar(junk[:, b % 2], dst_f[:], float(P * b), 0.0, ALU.is_lt, ALU.add,
                                       accum_out=below[:, b:b + 1]))
            V_BELOW[0] = done.n
            dve.wait_ge(off_counted, 1)
            link(dve.tensor_copy(off[:], psum[:, 0, 0:NB + 1]))
            done(dve.tensor_copy(off_i[:, 0, :], off[:]))
            link(dve.tensor_scalar(off_i[:, 1, :], off[:], float(P - 1), None, ALU.add))
            link(dve.tensor_scalar(row_i[:], off_i[:], 7, None, ALU.arith_shift_right))
            link(dve.tensor_copy(row_f[:], row_i[:]))
            link(dve.tensor_tensor(n_f[:, 0, :], row_f[:, 1, 1:], row_f[:, 0, 0:NB], ALU.subtract))
            link(dve.tensor_scalar(n_i[:], n_f[:, 0, :], 1.0, 1.0, ALU.max, ALU.add))
            link(dve.tensor_scalar(ngi[:], n_i[:], 1, None, ALU.arith_shift_right))
            link(dve.tensor_copy(n_f[:, 1, :], ngi[:]))
            link(dve.tensor_tensor_scan(t_in[:], T["ones"][:, 0:NB], n_f[:, 1, :], 0.0, ALU.mult, ALU.add))
            link(dve.tensor_tensor(t_ex[:], t_in[:], n_f[:, 1, :], ALU.subtract))
            link(dve.tensor_scalar(last_f[:], t_in[:], -1.0, float(P), ALU.add, ALU.mult))
            done(dve.tensor_scalar(T["last_rows"][:], last_f[:], T["part"][:], None, ALU.add))
            tin_b, tex_b = bcast_mid(t_in[0:Q], GQ), bcast_mid(t_ex[0:Q], GQ)
            gid_b = bcast_last(g_id[:], NB)
            link(dve.tensor_tensor(big4[:, 0], tin_b, gid_b, ALU.is_le))
            link(dve.tensor_reduce(b_g[:], big4[:, 0], AX.X, ALU.add))
            link(dve.tensor_scalar(b_g[:], b_g[:], float(NB - 1), None, ALU.min))
            link(dve.tensor_tensor(big4[:, 1], bcast_mid(blk[0:Q], GQ), bcast_last(b_g[:], NB), ALU.is_equal))
            done(dve.tensor_tensor(big4[:, 2], big4[:, 1], tex_b, ALU.mult))
            done(dve.tensor_tensor(big4[:, 3], big4[:, 1], bcast_mid(row_f[0:Q, 0, 0:NB], GQ), ALU.mult))
            after(done.n)
            done(dve.tensor_reduce(sel[:, 0, :], big4[:, 2], AX.X, ALU.add))
            link(dve.tensor_reduce(sel[:, 1, :], big4[:, 3], AX.X, ALU.add))
            link(dve.tensor_tensor(sel[:, 5, :], g_id[:], sel[:, 0, :], ALU.subtract))
            done(dve.tensor_scalar(sel[:, 3, :], sel[:, 5, :], 0.5, None, ALU.is_gt))
            link(dve.tensor_scalar(sel[:, 5, :], sel[:, 5, :], 2.0, None, ALU.mult))
            link(dve.tensor_tensor(sel[:, 5, :], sel[:, 5, :], sel[:, 1, :], ALU.add))
            rows_v = rows_s[:].rearrange("q (g t) -> q g t", t=2)
            done(dve.tensor_scalar(rows_v[:, :, 0], sel[:, 5, :], float(ROWS), None, ALU.min))
            link(dve.tensor_scalar(rows_v[:, :, 1], sel[:, 5, :], float(ROWS), 1.0, ALU.min, ALU.add))
            V_ROWS[0] = done.n
            link(dve.tensor_scalar(sel[:, 0, :], b_g[:], float(P), None, ALU.mult))
            done(dve.tensor_copy(tab_i[:], sel[:, 0, :]))
            V_TABS[0] = done.n
            dve.wait_ge(x_loaded, 32)
            for i in range(NB):
                done(dve.bn_stats(stats[:, i, :], T["x"][:, i, :]))
            after(done.n)
            dve.wait_ge(rows_gathered, 16 * 2 * J)
            done(dve.tensor_copy(srcT[:], srcT_i[:]))
            V_TURN[0] = done.n
            link(dve.tensor_copy(dstT[:], dstT_i[:]))
            g3 = lambda t: t[:].rearrange("q (g l) -> q g l", g=GQ)
            link(dve.tensor_tensor(g3(relT), g3(dstT), bcast_last(sel[:, 0, :], 2 * P), ALU.subtract))
            done(dve.tensor_copy(rel16[:], relT[:]))
            link(dve.tensor_scalar(valid[:], relT[:], 0.0, None, ALU.is_ge))
            link(dve.scalar_tensor_tensor(valid[:], relT[:], float(P), valid[:], ALU.is_lt, ALU.mult))
            link(dve.scalar_tensor_tensor(dstT[:], dstT[:], 1.0, valid[:], ALU.add, ALU.mult))
            link(dve.tensor_scalar(keyx[:, 1:1 + TL], dstT[:], -1.0, None, ALU.add))
            V_KEYS[0] = done.n
            link(dve.memset(T["cut9"][:], -BIG))
            for i in range(NB):
                done(dve.bn_aggr(mean_var[:, i, :], stats[:, i, :]))
            after(done.n)
            done(dve.tensor_copy(T["mean"][:], mean_var[:, :, 0]))
            V_STATS[0] = done.n
            dve.wait_ge(keys_back, 32)
            link(dve.tensor_tensor(cut[:], keyx[:, 0:TL + 1], keyx[:, 1:TL + 2], ALU.not_equal))
            link(dve.tensor_scalar(cut[:], cut[:], -BIG, None, ALU.mult))
            done(dve.scalar_tensor_tensor(is_last[:], cut[:, 1:], -1.0, valid[:], ALU.is_lt, ALU.mult))
            for c in range(2):
                done(dve.tensor_reduce(some[:, c, :], cut[:, c:TL + c].rearrange("q (g l) -> q g l", g=GQ),
                                       AX.X, ALU.min))
            V_TURN[1] = done.n
            dve.wait_ge(root_done, 1)
            done(dve.reciprocal(T["rstd"][:], root[:]))
            dve.wait_ge(some_back, 16)
            for c in range(2):
                per_chunk = some_row[0:1, c, :].rearrange("o (c g) -> o c g", g=CH)[:, :, ::-1 if c else 1]
                done(dve.tensor_copy(T["cut9"][0:1, :, c, :, 1:],
                                     per_chunk.unsqueeze(2).broadcast_to([1, NC, H1, CH])))
            for n in range(6):
                dve.wait_ge(turned, n + 1)
                h = n % 2
                ps = psum[:, 1 + n, :].rearrange("p (j l) -> p j l", j=4)[:, :, 0:Q]
                if n < 2:
                    to = T["src_lane"][:]
                elif n < 4:
                    to = T["rel_lane"][:]
                else:
                    to = T["is_last"][:]
                to = to.rearrange("p (q j) -> p j q", j=J)[:, 4 * h:4 * h + 4, :]
                done(dve.tensor_copy(to, ps))

        @block.gpsimd
        def _(pool):
            pool.memset(T["ones"][:], 1.0).then_inc(const_done, 1)
            pool.wait_ge(const_done, 1)
            pool.affine_select(out=T["ident"][:], in_=T["ones"][:], compare_op=ALU.is_equal, fill=0.0, base=0,
                               pattern=[[-1, P]], channel_multiplier=1).then_inc(const_done, 1)
            pool.iota(iot[:], pattern=[[1, P]], base=0, channel_multiplier=0).then_inc(const_done, 1)
            pool.iota(iot_p[:], pattern=[[0, 1]], base=0, channel_multiplier=1).then_inc(const_done, 1)
            pool.iota(iot_g[:], pattern=[[1, GQ]], base=0, channel_multiplier=GQ).then_inc(const_done, 1)
            pool.memset(pad_i[:, 0, :], 0).then_inc(const_done, 1)
            pool.memset(pad_i[:, 1, :], 1 << 20).then_inc(const_done, 1)
            pool.memset(T["x"][:, NB - 1, :], 0.0).then_inc(const_done, 1)
            pool.memset(edge_pad[:], -2.0).then_inc(const_done, 1)
            pool.memset(T["eps"][:], EPS).then_inc(const_done, 1)
            pool.wait_ge(dve_done, V_ROWS[0])
            pool.wait_ge(rows_stored, 64)
            for j in range(J):
                for table, to in ((T["src_rows"], srcT_i), (T["dst_rows"], dstT_i)):
                    pool.indirect_dma_start(
                        out=to[:, j * P:(j + 1) * P], out_offset=None, in_=table,
                        in_offset=bass.IndirectOffsetOnAxis(ap=rows_s[:, j:j + 1], axis=0),
                        bounds_check=EROWS - 1, oob_is_err=False).then_inc(rows_gathered, 16)

        @block.scalar
        def _(act):
            act.wait_ge(dve_done, V_STATS[0])
            act.activation(root[:], mean_var[:, :, 1], ACT.Sqrt, bias=T["eps"][:]).then_inc(root_done, 1)

        @block.sync
        def _(sp):
            sp.dma_start(dst_i[:], dst.rearrange("(p f) -> p f", p=ECH)).then_inc(in_loaded[0], 16)
            sp.dma_start(src_i[:], src.rearrange("(p f) -> p f", p=ECH)).then_inc(in_loaded[1], 16)
            sp.wait_ge(const_done, 10)
            sp.dma_start(T["x"][:, 0:NB - 1, :], x[0:P * (NB - 1)].rearrange("(b p) d -> p b d", p=P)
                         ).then_inc(x_loaded, 16)
            sp.dma_start(T["x"][0:LAST, NB - 1, :], x[P * (NB - 1):N]).then_inc(x_loaded, 16)
            flat_s = T["src_rows"].rearrange("r l -> (r l)")
            flat_d = T["dst_rows"].rearrange("r l -> (r l)")
            sp.wait_ge(in_loaded[0], 16)
            sp.dma_start(flat_d[0:E].rearrange("(p f) -> p f", p=ECH), dst_i[:]).then_inc(rows_stored, 16)
            sp.dma_start(flat_d[E:].rearrange("(o f) -> o f", o=1), pad_i[:, 1, :]).then_inc(rows_stored, 16)
            sp.wait_ge(in_loaded[1], 16)
            sp.dma_start(flat_s[0:E].rearrange("(p f) -> p f", p=ECH), src_i[:]).then_inc(rows_stored, 16)
            sp.dma_start(flat_s[E:].rearrange("(o f) -> o f", o=1), pad_i[:, 0, :]).then_inc(rows_stored, 16)
            sp.wait_ge(dve_done, V_TABS[0])
            for name, what in (("block_row", tab_i[:]), ("keep", sel[:, 3, :])):
                sp.dma_start(T[name].rearrange("(q g) -> q g", q=Q), what).then_inc(tabs_stored, 16)
            sp.wait_ge(tabs_stored, 32)
            sp.dma_start(T["block_row_s"][:], T["block_row"].unsqueeze(0)).then_inc(tabs_back, 16)
            sp.dma_start(T["keep_s"][:], T["keep"].partition_broadcast(P)).then_inc(tabs_back, 16)
            sp.wait_ge(dve_done, V_KEYS[0])
            sp.dma_start(T["keys"][1:1 + Q * TL].rearrange("(q l) -> q l", q=Q), keyx[:, 1:1 + TL]
                         ).then_inc(keys_stored, 16)
            sp.dma_start(T["keys"][0:1].unsqueeze(0), edge_pad[:, 0:1]).then_inc(keys_stored, 16)
            sp.dma_start(T["keys"][1 + Q * TL:].unsqueeze(0), edge_pad[:, 1:2]).then_inc(keys_stored, 16)
            sp.dma_start(T["rel"].rearrange("(q l) -> q l", q=Q), rel16[:]).then_inc(keys_stored, 16)
            sp.wait_ge(keys_stored, 64)
            sp.dma_start(keyx[:, 0:1], T["keys"][0:Q * TL].rearrange("(q l) -> q l", q=Q)[:, 0:1],
                         allow_slow_non_contiguous=True).then_inc(keys_back, 16)
            sp.dma_start(keyx[:, TL + 1:], T["keys"][2:2 + Q * TL].rearrange("(q l) -> q l", q=Q)[:, TL - 1:],
                         allow_slow_non_contiguous=True).then_inc(keys_back, 16)
            sp.wait_ge(dve_done, V_TURN[1])
            sp.dma_start(T["some_cut"].rearrange("c (q g) -> q c g", q=Q), some[:]).then_inc(some_stored, 16)
            windows = T["cuts"].rearrange("(q g) l -> q g l", q=Q)
            sp.dma_start(windows[:, :, 0:GL], cut[:, 0:TL].rearrange("q (g l) -> q g l", g=GQ)).then_inc(cuts_stored, 16)
            sp.dma_start(windows[:, :, GL:], cut[:, 1:].rearrange("q (g l) -> q g l", g=GQ)[:, :, GL - 1:],
                         allow_slow_non_contiguous=True).then_inc(cuts_stored, 16)
            sp.wait_ge(some_stored, 16)
            sp.dma_start(some_row[:], T["some_cut"].unsqueeze(0)).then_inc(some_back, 16)
            sp.wait_ge(cuts_stored, 32)
            sp.wait_ge(some_back, 16)
            sp.wait_ge(tabs_back, 32)
            sp.wait_ge(x_loaded, 32)

        @block.tensor
        def _(pe):
            pe.wait_ge(dve_done, V_BELOW[0])
            pe.matmul(psum[:, 0, 0:NB + 1], T["ones"][0:ECH, :], below[:], start=True, stop=True
                      ).then_inc(off_counted, 1)
            for n in range(6):
                pe.wait_ge(dve_done, V_TURN[0] if n < 2 else V_TURN[1])
                what = (srcT, relT, is_last)[n // 2]
                for j in range(4):
                    jj = 4 * (n % 2) + j
                    ins = pe.transpose(psum[:, 1 + n, j * P:j * P + Q], what[:, jj * P:(jj + 1) * P],
                                       T["ident"][0:Q, 0:Q])
                ins.then_inc(turned, 1)


def heads_of(ap, heads):
    return ap.rearrange("p (h c) -> p h c", h=heads)


def at_block(t, i):
    return t[:, bass.ds(i, 1), :].rearrange("p o f -> p (o f)")


def nodes(nc, ph, T, gnn, phase):
    sb, sem = ph.sb, ph.sem
    psum = T["psum"]
    SLOTS, R, FETCH_LEAD = 2 * BATCH, BATCH, 2 * BATCH
    merging, projecting = phase > 0, phase < 2
    heads = H1 if phase == 0 else 1
    old = H1 if phase == 1 else 1
    if projecting:
        w_l, w_r, att, _ = gnn[phase]
        h = sb("h", [P, 2, D])
        w = sb("w", [P, 2, 2, W])
        att_row = sb("att_row", [P, D])
        att_lin = sb("att_lin", [P, D])
        att_relu = sb("att_relu", [P, D])
        w_att = sb("w_att", [P, 4, D])
        hT = sb("hT", [P, 2, 2, P])
        proj = sb("proj", [P, R, 2, W])
        parts = sb("parts", [P, R, PARTS, W], BF16)
        rest = sb("rest", [P, 2, W])
        m_self = sb("m_self", [P, 2, W])
        r_self = sb("r_self", [P, 2, D])
        red = sb("red", [P, 2, H1])
    if merging:
        bias = gnn[phase - 1][3]
        bias_row = sb("bias_row", [P, D])
        sums = sb("sums", [P, NB, AW])
        sm = sb("sm", [P, 7, NB, old])
        own = sb("own", [P, R, D])
        va, vb, v, e_pos, e_neg, e_exp = (sb(n, [P, 2, D]) for n in ("va", "vb", "v", "e_pos", "e_neg", "e_exp"))
        me, mm, d1, d2, den, wa, wb = (sm[:, n] for n in range(7))

    weights_in, chain, w_ready = sem("weights_in"), sem("chain"), sem("w_ready")
    sums_in = [sem(f"sums_in{k}") for k in range(2)]
    max_steps, exp_ready, exp_done, den_steps, wts_ready = (
        sem("max_steps"), sem("exp_ready"), sem("exp_done"), sem("den_steps"), sem("wts_ready"))
    h_ready, h_turned, turned_sb = sem("h_ready"), sem("h_turned"), sem("turned_sb")
    projected, xl_copied, xr_copied = sem("projected"), sem("xl_copied"), sem("xr_copied")
    m_done, red_done, self_done = sem("m_done"), sem("red_done"), sem("self_done")
    a_done, b_done, b_steps, v_ready, elu_steps = (
        sem("a_done"), sem("b_done"), sem("b_steps"), sem("v_ready"), sem("elu_steps"))
    x_done, turns = sem("x_done"), sem("turns")
    first_done, rest_done, second_done, parts_done = (
        sem("first_done"), sem("rest_done"), sem("second_done"), sem("parts_done"))
    out_l = [sem(f"xl_out{k}") for k in range(R)]
    out_r = [sem(f"xr_out{k}") for k in range(R)]
    own_in = [sem(f"own_in{k}") for k in range(R)]
    n_weights = 5 * projecting + merging

    def use(k, n):
        return SLOTS // R * n + k // R

    def batch(k, n):
        return SLOTS // BATCH * n + k // BATCH

    def batches(body):
        return lambda i, k, n: body(i, k, n) if k % BATCH == 0 else None

    with nc.Block() as block:
        @block.vector
        def _(dve):
            steps = Mark(chain)
            if merging:
                dve.sem_inc(v_ready, 2)
                dve.sem_inc(a_done, R)
                dve.wait_ge(weights_in, 16 * n_weights)
            if projecting:
                dve.sem_inc(m_done, R)
                dve.sem_inc(rest_done, R)
                dve.sem_inc(parts_done, 2)
                dve.wait_ge(weights_in, 16 * n_weights)
                steps(dve.tensor_scalar(att_relu[:], att_row[:], 0.8, None, ALU.mult))
                steps(dve.tensor_scalar(att_lin[:], att_row[:], 0.2, None, ALU.mult))
                steps(dve.memset(w[:, :, :, D:], 0.0))
                dve.wait_ge(chain, steps.n)
                dve.wait_ge(chain, steps(dve.tensor_tensor(
                    w_att[:], w[:, :, :, 0:D].rearrange("p a b c -> p (a b) c"), bcast_mid(att_lin[:], 4), ALU.mult)))
                for a in range(4):
                    dve.tensor_reduce(w[:, a // 2, a % 2, D:D + heads], heads_of(w_att[:, a, :], heads),
                                      AX.X, ALU.add).then_inc(w_ready, 1)

            def maxima(i, k, n):
                b, these = batch(k, n), bass.ds(i, BATCH)
                own_l = T["self_logits"][:, these, 0:old]
                dve.wait_ge(sums_in[k // BATCH], 16 * BATCH * (n + 1))
                dve.tensor_scalar(me[:, these], sums[:, these, D + 2 * old:D + 2 * old + 1].broadcast_to([P, BATCH, old]),
                                  -1.0, BIG, ALU.add, ALU.mult).then_inc(max_steps, 1)
                dve.wait_ge(max_steps, 3 * b + 1)
                dve.tensor_tensor(me[:, these], me[:, these], sums[:, these, D + old:D + 2 * old], ALU.add
                                  ).then_inc(max_steps, 1)
                dve.wait_ge(max_steps, 3 * b + 2)
                dve.tensor_tensor(mm[:, these], me[:, these], own_l, ALU.max).then_inc(max_steps, 1)
                dve.wait_ge(max_steps, 3 * b + 3)
                dve.tensor_tensor(d1[:, these], me[:, these], mm[:, these], ALU.subtract).then_inc(exp_ready, 1)
                dve.tensor_tensor(d2[:, these], own_l, mm[:, these], ALU.subtract).then_inc(exp_ready, 1)

            def merge_weights(i, k, n):
                b, these = batch(k, n), bass.ds(i, BATCH)
                dve.wait_ge(exp_done, 2 * b + 2)
                dve.tensor_tensor(den[:, these], sums[:, these, D:D + old], d1[:, these], ALU.mult
                                  ).then_inc(den_steps, 1)
                dve.wait_ge(den_steps, 3 * b + 1)
                dve.tensor_tensor(den[:, these], den[:, these], d2[:, these], ALU.add).then_inc(den_steps, 1)
                dve.wait_ge(den_steps, 3 * b + 2)
                dve.sem_inc(turns, 1)
                dve.reciprocal(mm[:, these], den[:, these]).then_inc(den_steps, 1)
                dve.wait_ge(den_steps, 3 * b + 3)
                dve.tensor_tensor(wa[:, these], d1[:, these], mm[:, these], ALU.mult).then_inc(wts_ready, 1)
                dve.tensor_tensor(wb[:, these], d2[:, these], mm[:, these], ALU.mult).then_inc(wts_ready, 1)

            def normalised(i, k, n):
                dve.wait_ge(h_turned, i + 1)
                dve.tensor_scalar(h[:, k % 2, :], at_block(T["x"], i), T["mean"][:, bass.ds(i, 1)],
                                  T["rstd"][:, bass.ds(i, 1)], ALU.subtract, ALU.mult).then_inc(h_ready, 1)

            def merged(i, k, n):
                s = k % 2
                dve.wait_ge(wts_ready, 2 * batch(k, n) + 2)
                dve.tensor_tensor(heads_of(va[:, s, :], old), heads_of(at_block(sums, i)[:, 0:D], old),
                                  bcast_last(at_block(wa, i), D // old), ALU.mult).then_inc(a_done, 1)
                dve.wait_ge(elu_steps, 3 * i + 3)
                dve.wait_ge(b_done, i + 1)
                dve.wait_ge(a_done, i + 1 + R)
                dve.tensor_tensor(v[:, s, :], va[:, s, :], vb[:, s, :], ALU.add).then_inc(v_ready, 1)

            def joined(i, k, n):
                s = k % 2
                dve.wait_ge(elu_steps, 3 * i + 9)
                dve.wait_ge(h_turned, i + 1)
                dve.scalar_tensor_tensor(h[:, s, :], e_exp[:, s, :], -1.0, e_pos[:, s, :], ALU.add, ALU.add
                                         ).then_inc(h_ready, 1)

            def merged_alone(i, k, n):
                s = k % 2
                dve.wait_ge(wts_ready, 2 * batch(k, n) + 2)
                dve.wait_ge(own_in[k % R], 16 * (use(k, n) + 1))
                dve.scalar_tensor_tensor(vb[:, s, :], own[:, k % R, :], at_block(wb, i), bias_row[:],
                                         ALU.mult, ALU.add).then_inc(a_done, 1)
                dve.wait_ge(a_done, i + 1 + R)
                dve.scalar_tensor_tensor(v[:, s, :], at_block(sums, i)[:, 0:D], at_block(wa, i), vb[:, s, :],
                                         ALU.mult, ALU.add).then_inc(v_ready, 1)

            def onto_x(i, k, n):
                dve.wait_ge(v_ready, i + 3)
                dve.tensor_tensor(at_block(T["x"], i), at_block(T["x"], i), v[:, k % 2, :], ALU.add
                                  ).then_inc(x_done, 1)

            def own_sum(i, k, n):
                dve.wait_ge(xl_copied, i + 3)
                dve.wait_ge(xr_copied, i + 3)
                dve.tensor_tensor(m_self[:, k % 2, :], proj[:, k % R, 0, :], proj[:, k % R, 1, :], ALU.add
                                  ).then_inc(m_done, 1)

            def own_logits(i, k, n):
                s = k % 2
                dve.wait_ge(m_done, i + 1 + R)
                for g in range(heads):
                    cols = slice(g * (D // heads), (g + 1) * (D // heads))
                    ins = dve.scalar_tensor_tensor(r_self[:, s, cols], m_self[:, s, cols], 0.0, att_relu[:, cols],
                                                   ALU.max, ALU.mult, accum_out=red[:, s, g:g + 1])
                ins.then_inc(red_done, 1)
                dve.wait_ge(red_done, i + 1)
                dve.tensor_tensor(at_block(T["self_logits"], i)[:, 0:heads], red[:, s, 0:heads],
                                  m_self[:, s, D:D + heads], ALU.add).then_inc(self_done, 1)

            def first_rest(i, k, n):
                dve.wait_ge(first_done, i + 1)
                dve.wait_ge(parts_done, i + 1)
                dve.tensor_tensor(rest[:, k % 2, :], proj[:, k % R, 1, :], parts[:, k % R, 0, :], ALU.subtract
                                  ).then_inc(rest_done, 1)

            def third_part(i, k, n):
                dve.wait_ge(second_done, i + 1)
                dve.tensor_tensor(parts[:, k % R, 2, :], rest[:, k % 2, :], parts[:, k % R, 1, :], ALU.subtract
                                  ).then_inc(parts_done, 1)

            if phase == 0:
                staged(dve, NB, SLOTS, (3, normalised), (1, own_sum), (1, first_rest), (1, own_logits),
                       (0, third_part))
            elif phase == 1:
                staged(dve, NB, SLOTS, (9, batches(maxima)), (6, batches(merge_weights)), (4, merged), (3, joined),
                       (1, own_sum), (1, first_rest), (1, own_logits), (0, third_part))
            else:
                staged(dve, NB, SLOTS, (7, batches(maxima)), (4, batches(merge_weights)), (1, merged_alone),
                       (0, onto_x))

        @block.scalar
        def _(act):
            if phase == 1:
                act.sem_inc(elu_steps, 6)
            if projecting:
                for credited in out_l + out_r:
                    act.sem_inc(credited, 16)

            def exponentials(i, k, n):
                these = bass.ds(i, BATCH)
                for which, d in enumerate((d1, d2)):
                    act.wait_ge(exp_ready, 2 * batch(k, n) + 1 + which)
                    act.sem_inc(turns, 1)
                    act.activation(d[:, these], d[:, these], ACT.Exp).then_inc(exp_done, 1)

            def elu(i, k, n):
                s = k % 2
                act.wait_ge(h_ready, i)
                act.wait_ge(v_ready, i + 3)
                act.activation(e_neg[:, s, :], v[:, s, :], ACT.Relu, scale=-1.0).then_inc(elu_steps, 1)
                act.activation(e_pos[:, s, :], v[:, s, :], ACT.Relu).then_inc(elu_steps, 1)
                act.wait_ge(elu_steps, 3 * i + 7)
                act.activation(e_exp[:, s, :], e_neg[:, s, :], ACT.Exp, scale=-1.0).then_inc(elu_steps, 1)

            def turned_copy(i, k, n):
                act.wait_ge(projected, 2 * i + 2)
                act.wait_ge(h_turned, i + 3)
                act.copy(hT[:, k % 2].rearrange("p a f -> p (a f)"), psum[:, k % 2, 0:D]).then_inc(turned_sb, 1)

            def projections(i, k, n):
                for side, (stored, copied) in enumerate(((out_l, xl_copied), (out_r, xr_copied))):
                    act.wait_ge(stored[k % R], 16 * (use(k, n) + 1))
                    act.wait_ge(m_done, i + 1)
                    act.wait_ge(projected, 2 * i + 5 + side)
                    if side:
                        act.copy(parts[:, k % R, 0, :], psum[:, 4 + k % 2, 0:W]).then_inc(first_done, 1)
                        act.wait_ge(rest_done, i + 1)
                    act.copy(proj[:, k % R, side, :], psum[:, 2 + 2 * side + k % 2, 0:W]).then_inc(copied, 1)

            def second_part(i, k, n):
                act.wait_ge(rest_done, i + 1 + R)
                act.copy(parts[:, k % R, 1, :], rest[:, k % 2, :]).then_inc(second_done, 1)

            if phase == 0:
                staged(act, NB, SLOTS, (2, turned_copy), (1, projections), (0, second_part))
            elif phase == 1:
                staged(act, NB, SLOTS, (2, turned_copy), (1, projections), (0, second_part),
                       (8, batches(exponentials)), (4, elu))
            else:
                staged(act, NB, SLOTS, (0, batches(exponentials)))

        @block.tensor
        def _(pe):
            def turn(i, k, n):
                pe.wait_ge(turned_sb, i + 1)
                pe.wait_ge(h_ready, i + 1)
                for a in range(2):
                    ins = pe.transpose(psum[:, k % 2, a * P:(a + 1) * P], h[:, k % 2, a * P:(a + 1) * P],
                                       T["ident"][:])
                ins.then_inc(h_turned, 1)

            def project(i, k, n):
                pe.wait_ge(turned_sb, i + 3)
                for side, copied in enumerate((xl_copied, xr_copied)):
                    pe.wait_ge(copied, i + 1)
                    for a in range(2):
                        ins = pe.matmul(psum[:, 2 + 2 * side + k % 2, 0:W], hT[:, k % 2, a, :], w[:, a, side, :],
                                        start=a == 0, stop=a == 1)
                    ins.then_inc(projected, 1)

            if projecting:
                for credited, slots in ((h_turned, 2), (turned_sb, 2), (xl_copied, 2), (xr_copied, 2), (projected, 4)):
                    pe.sem_inc(credited, slots)
                pe.wait_ge(w_ready, 4)
                staged(pe, NB, SLOTS, (1, turn), (0, project))

        @block.gpsimd
        def _(pool):
            def fetch_sums(i, k, n):
                b = i // BATCH
                if b > 1:
                    pool.wait_ge(sums_in[b % 2], 16 * BATCH * (b // 2))
                pool.indirect_dma_start(
                    out=sums[:, i, :], out_offset=None, in_=T["totals"],
                    in_offset=bass.IndirectOffsetOnAxis(ap=T["last_rows"][:, i:i + 1], axis=0),
                    bounds_check=NG * P - 1, oob_is_err=False).then_inc(sums_in[b % 2], 16)

            def own_part(i, k, n):
                s = k % 2
                pool.wait_ge(wts_ready, 2 * batch(k, n) + 2)
                pool.wait_ge(v_ready, i + 1)
                pool.wait_ge(own_in[k % R], 16 * (use(k, n) + 1))
                pool.tensor_tensor(heads_of(vb[:, s, :], old), heads_of(own[:, k % R, :], old),
                                   bcast_last(at_block(wb, i), D // old), ALU.mult).then_inc(b_steps, 1)
                pool.wait_ge(b_steps, i + 1 + R)
                pool.tensor_tensor(vb[:, s, :], vb[:, s, :], bias_row[:], ALU.add).then_inc(b_done, 1)

            if phase == 1:
                pool.sem_inc(b_steps, R)
                pool.wait_ge(weights_in, 16 * n_weights)
                for t in range(-FETCH_LEAD, NB):
                    for i, body in ((t + FETCH_LEAD, fetch_sums), (t, own_part)):
                        if 0 <= i < NB:
                            body(i, i % SLOTS, i // SLOTS)
            elif phase == 2:
                for i in range(NB):
                    fetch_sums(i, i % SLOTS, i // SLOTS)

        @block.sync
        def _(sp):
            if projecting:
                for side, m in enumerate((w_l, w_r)):
                    for a in range(2):
                        sp.dma_start(w[:, a, side, 0:D], m[a * P:(a + 1) * P, :]).then_inc(weights_in, 16)
                sp.dma_start(att_row[:], att.rearrange("h c -> (h c)").partition_broadcast(P)).then_inc(weights_in, 16)
            if merging:
                sp.dma_start(bias_row[:], bias.partition_broadcast(P)).then_inc(weights_in, 16)

            def load(i, k, n):
                sp.wait_ge(b_steps if phase == 1 else a_done, i + 1)
                sp.dma_start(own[:, k % R, :], T["xl"][bass.ds(i * P, P), 0:D]).then_inc(own_in[k % R], 16)

            def store(i, k, n):
                sp.wait_ge(xl_copied, i + 3)
                sp.dma_start(T["xl"][bass.ds(i * P, P), :], proj[:, k % R, 0, :]).then_inc(out_l[k % R], 16)
                sp.wait_ge(parts_done, i + 3)
                sp.dma_start(T["xr"][bass.ds(i * P, P)].rearrange("p c w -> p (c w)"),
                             parts[:, k % R].rearrange("p c w -> p (c w)")).then_inc(out_r[k % R], 16)

            if phase == 0:
                staged(sp, NB, SLOTS, (0, store))
            elif phase == 1:
                staged(sp, NB, SLOTS, (6, load), (0, store))
            else:
                staged(sp, NB, SLOTS, (0, load))
            if projecting:
                for k in range(R):
                    uses = (NB - k + R - 1) // R
                    sp.wait_ge(out_l[k], 16 * (uses + 1))
                    sp.wait_ge(out_r[k], 16 * (uses + 1))


def edges(nc, ph, T, weights, layer):
    sb, sem = ph.sb, ph.sem
    psum = T["psum"]
    heads = H1 if layer == 0 else 1
    S = 3
    SLOTS_G = S * CH
    LEAD = 2 * CH + 2
    HG = heads * CH
    WIDE = D + 2 * heads + 1
    XR, R, HALF = 4, 8, 4
    TURN, SMALL, SUM = 4, 5, 6
    act_scales = list(range(CH)) if heads == 1 else [0, 2, 3, 4, 5]
    dve_scales = [g for g in range(CH) if g not in act_scales]
    xg = sb("xg", [P, 2 * SLOTS_G, AW])
    index = sb("index", [P, S, 2 * CH], I32)
    rel_row = sb("rel_row", [P, 2, HALF * GL], BF16)
    pick = sb("pick", [P, 2, HALF * GL], BF16)
    xr = sb("xr", [P, XR, PARTS, W], BF16)
    relu = sb("relu", [P, 2, 2, D])
    red = sb("red", [P, 2, 2, H1])
    att_row = sb("att_row", [P, D])
    att_relu = sb("att_relu", [P, D])
    logits = sb("logits", [P, S, 2, heads, CH])
    cut = sb("cut", [HG, S, GL + 1])
    local = sb("local", [HG, 2, GL])
    prefix = sb("prefix", [HG, GL])
    highest = sb("highest", [HG, GL])
    shifted = sb("shifted", [HG, GL + 1])
    expd = sb("expd", [HG, GL + 1])
    at_end = sb("at_end", [HG, GL])
    tails = sb("tails", [1, 2, heads, CH + 1])
    over = sb("over", [1, 2, heads * (CH + 1) + CH])
    carry_row = sb("carry_row", [1, 2, heads, CH])
    carry = sb("carry", [HG, 2])
    factors = sb("factors", [1, heads])
    regrow = sb("regrow", [1, S, heads])
    put = sb("put", [P, R, 2, P])
    apart = sb("apart", [P, 2, 2, P])
    keep_h = sb("keep_h", [P, heads])
    grown = sb("grown", [P, WIDE])
    total = sb("total", [P, R, AW])
    landed = [sem(f"landed{k}") for k in range(2 * CH)]
    xr_in = [sem(f"xr_in{k}") for k in range(XR)]
    rel_in = [sem(f"rel_in{k}") for k in range(2)]
    cut_in = [sem(f"cut_in{k}") for k in range(S)]
    stored = [sem(f"stored{k}") for k in range(R)]
    att_in, att_done, index_done, turns = sem("att_in"), sem("att_done"), sem("index_done"), sem("turns")
    picked, mixed, relu_done, red_done = sem("picked"), sem("mixed"), sem("relu_done"), sem("red_done")
    logits_done, lg_turned, tails_ready, tails_turned = (
        sem("logits_done"), sem("lg_turned"), sem("tails_ready"), sem("tails_turned"))
    tails_copied, over_done, row_ready, carried = (
        sem("tails_copied"), sem("over_done"), sem("row_ready"), sem("carried"))
    carry_turned, carry_done, prefix_done, highest_done = (
        sem("carry_turned"), sem("carry_done"), sem("prefix_done"), sem("highest_done"))
    shift_done, end_done, exp_done, ex_back = sem("shift_done"), sem("end_done"), sem("exp_done"), sem("ex_back")
    factors_done = sem("factors_done")
    aux_done, regrow_done, apart_done, put_done = (
        sem("aux_done"), sem("regrow_done"), sem("apart_done"), sem("put_done"))
    scaled_act, scaled_dve = sem("scaled_act"), sem("scaled_dve")
    summed, grow_steps, totalled = sem("summed"), sem("grow_steps"), sem("totalled")

    def chunk(k, n):
        return S * n + k // CH

    def scale_slots(k):
        return xg[:, 2 * k:2 * k + 2, :]

    def chunk_slots(k):
        return xg[:, 2 * k:2 * k + 2 * CH, :].rearrange("p (g t) f -> p t f g", t=2)

    def begins(body):
        return lambda i, k, n: body(i, k, n) if k % CH == 0 else None

    with nc.Block() as block:
        @block.gpsimd
        def _(pool):
            def gather(i, k, n):
                c, kc, g = chunk(k, n), k // CH, k % CH
                if g == 0:
                    pool.wait_ge(index_done, c + 1)
                pool.wait_ge(summed, i + 1)
                pool.wait_ge(mixed, i + 1 + SLOTS_G - CH)
                for t in range(2):
                    pool.sem_inc(turns, 1)
                    pool.indirect_dma_start(
                        out=xg[:, 2 * k + t, 0:W], out_offset=None, in_=T["xl"],
                        in_offset=bass.IndirectOffsetOnAxis(ap=index[:, kc, 2 * g + t:2 * g + t + 1], axis=0),
                        bounds_check=NPAD - 1, oob_is_err=False).then_inc(landed[2 * g + t], 16)

            for credited in stored:
                pool.sem_inc(credited, 16)
            staged(pool, NG, SLOTS_G, (0, gather))

        @block.sync
        def _(sp):
            sp.dma_start(att_row[:], weights[2].rearrange("h c -> (h c)").partition_broadcast(P)).then_inc(att_in, 16)
            sp.sem_inc(picked, 2)
            sp.sem_inc(end_done, S)

            def rel_rows(i, k, n):
                if k % HALF == 0:
                    h = 2 * S * n + k // HALF
                    sp.wait_ge(picked, h + 1)
                    sp.dma_start(rel_row[:, k // HALF % 2, :],
                                 T["rel"][bass.ds(GL * i, HALF * GL)].partition_broadcast(P)
                                 ).then_inc(rel_in[k // HALF % 2], 16)

            def cut_rows(i, k, n):
                kc = k // CH
                sp.wait_ge(end_done, chunk(k, n) + 1)
                for h in range(heads):
                    sp.dma_start(cut[h * CH:(h + 1) * CH, kc, :], T["cuts"][bass.ds(i, CH)]).then_inc(cut_in[kc], 16)

            def right_rows(i, k, n):
                row = sp.value_load(T["block_row_s"][0:1, bass.ds(i, 1)], min_val=0, max_val=NPAD - P)
                sp.wait_ge(mixed, i + 1 + SLOTS_G - XR)
                sp.dma_start(xr[:, k % XR].rearrange("p c w -> p (c w)"),
                             T["xr"][bass.ds(row, P)].rearrange("p c w -> p (c w)")).then_inc(xr_in[k % XR], 16)

            def store(i, k, n):
                sp.wait_ge(totalled, i + R + 1)
                sp.dma_start(T["totals"][bass.ds(P * i, P), :], total[:, k % R, :]).then_inc(stored[k % R], 16)

            staged(sp, NG, SLOTS_G, (LEAD + 7, rel_rows), (LEAD + 5, right_rows), (14, begins(cut_rows)), (0, store))
            for k in range(R):
                sp.wait_ge(stored[k], 16 * NG // R + 16)

        @block.scalar
        def _(act):
            act.sem_inc(over_done, 2)

            def indices(i, k, n):
                act.wait_ge(mixed, i + CH)
                act.sem_inc(turns, 1)
                act.copy(index[:, k // CH, :], T["src_lane"][:, bass.ds(2 * i, 2 * CH)]).then_inc(index_done, 1)

            def one_hots(i, k, n):
                for t in range(2):
                    act.activation(apart[:, k % 2, t, :], T["lane"][:, 0, :], ACT.Abs, scale=-1.0,
                                   bias=T["rel_lane"][:, bass.ds(2 * i + t, 1)]).then_inc(apart_done, 1)
                act.wait_ge(apart_done, 2 * i + 2)
                act.wait_ge(summed, i + 1 + SLOTS_G - R)
                act.activation(put[:, k % R], apart[:, k % 2], ACT.Relu, scale=-1.0, bias=1.0).then_inc(put_done, 1)

            def copy_tails(i, k, n):
                c = chunk(k, n)
                act.wait_ge(over_done, 2 * c + 2)
                act.wait_ge(tails_turned, c + 1)
                for d in range(2):
                    act.copy(tails[:, d, :, 1 - d:CH + 1 - d],
                             psum[0:1, SMALL, d * HG:(d + 1) * HG].rearrange("o (h g) -> o h g", h=heads)
                             ).then_inc(tails_copied, 1)

            def copy_carries(i, k, n):
                act.wait_ge(carry_turned, chunk(k, n) + 1)
                act.wait_ge(highest_done, chunk(k, n))
                act.copy(carry[:], psum[0:HG, SMALL, 300:302]).then_inc(carry_done, 1)

            def exponentials(i, k, n):
                act.wait_ge(shift_done, 2 * chunk(k, n) + 3)
                act.activation(expd[:], shifted[:], ACT.Exp).then_inc(exp_done, 1)

            def aux_columns(i, k, n):
                c = chunk(k, n)
                act.wait_ge(ex_back, c + 1)
                act.wait_ge(regrow_done, c)
                act.copy(factors[:], psum[0:1, SMALL, 320:320 + HG].rearrange("o (h g) -> o h g", h=heads)[:, :, 0]
                         ).then_inc(factors_done, 1)
                for what in range(2):
                    frm = psum[:, SMALL, 128 + 64 * what:128 + 64 * what + 2 * HG].rearrange(
                        "p (t h g) -> p t h g", t=2, h=heads)
                    act.copy(chunk_slots(k)[:, :, D + what * heads:D + (what + 1) * heads, :], frm
                             ).then_inc(aux_done, 1)
                act.copy(xg[:, 2 * k:2 * k + 2 * CH, WIDE - 1], T["is_last"][:, bass.ds(2 * i, 2 * CH)]
                         ).then_inc(aux_done, 1)

            def scale(i, k, n):
                if k % CH not in act_scales:
                    return
                act.wait_ge(aux_done, 3 * chunk(k, n) + 3)
                for t in range(2):
                    row = xg[:, 2 * k + t, :]
                    for h in range(heads):
                        part = row[:, h * (D // heads):(h + 1) * (D // heads)]
                        ins = act.activation(part, part, ACT.Copy, scale=row[:, D + h:D + h + 1])
                ins.then_inc(scaled_act, 1)

            staged(act, NG, SLOTS_G, (28, begins(indices)), (9, begins(copy_tails)), (7, begins(copy_carries)),
                   (6, begins(exponentials)), (4, begins(aux_columns)), (5, one_hots), (3, scale))

        @block.vector
        def _(dve):
            for k in range(R):
                dve.memset(total[:, k, :], 0.0).then_inc(att_done, 1)
            dve.memset(tails[:], -BIG).then_inc(att_done, 1)
            dve.wait_ge(att_in, 16)
            dve.tensor_scalar(att_relu[:], att_row[:], 0.8, None, ALU.mult).then_inc(att_done, 1)
            dve.wait_ge(att_done, R + 2)
            dve.sem_inc(tails_copied, 2)
            dve.sem_inc(totalled, R)
            dve.sem_inc(logits_done, 2)
            dve.sem_inc(shift_done, 1)

            def make_pick(i, k, n):
                if k % HALF == 0:
                    half = k // HALF % 2
                    dve.wait_ge(rel_in[half], 16 * (S * n + k // CH + 1))
                    dve.wait_ge(mixed, i + SLOTS_G - HALF)
                    dve.tensor_scalar(pick[:, half, :], rel_row[:, half, :], T["part"][:], None, ALU.is_equal
                                      ).then_inc(picked, 1)

            def score(i, k, n):
                pair, b = k % 2, 2 * k % 4
                dve.wait_ge(mixed, i + SLOTS_G + 1)
                for t in range(2):
                    for h in range(heads):
                        cols = slice(h * (D // heads), (h + 1) * (D // heads))
                        ins = dve.scalar_tensor_tensor(relu[:, pair, t, cols], psum[:, b + t, cols], 0.0,
                                                       att_relu[:, cols], ALU.max, ALU.mult,
                                                       accum_out=red[:, pair, t, h:h + 1])
                ins.then_inc(red_done, 1)
                dve.wait_ge(red_done, i + 1)
                dve.tensor_tensor(logits[:, k // CH, :, :, k % CH], red[:, pair, :, 0:heads],
                                  psum[:, b:b + 2, D:D + heads], ALU.add).then_inc(logits_done, 1)

            def scan_groups(i, k, n):
                c, kc = chunk(k, n), k // CH
                dve.wait_ge(cut_in[kc], 16 * heads * (n + 1))
                dve.wait_ge(lg_turned, c + 1)
                for d in range(2):
                    order = slice(None, None, -1 if d else None)
                    dve.tensor_tensor_scan(local[:, d, order], cut[:, kc, d:GL + d][:, order],
                                           psum[0:HG, TURN, 0:GL][:, order], -BIG, ALU.add, ALU.max
                                           ).then_inc(tails_ready, 1)

            def scan_over(i, k, n):
                c, long = chunk(k, n), heads * (CH + 1)
                dve.wait_ge(tails_copied, 2 * c + 4)
                dve.wait_ge(carried, c)
                for d in range(2):
                    order = slice(None, None, -1 if d else None)
                    at = T["cut9"][0:1, bass.ds(c, 1), d, 0:heads, :].rearrange("o c h g -> o (c h g)")
                    dve.tensor_tensor_scan(over[:, d, CH - 1 - d:CH - 1 - d + long][:, order], at,
                                           tails[:, d].rearrange("o h g -> o (h g)")[:, order],
                                           -BIG, ALU.add, ALU.max).then_inc(over_done, 1)
                dve.wait_ge(over_done, 2 * c + 4)
                line = over[:, :, CH - 1:CH - 1 + long].rearrange("o d (h g) -> o d h g", h=heads)
                dve.tensor_copy(carry_row[:], line[:, :, :, 0:CH]).then_inc(row_ready, 1)
                dve.tensor_copy(tails[:, 0, :, 0], line[:, 0, :, CH]).then_inc(carried, 1)

            def maxima(i, k, n):
                c, kc = chunk(k, n), k // CH
                dve.wait_ge(carry_done, c + 1)
                dve.tensor_tensor_scan(prefix[:], cut[:, kc, 0:GL], psum[0:HG, TURN, 0:GL], carry[:, 0:1],
                                       ALU.add, ALU.max).then_inc(prefix_done, 1)
                dve.wait_ge(prefix_done, c + 1)
                dve.tensor_tensor_scan(highest[:, ::-1], cut[:, kc, 1:][:, ::-1], prefix[:, ::-1], carry[:, 1:2],
                                       ALU.add, ALU.max).then_inc(highest_done, 1)

            def subtract(i, k, n):
                c, kc = chunk(k, n), k // CH
                dve.wait_ge(highest_done, c + 1)
                dve.wait_ge(exp_done, c)
                dve.tensor_tensor(shifted[:, 0:GL], psum[0:HG, TURN, 0:GL], highest[:], ALU.subtract
                                  ).then_inc(shift_done, 1)
                dve.scalar_tensor_tensor(shifted[:, GL:], carry[:, 0:1], cut[:, kc, 0:1], highest[:, 0:1],
                                         ALU.add, ALU.subtract).then_inc(shift_done, 1)
                dve.wait_ge(ex_back, c)
                dve.scalar_tensor_tensor(at_end[:], cut[:, kc, 1:], -1.0, highest[:], ALU.is_lt, ALU.mult
                                         ).then_inc(end_done, 1)

            def scale(i, k, n):
                if k % CH == 0:
                    dve.wait_ge(factors_done, chunk(k, n) + 1)
                    dve.tensor_scalar(regrow[:, k // CH, :], factors[:], -1.0, None, ALU.add).then_inc(regrow_done, 1)
                if k % CH in dve_scales:
                    dve.wait_ge(aux_done, 3 * chunk(k, n) + 3)
                    both = scale_slots(k)
                    rows = both[:, :, 0:D].rearrange("p t (h c) -> p t h c", h=heads)
                    dve.tensor_tensor(rows, rows, bcast_last(both[:, :, D:D + heads], D // heads), ALU.mult
                                      ).then_inc(scaled_dve, 1)

            def add(i, k, n):
                keep = T["keep_s"][:, bass.ds(i, 1)]
                sum_, old, new = psum[:, SUM + k % 2, :], total[:, (k - 1) % R], total[:, k % R]
                dve.wait_ge(summed, i + SLOTS_G + 1)
                dve.wait_ge(stored[k % R], 16 * (chunk(k, n) + 1))
                dve.wait_ge(totalled, i + R)
                if k % CH:
                    dve.scalar_tensor_tensor(new[:, 0:WIDE], old[:, 0:WIDE], keep, sum_[:, 0:WIDE],
                                             ALU.mult, ALU.add).then_inc(totalled, 1)
                    return
                steps = 5 * chunk(k, n)
                dve.tensor_scalar(keep_h[:], sum_[:, WIDE:WIDE + heads], keep, keep, ALU.mult, ALU.add
                                  ).then_inc(grow_steps, 1)
                dve.wait_ge(grow_steps, steps + 1)
                dve.tensor_tensor(heads_of(grown[:, 0:D], heads), heads_of(old[:, 0:D], heads),
                                  bcast_last(keep_h[:], D // heads), ALU.mult).then_inc(grow_steps, 1)
                dve.tensor_tensor(grown[:, D:D + heads], old[:, D:D + heads], keep_h[:], ALU.mult
                                  ).then_inc(grow_steps, 1)
                dve.tensor_scalar(grown[:, D + heads:], old[:, D + heads:WIDE], keep, None, ALU.mult
                                  ).then_inc(grow_steps, 1)
                dve.sem_inc(grow_steps, 1)
                dve.wait_ge(grow_steps, steps + 5)
                dve.tensor_tensor(new[:, 0:WIDE], grown[:], sum_[:, 0:WIDE], ALU.add).then_inc(totalled, 1)

            staged(dve, NG, SLOTS_G, (LEAD + 1, score), (11, begins(scan_groups)), (9, begins(scan_over)),
                   (7, begins(maxima)), (6, begins(subtract)), (3, scale), (0, add), (LEAD + 3, make_pick))

        @block.tensor
        def _(pe):
            pe.sem_inc(mixed, SLOTS_G)
            pe.sem_inc(summed, SLOTS_G)

            def mix(i, k, n):
                g, b = k % CH, 2 * k % 4
                if k % HALF == 0:
                    pe.wait_ge(picked, 2 * S * n + k // HALF + 3)
                pe.wait_ge(xr_in[k % XR], 16 * (SLOTS_G // XR * n + k // XR + 1))
                pe.wait_ge(logits_done, i + 1)
                for t in range(2):
                    pe.wait_ge(landed[2 * g + t], 16 * (chunk(k, n) + 1))
                    pe.matmul(psum[:, b + t, 0:W], T["ident"][:], xg[:, 2 * k + t, 0:W], start=True, stop=False)
                    lanes = (k % HALF) * GL + t * P
                    for part in range(PARTS):
                        ins = pe.matmul(psum[:, b + t, 0:W], pick[:, k // HALF % 2, lanes:lanes + P],
                                        xr[:, k % XR, part, :], start=False, stop=part == PARTS - 1)
                ins.then_inc(mixed, 1)

            def turn_logits(i, k, n):
                pe.wait_ge(logits_done, i + CH + 2)
                pe.wait_ge(shift_done, 2 * chunk(k, n) + 1)
                for t in range(2):
                    ins = pe.transpose(psum[0:HG, TURN, t * P:(t + 1) * P],
                                       logits[:, k // CH, t].rearrange("p h g -> p (h g)"), T["ident"][:])
                ins.then_inc(lg_turned, 1)

            def turn_tails(i, k, n):
                pe.wait_ge(tails_ready, 2 * chunk(k, n) + 2)
                pe.wait_ge(aux_done, 3 * chunk(k, n))
                pe.sem_inc(turns, 1)
                for d in range(2):
                    lane = 0 if d else GL - 1
                    ins = pe.transpose(psum[0:1, SMALL, d * HG:(d + 1) * HG], local[:, d, lane:lane + 1],
                                       T["ident"][0:HG, 0:HG])
                ins.then_inc(tails_turned, 1)

            def turn_carries(i, k, n):
                pe.wait_ge(row_ready, chunk(k, n) + 1)
                pe.sem_inc(turns, 1)
                for d in range(2):
                    ins = pe.transpose(psum[0:HG, SMALL, 300 + d:301 + d],
                                       carry_row[:, d].rearrange("o h g -> o (h g)"), T["ident"][0:1, 0:1])
                ins.then_inc(carry_turned, 1)

            def turn_back(i, k, n):
                c = chunk(k, n)
                pe.wait_ge(exp_done, c + 1)
                pe.wait_ge(end_done, c + 1 + S)
                pe.sem_inc(turns, 1)
                pe.transpose(psum[0:1, SMALL, 320:320 + HG], expd[:, GL:], T["ident"][0:HG, 0:HG])
                for what, frm in enumerate((expd, at_end)):
                    for t in range(2):
                        at = 128 + 64 * what + t * HG
                        ins = pe.transpose(psum[:, SMALL, at:at + HG], frm[:, t * P:(t + 1) * P],
                                           T["ident"][0:HG, 0:HG])
                ins.then_inc(ex_back, 1)

            def add_up(i, k, n):
                c, bank = chunk(k, n), SUM + k % 2
                pe.wait_ge(put_done, i + 1)
                pe.wait_ge(aux_done, 3 * c + 3)
                g = k % CH
                mine, who = (act_scales, scaled_act) if g in act_scales else (dve_scales, scaled_dve)
                pe.wait_ge(who, len(mine) * c + mine.index(g) + 1)
                pe.wait_ge(totalled, i + R - 1)
                if k % CH == 0:
                    pe.wait_ge(regrow_done, c + 1)
                    pe.matmul(psum[:, bank, WIDE:WIDE + heads], put[0:1, k % R, 0, :], regrow[:, k // CH, :],
                              start=True, stop=True)
                for t in range(2):
                    ins = pe.matmul(psum[:, bank, 0:WIDE], put[:, k % R, t, :], xg[:, 2 * k + t, 0:WIDE],
                                    start=t == 0, stop=t == 1)
                ins.then_inc(summed, 1)

            staged(pe, NG, SLOTS_G, (8, begins(turn_tails)), (6, begins(turn_carries)), (3, begins(turn_back)),
                   (LEAD, mix), (10, begins(turn_logits)), (0, add_up))


def experts(nc, T, ffn, out):
    with ExitStack() as stack:
        T["give"] = stack.enter_context(nc.sbuf_tensor("give", [P, NB], I32))
        with Phase(nc, "route") as ph:
            route(nc, ph, T, ffn, out)
        with Phase(nc, "ffn") as ph:
            feed_forward(nc, ph, T, ffn, out)


def route(nc, ph, T, ffn, out):
    sb, sem = ph.sb, ph.sem
    psum = T["psum"]
    gate_w, gate_b = ffn[0:2]
    stats = sb("stats", [P, NB, 6])
    mean_var = sb("mean_var", [P, NB, 2])
    rstd = sb("rstd", [P, 2, NB])
    token = sb("token", [P, NB, W])
    number = sb("number", [P, NB], I32)
    h = sb("h", [P, 2, D])
    hT = sb("hT", [P, 2, 2, P])
    gw = sb("gw", [P, 2, NX])
    gb = sb("gb", [P, NX])
    lo = sb("lo", [P, NB, NX])
    pr = sb("pr", [P, NB, NX])
    one_hot = sb("one_hot", [P, NB, NX])
    cand = sb("cand", [P, NB, NX])
    incl = sb("incl", [P, NB, NX])
    tri = sb("tri", [P, P])
    back8 = sb("back8", [P, NX])
    col = sb("col", [P, 6, NB])
    zeros = sb("zeros", [P, 4 * W])
    chain, stats_done, root_done = sem("chain"), sem("stats_done"), sem("root_done")
    h_ready, h_turned, turned_sb, kept_copy = sem("h_ready"), sem("h_turned"), sem("turned_sb"), sem("kept_copy")
    gated, logit_done, diff_done, exp_done = sem("gated"), sem("logit_done"), sem("diff_done"), sem("exp_done")
    tri_done, hot_done, counted, slots_done = sem("tri_done"), sem("hot_done"), sem("counted"), sem("slots_done")
    x_out = sem("x_out")
    gate_in, zeroed, given, made = sem("gate_in"), sem("zeroed"), sem("given"), sem("made")

    with nc.Block() as block:
        @block.vector
        def _(dve):
            done = Mark(chain)

            def link(ins):
                dve.wait_ge(chain, done(ins))

            link(dve.memset(token[:, :, D:], 0.0))
            dve.wait_ge(made, 3)
            done(dve.tensor_copy(token[:, :, D + 1], number[:]))
            for i in range(NB):
                done(dve.bn_stats(stats[:, i, :], T["x"][:, i, :]))
            dve.wait_ge(chain, done.n)
            for i in range(NB):
                dve.bn_aggr(mean_var[:, i, :], stats[:, i, :]).then_inc(stats_done, 1)
            for e in range(NX):
                done(dve.memset(back8[:, e:e + 1], float(NX - e)))
            dve.wait_ge(root_done, 1)
            link(dve.reciprocal(rstd[:, 1, :], rstd[:, 0, :]))
            dve.wait_ge(gate_in, 48)

            def normalised(i, k, n):
                dve.wait_ge(h_turned, i + 1)
                dve.wait_ge(kept_copy, i + 1)
                dve.tensor_scalar(h[:, k, :], at_block(T["x"], i), mean_var[:, bass.ds(i, 1), 0],
                                  rstd[:, 1, bass.ds(i, 1)], ALU.subtract, ALU.mult).then_inc(h_ready, 1)

            def logits(i, k, n):
                dve.wait_ge(gated, i + 3)
                dve.tensor_tensor(at_block(lo, i), psum[:, 2 + k, 0:NX], gb[:], ALU.add).then_inc(logit_done, 1)

            staged(dve, NB, 2, (2, normalised), (0, logits))
            dve.wait_ge(logit_done, NB + 2)
            top, total, prob, best, pos, ok = (col[:, n] for n in range(6))
            link(dve.tensor_reduce(top, lo[:], AX.X, ALU.max))
            dve.tensor_tensor(pr[:], lo[:], bcast_last(top, NX), ALU.subtract).then_inc(diff_done, 1)
            link(dve.tensor_tensor(one_hot[:], lo[:], bcast_last(top, NX), ALU.is_equal))
            link(dve.tensor_tensor(cand[:], one_hot[:], bcast_mid(back8[:], NB), ALU.mult))
            link(dve.tensor_reduce(best, cand[:], AX.X, ALU.max))
            dve.tensor_tensor(one_hot[:], bcast_mid(back8[:], NB), bcast_last(best, NX), ALU.is_equal
                              ).then_inc(hot_done, 1)
            dve.wait_ge(exp_done, 1)
            link(dve.tensor_reduce(total, pr[:], AX.X, ALU.add))
            link(dve.reciprocal(prob, total))
            done(dve.tensor_copy(token[:, :, D], prob))
            dve.wait_ge(counted, 2)
            f2 = lambda t: t[:].rearrange("p b e -> p (b e)")
            n = NB * NX
            link(dve.tensor_copy(f2(cand), psum[:, 5, 0:n]))
            for e in range(NX):
                done(dve.tensor_tensor_scan(incl[:, :, e], T["ones"][:, 0:NB], cand[:, :, e], 0.0, ALU.mult, ALU.add))
            dve.wait_ge(chain, done.n)
            link(dve.tensor_tensor(incl[:], incl[:], cand[:], ALU.subtract))
            link(dve.tensor_tensor(f2(incl), f2(incl), psum[:, 4, 0:n], ALU.add))
            link(dve.tensor_tensor(incl[:], incl[:], one_hot[:], ALU.mult))
            link(dve.tensor_reduce(pos, incl[:], AX.X, ALU.add))
            done(dve.tensor_scalar(ok, pos, CAP + 0.5, None, ALU.is_lt))
            link(dve.tensor_scalar(best, best, -float(SLOTS), float(NX * SLOTS - 1), ALU.mult, ALU.add))
            link(dve.tensor_tensor(pos, pos, best, ALU.add))
            link(dve.tensor_scalar(top, ok, -65536.0, 65536.0, ALU.mult, ALU.add))
            dve.tensor_tensor(T["give"][:], pos, top, ALU.add).then_inc(slots_done, 1)
            dve.wait_ge(chain, done.n)

        @block.scalar
        def _(act):
            act.wait_ge(stats_done, NB)
            act.sem_inc(kept_copy, 2)
            act.activation(rstd[:, 0, :], mean_var[:, :, 1], ACT.Sqrt, bias=T["eps"][:]).then_inc(root_done, 1)

            def turned_copy(i, k, n):
                act.wait_ge(gated, i + 1)
                act.wait_ge(h_turned, i + 3)
                act.copy(hT[:, k].rearrange("p a f -> p (a f)"), psum[:, k, 0:D]).then_inc(turned_sb, 1)
                act.copy(at_block(token, i)[:, 0:D], h[:, k, :]).then_inc(kept_copy, 1)

            staged(act, NB, 2, (0, turned_copy))
            act.wait_ge(diff_done, 1)
            act.activation(pr[:], pr[:], ACT.Exp).then_inc(exp_done, 1)

        @block.tensor
        def _(pe):
            pe.wait_ge(gate_in, 48)

            def turn(i, k, n):
                pe.wait_ge(turned_sb, i + 1)
                pe.wait_ge(h_ready, i + 1)
                for a in range(2):
                    ins = pe.transpose(psum[:, k, a * P:(a + 1) * P], h[:, k, a * P:(a + 1) * P], T["ident"][:])
                ins.then_inc(h_turned, 1)

            def gate(i, k, n):
                pe.wait_ge(logit_done, i + 1)
                pe.wait_ge(turned_sb, i + 3)
                for a in range(2):
                    ins = pe.matmul(psum[:, 2 + k, 0:NX], hT[:, k, a, :], gw[:, a, :], start=a == 0, stop=a == 1)
                ins.then_inc(gated, 1)

            for credited in (h_turned, turned_sb, logit_done, gated):
                pe.sem_inc(credited, 2)
            staged(pe, NB, 2, (1, turn), (0, gate))
            pe.wait_ge(hot_done, 1)
            pe.wait_ge(tri_done, 1)
            hot = one_hot[:].rearrange("p b e -> p (b e)")
            pe.matmul(psum[:, 4, 0:NB * NX], tri[:], hot, start=True, stop=True).then_inc(counted, 1)
            pe.matmul(psum[:, 5, 0:NB * NX], T["ones"][:], hot, start=True, stop=True).then_inc(counted, 1)

        @block.gpsimd
        def _(pool):
            pool.iota(number[:], pattern=[[P, NB]], base=0, channel_multiplier=1).then_inc(made, 1)
            pool.memset(zeros[:], 0.0).then_inc(made, 1)
            pool.wait_ge(made, 2)
            pool.memset(zeros[:].rearrange("p (r w) -> p r w", w=W)[:, :, D + 1], float(NOWHERE)).then_inc(made, 1)
            pool.affine_select(out=tri[:], in_=T["ones"][:], compare_op=ALU.is_ge, fill=0.0, base=0,
                               pattern=[[1, P]], channel_multiplier=-1).then_inc(tri_done, 1)
            pool.wait_ge(slots_done, 1)
            pool.wait_ge(kept_copy, NB + 2)
            pool.wait_ge(zeroed, 16 * 16)
            for i in range(NB):
                pool.indirect_dma_start(
                    out=T["tokens"], out_offset=bass.IndirectOffsetOnAxis(ap=T["give"][:, i:i + 1], axis=0),
                    in_=token[:, i, :], in_offset=None, bounds_check=NX * SLOTS - 1, oob_is_err=False
                ).then_inc(given, 16)
            pool.wait_ge(given, 16 * NB)

        @block.sync
        def _(sp):
            for a in range(2):
                sp.dma_start(gw[:, a, :], gate_w[a * P:(a + 1) * P, :]).then_inc(gate_in, 16)
            sp.dma_start(gb[:], gate_b.partition_broadcast(P)).then_inc(gate_in, 16)
            sp.wait_ge(made, 3)
            for n in range(16):
                rows = NX * SLOTS // 16
                sp.dma_start(T["tokens"][n * rows:(n + 1) * rows, :].rearrange("(p r) w -> p (r w)", p=P), zeros[:]
                             ).then_inc(zeroed, 16)
            sp.dma_start(T["x_rows"].rearrange("(b p) d -> p b d", p=P), T["x"][:]).then_inc(x_out, 16)
            sp.dma_start(out[0:P * (NB - 1)].rearrange("(b p) d -> p b d", p=P), T["x"][:, 0:NB - 1, :]
                         ).then_inc(x_out, 16)
            sp.dma_start(out[P * (NB - 1):N], T["x"][0:LAST, NB - 1, :]).then_inc(x_out, 16)
            sp.wait_ge(x_out, 48)


def feed_forward(nc, ph, T, ffn, out):
    sb, sem = ph.sb, ph.sem
    psum = T["psum"]
    _, _, w1, b1, w2, b2 = ffn
    KF = F // P
    TT = -(-CAP // P)
    REST = CAP - P * (TT - 1)
    HALVES = ((0, 512), (512, CAP - 512))
    tok = sb("tok", [P, 2, TT, W])
    tT = sb("tT", [P, 2, 2, TT * P])
    w1_s = sb("w1", [P, 2, 2, F])
    w2_s = sb("w2", [P, 2, KF, D])
    b1_rows = sb("b1_rows", [NX * KF, P])
    b1_s = sb("b1", [P, NX, KF])
    b2_s = sb("b2", [P, NX, D])
    mid = sb("mid", [P, KF, TT * P])
    y = sb("y", [P, 2, D])
    mask = sb("mask", [P, 2, D], I32)
    raw = sb("raw", [P, 2, 2, D])
    fix = sb("fix", [P, 2, D])
    b1_now = sb("b1_now", [P, 2, KF])
    number = sb("number", [P, 2, TT], I32)
    x_back = sb("x_back", [P, TT, D])
    tok_in = [sem(f"tok_in{k}") for k in range(2)]
    w1_in = [sem(f"w1_in{k}") for k in range(2)]
    w2_in = [sem(f"w2_in{k}") for k in range(2)]
    bias_in, b1_turned, b1_ready, b1_picked = sem("bias_in"), sem("b1_turned"), sem("b1_ready"), sem("b1_picked")
    turned, turned_sb, first, mid_done, second = (
        sem("turned"), sem("turned_sb"), sem("first"), sem("mid_done"), sem("second"))
    y_steps, y_done = sem("y_steps"), sem("y_done")
    x_in = [sem(f"x_in{k}") for k in range(TT)]
    y_out, y_free, numbered, asked = sem("y_out"), sem("y_free"), sem("numbered"), sem("asked")
    BIGGEST = 3.4028234663852886e38

    def per_expert(eng, body):
        with eng.Fori(0, NX // 2) as n:
            for k in range(2):
                body(2 * n + k, k, n)

    def tile_rows(t):
        return P if t < TT - 1 else REST

    with nc.Block() as block:
        @block.sync
        def _(sp):
            sp.dma_start(b1_rows[:], b1.rearrange("e (c p) -> (e c) p", p=P)).then_inc(bias_in, 16)
            sp.dma_start(b2_s[:].rearrange("p e d -> p (e d)"), b2.rearrange("e d -> (e d)").partition_broadcast(P)
                         ).then_inc(bias_in, 16)

            def body(e, k, n):
                sp.wait_ge(second, TT * e + TT)
                sp.wait_ge(y_done, TT * e + TT)
                sp.dma_start(tok[:, k], T["tokens"][bass.ds(e * SLOTS, SLOTS), :].rearrange("(t p) w -> p t w", p=P)
                             ).then_inc(tok_in[k], 16)
                sp.dma_start(w1_s[:, k], w1[bass.ds(e, 1)].rearrange("o (a p) f -> p (o a) f", p=P)
                             ).then_inc(w1_in[k], 16)
                sp.dma_start(w2_s[:, k], w2[bass.ds(e, 1)].rearrange("o (c p) d -> p (o c) d", p=P)
                             ).then_inc(w2_in[k], 16)

            per_expert(sp, body)

        @block.tensor
        def _(pe):
            pe.sem_inc(second, 2 * TT)
            pe.wait_ge(bias_in, 32)
            pe.transpose(psum[:, 0, 0:NX * KF], b1_rows[:], T["ident"][0:NX * KF, 0:NX * KF]).then_inc(b1_turned, 1)
            pe.wait_ge(b1_ready, 1)

            def turn(e, k, n):
                pe.wait_ge(tok_in[k], 16 * (n + 1))
                for piece in range(4):
                    a, t0 = piece // 2, piece % 2 * 4
                    pe.wait_ge(turned_sb, 4 * e + piece + 1)
                    for t in range(4):
                        ins = pe.transpose(psum[:, piece % 2, t * P:(t + 1) * P], tok[:, k, t0 + t, a * P:(a + 1) * P],
                                           T["ident"][:])
                    ins.then_inc(turned, 1)

            def first_products(e, k, n):
                pe.wait_ge(turned_sb, 4 * e + 6)
                pe.wait_ge(w1_in[k], 16 * (n + 1))
                for c in range(KF):
                    for half, (t0, size) in enumerate(HALVES):
                        m = 2 * c + half
                        pe.wait_ge(mid_done, 2 * KF * e + m + 1)
                        for a in range(2):
                            ins = pe.matmul(psum[:, 2 + half, 0:size], w1_s[:, k, a, c * P:(c + 1) * P],
                                            tT[:, k, a, t0:t0 + size], start=a == 0, stop=a == 1)
                        ins.then_inc(first, 1)

            def second_products(e, k, n):
                pe.wait_ge(mid_done, 2 * KF * e + 2 * KF + 2)
                pe.wait_ge(w2_in[k], 16 * (n + 1))
                for t in range(TT):
                    r = tile_rows(t)
                    pe.wait_ge(y_done, TT * e + t + 2 * TT - 1)
                    for c in range(KF):
                        ins = pe.matmul(psum[0:r, 4 + t % 2, 0:D], mid[:, c, t * P:t * P + r], w2_s[:, k, c, :],
                                        start=c == 0, stop=c == KF - 1)
                    ins.then_inc(second, 1)

            staged(pe, NX, 2, (0, first_products), (1, turn), (0, second_products))

        @block.scalar
        def _(act):
            act.sem_inc(mid_done, 2)
            act.sem_inc(turned_sb, 2)

            def turned_copies(e, k, n):
                for piece in range(4):
                    a, t0 = piece // 2, piece % 2 * 4
                    act.wait_ge(turned, 4 * e + piece + 1)
                    act.copy(tT[:, k, a, t0 * P:(t0 + 4) * P], psum[:, piece % 2, :]).then_inc(turned_sb, 1)

            def hidden(e, k, n):
                act.copy(b1_now[:, k, :], at_block(b1_s, e)).then_inc(b1_picked, 1)
                act.wait_ge(b1_picked, e + 1)
                act.wait_ge(second, TT * e + 2 * TT)
                for c in range(KF):
                    for half, (t0, size) in enumerate(HALVES):
                        act.wait_ge(first, 2 * KF * e + 2 * c + half + 1)
                        act.activation(mid[:, c, t0:t0 + size], psum[:, 2 + half, 0:size], ACT.Relu,
                                       bias=b1_now[:, k, c:c + 1]).then_inc(mid_done, 1)

            act.wait_ge(b1_turned, 1)
            act.copy(b1_s[:].rearrange("p e c -> p (e c)"), psum[:, 0, 0:NX * KF]).then_inc(b1_ready, 1)
            act.wait_ge(b1_ready, 1)
            staged(act, NX, 2, (0, hidden), (1, turned_copies))

        @block.gpsimd
        def _(pool):
            pool.sem_inc(y_free, 2)

            def body(e, k, n):
                pool.wait_ge(numbered, e + 2)
                for t in range(TT):
                    pool.sem_inc(asked, 1)
                    pool.indirect_dma_start(
                        out=x_back[0:tile_rows(t), t, :], out_offset=None, in_=T["x_rows"],
                        in_offset=bass.IndirectOffsetOnAxis(ap=number[0:tile_rows(t), k, t:t + 1], axis=0),
                        bounds_check=N - 1, oob_is_err=False).then_inc(x_in[t], 16)
                for t in range(TT):
                    pool.wait_ge(y_done, TT * e + t + 2 * TT + 1)
                    pool.sem_inc(asked, 1)
                    pool.indirect_dma_start(
                        out=out, out_offset=bass.IndirectOffsetOnAxis(ap=number[0:tile_rows(t), k, t:t + 1], axis=0),
                        in_=y[0:tile_rows(t), t % 2, :], in_offset=None, bounds_check=N - 1, oob_is_err=False
                    ).then_inc(y_out, 16)
                    pool.wait_ge(y_out, 16 * (TT * e + t + 1))
                    pool.sem_inc(y_free, 1)

            per_expert(pool, body)

        @block.vector
        def _(dve):
            dve.sem_inc(y_done, 2 * TT)
            dve.memset(x_back[:], 0.0).then_inc(numbered, 1)
            dve.wait_ge(bias_in, 32)

            def body(e, k, n):
                dve.wait_ge(tok_in[k], 16 * (n + 1))
                dve.tensor_copy(number[:, k, :], tok[:, k, :, D + 1]).then_inc(numbered, 1)
                for t in range(TT):
                    r, s, tile = tile_rows(t), t % 2, TT * e + t
                    yt, r0, r1 = y[0:r, s, :], raw[0:r, s, 0, :], raw[0:r, s, 1, :]
                    fin, fx = mask[0:r, s, :], fix[0:r, s, :]
                    dve.wait_ge(tok_in[k], 16 * (n + 1))
                    dve.wait_ge(second, tile + 2 * TT + 1)
                    dve.tensor_tensor(r0, psum[0:r, 4 + s, 0:D], at_block(b2_s, e)[0:r], ALU.add
                                      ).then_inc(y_steps, 1)
                    dve.wait_ge(y_steps, 8 * tile + 1)
                    dve.tensor_scalar(r1, r0, tok[0:r, k, t, D:D + 1], None, ALU.mult).then_inc(y_steps, 1)
                    dve.wait_ge(y_steps, 8 * tile + 2)
                    dve.tensor_scalar(fin, r1, 0.0, 0.0, ALU.mult, ALU.is_equal).then_inc(y_steps, 1)
                    dve.tensor_scalar(fx, r1, -BIGGEST, -1.0e4, ALU.is_lt, ALU.mult).then_inc(y_steps, 1)
                    dve.tensor_scalar(r0, r1, BIGGEST, 1.0e4, ALU.is_gt, ALU.mult).then_inc(y_steps, 1)
                    dve.wait_ge(y_free, tile + 1)
                    dve.wait_ge(y_steps, 8 * tile + 5)
                    dve.tensor_tensor(yt, fx, r0, ALU.add).then_inc(y_steps, 1)
                    dve.wait_ge(y_steps, 8 * tile + 6)
                    dve.sem_inc(y_steps, 1)
                    dve.copy_predicated(yt, fin, r1).then_inc(y_steps, 1)
                    dve.wait_ge(x_in[t], 16 * (e + 1))
                    dve.wait_ge(y_steps, 8 * tile + 8)
                    dve.tensor_tensor(yt, yt, x_back[0:r, t, :], ALU.add).then_inc(y_done, 1)

            per_expert(dve, body)


def kernel(x, src, dst, L0_gnn_Wl1, L0_gnn_Wr1, L0_gnn_att1, L0_gnn_b1, L0_gnn_Wl2, L0_gnn_Wr2, L0_gnn_att2,
           L0_gnn_b2, L0_ffn_gate_w, L0_ffn_gate_b, L0_ffn_w1, L0_ffn_b1, L0_ffn_w2, L0_ffn_b2):
    import numpy as np
    import concourse.bacc as bacc
    from concourse.bass_utils import run_bass_kernel_spmd

    nc = bacc.Bacc("TRN2", target_bir_lowering=False, num_devices=1)
    inputs = dict(x=x, src=src, dst=dst, wl1=L0_gnn_Wl1, wr1=L0_gnn_Wr1, att1=L0_gnn_att1, b1=L0_gnn_b1,
                  wl2=L0_gnn_Wl2, wr2=L0_gnn_Wr2, att2=L0_gnn_att2, b2=L0_gnn_b2, gate_w=L0_ffn_gate_w,
                  gate_b=L0_ffn_gate_b, ffn_w1=L0_ffn_w1, ffn_b1=L0_ffn_b1, ffn_w2=L0_ffn_w2, ffn_b2=L0_ffn_b2)
    arrays = {f"in_{name}": np.ascontiguousarray(a) for name, a in inputs.items()}
    ap = {name: nc.dram_tensor(f"in_{name}", arrays[f"in_{name}"].shape,
                               mybir.dt.from_np(arrays[f"in_{name}"].dtype), kind="ExternalInput").ap()
          for name in inputs}
    out = nc.dram_tensor("out", (N, D), F32, kind="ExternalOutput").ap()
    gnn = [tuple(ap[f"{n}{i}"] for n in ("wl", "wr", "att", "b")) for i in (1, 2)]
    ffn = tuple(ap[n] for n in ("gate_w", "gate_b", "ffn_w1", "ffn_b1", "ffn_w2", "ffn_b2"))
    build(nc, ap["x"], ap["src"], ap["dst"], gnn, ffn, out)
    return run_bass_kernel_spmd(nc, [arrays], core_ids=[0]).results[0]["out"]
```
